# Optimizing a Trainium2 kernel written in Bass

```python
import numpy as np
import jax
import jax.numpy as jnp

def _softmax(x, axis=-1):
    return jax.nn.softmax(x, axis=axis)

def _gelu(x):
    return jax.nn.gelu(x, approximate=True)

def _silu(x):
    return jax.nn.silu(x)

def _sigmoid(x):
    return jax.nn.sigmoid(x)

def _layernorm(x, axis=-1, eps=1e-05):
    m = jnp.mean(x, axis=axis, keepdims=True)
    v = jnp.var(x, axis=axis, keepdims=True)
    return (x - m) / jnp.sqrt(v + eps)

def _scatter_add(tgt, idx, src, axis=0):
    return tgt.at[idx].add(src)

def _segment_sum(src, seg, n):
    return jax.ops.segment_sum(src, seg, n)
kernel_name = 'mk_gps_d2_gnn_r8_1b3df5'

def setup_inputs(seed: int=0):
    np.random.seed(seed)
    _w = jnp.asarray

    def _rec_inputs():
        import jax
        import jax.numpy as jnp
        _gk = jax.random.key(seed)
        x = -8.776e-05 + 1 * jax.random.normal(jax.random.fold_in(_gk, 1), (1250, 512), jnp.float32)
        src = jax.random.randint(jax.random.fold_in(_gk, 2), (40000,), 0, 1250, jnp.int32)
        dst = jax.random.randint(jax.random.fold_in(_gk, 3), (40000,), 0, 1250, jnp.int32)
        _o = jnp.argsort(dst, stable=True)
        src = src[_o]
        dst = dst[_o]
        edge_attr_20 = jax.random.uniform(jax.random.fold_in(_gk, 12), (40000, 20), jnp.float32, 0.0, 0.999999)
        edge_attr_3 = -0.0005747 + 0.998114 * jax.random.normal(jax.random.fold_in(_gk, 13), (40000, 3), jnp.float32)
        edge_weight = jax.random.uniform(jax.random.fold_in(_gk, 15), (40000,), jnp.float32, 0.0, 0.999973)
        return (x, src, dst, edge_attr_20, edge_attr_3, edge_weight)
    x, src, dst, edge_attr_20, edge_attr_3, edge_weight = _rec_inputs()

    def _L0_gnn_setup():
        import jax, jax.numpy as jnp
        import numpy as np
        N, E, D, H = (1250, 20000, 512, 8)
        C = D // H
        key = jax.random.key(seed)
        ks = jax.random.split(key, 5)
        x = jax.random.normal(ks[0], (N, D), dtype=jnp.float32)
        edge_index = jax.random.randint(ks[1], (2, E), 0, N, dtype=jnp.int64 if jax.config.jax_enable_x64 else jnp.int32)
        scale = 1.0 / np.sqrt(D).astype(np.float32)
        W_l = jax.random.normal(ks[2], (D, D), dtype=jnp.float32) * scale
        W_r = jax.random.normal(ks[3], (D, D), dtype=jnp.float32) * scale
        att = jax.random.normal(ks[4], (H, C), dtype=jnp.float32) * np.float32(1.0 / np.sqrt(C))
        bias = jnp.zeros((D,), dtype=jnp.float32)
        return {'x': x, 'edge_index': edge_index, 'W_l': W_l, 'W_r': W_r, 'att': att, 'bias': bias}
    _L0_gnn_all = _L0_gnn_setup()
    _L0_gnn_in = {k: v for k, v in _L0_gnn_all.items() if k in ('W_l', 'W_r', 'att', 'bias')}
    del _L0_gnn_all

    def _L0_mix_setup():
        import jax, jax.numpy as jnp
        import numpy as np
        DIM = 512
        NUM_HEADS = 8
        HEAD_DIM = DIM // NUM_HEADS
        EPS = 1e-06

        def _feature_map(x):
            return jax.nn.elu(x) + 1.0
        key = jax.random.key(seed)
        k_x, k_qkv, k_out, k_b = jax.random.split(key, 4)
        B, N = (8, 512)
        x = jax.random.normal(k_x, (B, N, DIM), dtype=jnp.float32)
        s_qkv = 1.0 / np.sqrt(DIM)
        W_qkv = jax.random.uniform(k_qkv, (DIM, 3 * DIM), minval=-s_qkv, maxval=s_qkv, dtype=jnp.float32)
        W_out = jax.random.uniform(k_out, (DIM, DIM), minval=-s_qkv, maxval=s_qkv, dtype=jnp.float32)
        b_out = jax.random.uniform(k_b, (DIM,), minval=-s_qkv, maxval=s_qkv, dtype=jnp.float32)
        return {'x': x, 'W_qkv': W_qkv, 'W_out': W_out, 'b_out': b_out}
    _L0_mix_all = _L0_mix_setup()
    _L0_mix_in = {k: v for k, v in _L0_mix_all.items() if k in ('W_qkv', 'W_out', 'b_out')}
    del _L0_mix_all

    def _L0_ffn_setup():
        import jax, jax.numpy as jnp
        import numpy as np
        B, S, H, E, F = (4, 256, 512, 8, 512)
        key = jax.random.key(seed)
        k = jax.random.split(key, 7)
        x = jax.random.normal(k[0], (B, S, H), dtype=jnp.float32)
        Wr = jax.random.normal(k[1], (H, E), dtype=jnp.float32) / np.sqrt(H)
        br = jnp.zeros((E,), dtype=jnp.float32)
        W1 = jax.random.normal(k[2], (E, H, F), dtype=jnp.float32) / np.sqrt(H)
        b1 = jnp.zeros((E, F), dtype=jnp.float32)
        W2 = jax.random.normal(k[3], (E, F, H), dtype=jnp.float32) / np.sqrt(F)
        b2 = jnp.zeros((E, H), dtype=jnp.float32)
        return {'x': x, 'Wr': Wr, 'br': br, 'W1': W1, 'b1': b1, 'W2': W2, 'b2': b2}
    _L0_ffn_all = _L0_ffn_setup()
    _L0_ffn_in = {k: v for k, v in _L0_ffn_all.items() if k in ('Wr', 'br', 'W1', 'b1', 'W2', 'b2')}
    del _L0_ffn_all

    def _L1_gnn_setup():
        import jax, jax.numpy as jnp
        import numpy as np
        N_ATOMS = 625
        N_EDGES = 6250
        C = 128
        F = 128
        N_RBF = 20
        LOG2 = float(np.log(2.0))
        Y0 = float(1.0 / np.sqrt(4.0 * np.pi))
        Y1_SCALE = float(np.sqrt(3.0 / (4.0 * np.pi)))

        def shifted_softplus(x):
            return jax.nn.softplus(x) - LOG2

        def _forward(x, idx_i, idx_j, f_ij, rcut_ij, r_ij, W_in2f_s, W_in2f_v, Wf1, bf1, Wf2, bf2, W1_s, W1_v, W2_s, W2_v):
            n = x.shape[0]
            e = r_ij.shape[0]
            xs = x[:, :C] @ (W_in2f_s / np.sqrt(C))
            xv = jnp.einsum('nci,cf->nfi', x[:, C:].reshape(n, C, 3), W_in2f_v) / np.sqrt(C)
            sj = xs[idx_j]
            vj = xv[idx_j]
            u = r_ij / jnp.linalg.norm(r_ij, axis=-1, keepdims=True)
            Yv = Y1_SCALE * u
            o0a = sj * Y0
            o0b = jnp.einsum('efi,ei->ef', vj, Yv) / np.sqrt(3.0)
            s2 = jnp.stack([o0a, o0b], axis=-1).reshape(e, 2 * F)
            ova = sj[:, :, None] * Yv[:, None, :]
            ovb = vj * Y0
            v2 = jnp.stack([ova, ovb], axis=2)
            w1 = jnp.cross(vj, Yv[:, None, :]) / np.sqrt(2.0)
            ax, ay, az = (vj[..., 0], vj[..., 1], vj[..., 2])
            bx, by, bz = (Yv[:, None, 0], Yv[:, None, 1], Yv[:, None, 2])
            t = jnp.stack([(ax * by + ay * bx) / np.sqrt(2.0), (ay * bz + az * by) / np.sqrt(2.0), (2.0 * az * bz - ax * bx - ay * by) / np.sqrt(6.0), (az * bx + ax * bz) / np.sqrt(2.0), (ax * bx - ay * by) / np.sqrt(2.0)], axis=-1)
            h = shifted_softplus(f_ij @ Wf1 + bf1)
            W = (h @ Wf2 + bf2) * rcut_ij[:, None]
            m_s = s2 * W[:, :2 * F]
            m_v = (v2.reshape(e, 2 * F, 3) * W[:, 2 * F:4 * F, None]).reshape(e, 6 * F)
            m_w = (w1 * W[:, 4 * F:5 * F, None]).reshape(e, 3 * F)
            m_t = (t * W[:, 5 * F:6 * F, None]).reshape(e, 5 * F)
            x_ij = jnp.concatenate([m_s, m_v, m_w, m_t], axis=1)
            agg = jax.ops.segment_sum(x_ij, idx_i, num_segments=n)
            S = agg[:, :2 * F] @ (W1_s / np.sqrt(2 * F))
            V = jnp.einsum('nmi,mc->nci', agg[:, 2 * F:8 * F].reshape(n, 2 * F, 3), W1_v) / np.sqrt(2 * F)
            S = shifted_softplus(S)
            S = S @ (W2_s / np.sqrt(C))
            V = jnp.einsum('nci,cd->ndi', V, W2_v) / np.sqrt(C)
            return jnp.concatenate([S, V.reshape(n, 3 * C)], axis=1)
        key = jax.random.key(seed)
        ks = jax.random.split(key, 16)
        f32 = jnp.float32
        x = jax.random.normal(ks[0], (N_ATOMS, 4 * C), f32)
        idx_i = jnp.sort(jax.random.randint(ks[1], (N_EDGES,), 0, N_ATOMS))
        idx_j = jax.random.randint(ks[2], (N_EDGES,), 0, N_ATOMS)
        f_ij = jax.random.uniform(ks[3], (N_EDGES, N_RBF), f32)
        rcut_ij = jax.random.uniform(ks[4], (N_EDGES,), f32)
        r_ij = jax.random.normal(ks[5], (N_EDGES, 3), f32)
        W_in2f_s = jax.random.normal(ks[6], (C, F), f32)
        W_in2f_v = jax.random.normal(ks[7], (C, F), f32)
        Wf1 = jax.random.normal(ks[8], (N_RBF, F), f32) / np.sqrt(N_RBF)
        bf1 = 0.1 * jax.random.normal(ks[9], (F,), f32)
        Wf2 = jax.random.normal(ks[10], (F, 6 * F), f32) / np.sqrt(F)
        bf2 = 0.1 * jax.random.normal(ks[11], (6 * F,), f32)
        W1_s = jax.random.normal(ks[12], (2 * F, C), f32)
        W1_v = jax.random.normal(ks[13], (2 * F, C), f32)
        W2_s = jax.random.normal(ks[14], (C, C), f32)
        W2_v = jax.random.normal(ks[15], (C, C), f32)
        return dict(x=x, idx_i=idx_i, idx_j=idx_j, f_ij=f_ij, rcut_ij=rcut_ij, r_ij=r_ij, W_in2f_s=W_in2f_s, W_in2f_v=W_in2f_v, Wf1=Wf1, bf1=bf1, Wf2=Wf2, bf2=bf2, W1_s=W1_s, W1_v=W1_v, W2_s=W2_s, W2_v=W2_v)
    _L1_gnn_all = _L1_gnn_setup()
    _L1_gnn_in = {k: v for k, v in _L1_gnn_all.items() if k in ('W_in2f_s', 'W_in2f_v', 'Wf1', 'bf1', 'Wf2', 'bf2', 'W1_s', 'W1_v', 'W2_s', 'W2_v')}
    del _L1_gnn_all

    def _L1_mix_setup():
        import jax, jax.numpy as jnp
        import numpy as np
        import math
        E = 512
        H = 8
        D = E // H
        M = 64
        EPS = 1e-08
        CLAMP_MAX = 50.0

        def _make_omega(key):
            w = jax.random.normal(key, (D, M), dtype=jnp.float32) / np.sqrt(D)
            q, _ = jnp.linalg.qr(w)
            return q

        def _positive_random_feature_map(v, omega):
            f = jnp.minimum(v @ omega, CLAMP_MAX)
            l2 = jnp.maximum(jnp.linalg.norm(v, axis=-1, keepdims=True), EPS)
            norm_term = jnp.maximum(jnp.exp(-0.5 * l2 * l2), EPS)
            return norm_term * jnp.exp(f)
        key = jax.random.key(seed)
        ks = jax.random.split(key, 8)
        B, S = (2, 2048)
        x = jax.random.normal(ks[0], (B, S, E), dtype=jnp.float32)
        sc = 1.0 / np.sqrt(E)
        Wq = jax.random.normal(ks[1], (E, E), dtype=jnp.float32) * sc
        Wk = jax.random.normal(ks[2], (E, E), dtype=jnp.float32) * sc
        Wv = jax.random.normal(ks[3], (E, E), dtype=jnp.float32) * sc
        Wo = jax.random.normal(ks[4], (E, E), dtype=jnp.float32) * sc
        omega_q = _make_omega(ks[5])
        omega_k = _make_omega(ks[6])
        return {'x': x, 'Wq': Wq, 'Wk': Wk, 'Wv': Wv, 'Wo': Wo, 'omega_q': omega_q, 'omega_k': omega_k}
    _L1_mix_all = _L1_mix_setup()
    _L1_mix_in = {k: v for k, v in _L1_mix_all.items() if k in ('Wq', 'Wk', 'Wv', 'Wo', 'omega_q', 'omega_k')}
    del _L1_mix_all

    def _L1_ffn_setup():
        import jax, jax.numpy as jnp
        import numpy as np
        B, S, D, H, E, K = (2, 256, 512, 1024, 8, 2)

        def _moe(x, router_w, w_gate, w_up, w_down):
            bsz, seq, d = x.shape
            flat = x.reshape(-1, d)
            logits = flat @ router_w.T
            topk_vals, topk_idx = jax.lax.top_k(logits, K)
            topk_w = jax.nn.softmax(topk_vals, axis=-1)
            s = flat.shape[0]
            dense_w = jnp.zeros((s, E), dtype=flat.dtype).at[jnp.arange(s)[:, None], topk_idx].add(topk_w)
            g = jnp.einsum('sd,edh->esh', flat, w_gate)
            u = jnp.einsum('sd,edh->esh', flat, w_up)
            y = jnp.einsum('esh,ehd->esd', jax.nn.silu(g) * u, w_down)
            out = jnp.einsum('esd,se->sd', y, dense_w)
            return out.reshape(bsz, seq, d)
        key = jax.random.key(seed)
        k1, k2, k3, k4, k5 = jax.random.split(key, 5)
        return {'x': jax.random.normal(k1, (B, S, D), dtype=jnp.float32), 'router_w': jax.random.normal(k2, (E, D), dtype=jnp.float32) * D ** (-0.5), 'w_gate': jax.random.normal(k3, (E, D, H), dtype=jnp.float32) * D ** (-0.5), 'w_up': jax.random.normal(k4, (E, D, H), dtype=jnp.float32) * D ** (-0.5), 'w_down': jax.random.normal(k5, (E, H, D), dtype=jnp.float32) * H ** (-0.5)}
    _L1_ffn_all = _L1_ffn_setup()
    _L1_ffn_in = {k: v for k, v in _L1_ffn_all.items() if k in ('router_w', 'w_gate', 'w_up', 'w_down')}
    del _L1_ffn_all
    return {'x': x, 'src': src, 'dst': dst, 'edge_attr_20': edge_attr_20, 'edge_attr_3': edge_attr_3, 'edge_weight': edge_weight, 'L0_gnn_W_l': _L0_gnn_in['W_l'], 'L0_gnn_W_r': _L0_gnn_in['W_r'], 'L0_gnn_att': _L0_gnn_in['att'], 'L0_gnn_bias': _L0_gnn_in['bias'], 'L0_mix_W_qkv': _L0_mix_in['W_qkv'], 'L0_mix_W_out': _L0_mix_in['W_out'], 'L0_mix_b_out': _L0_mix_in['b_out'], 'L0_ffn_Wr': _L0_ffn_in['Wr'], 'L0_ffn_br': _L0_ffn_in['br'], 'L0_ffn_W1': _L0_ffn_in['W1'], 'L0_ffn_b1': _L0_ffn_in['b1'], 'L0_ffn_W2': _L0_ffn_in['W2'], 'L0_ffn_b2': _L0_ffn_in['b2'], 'L1_gnn_W_in2f_s': _L1_gnn_in['W_in2f_s'], 'L1_gnn_W_in2f_v': _L1_gnn_in['W_in2f_v'], 'L1_gnn_Wf1': _L1_gnn_in['Wf1'], 'L1_gnn_bf1': _L1_gnn_in['bf1'], 'L1_gnn_Wf2': _L1_gnn_in['Wf2'], 'L1_gnn_bf2': _L1_gnn_in['bf2'], 'L1_gnn_W1_s': _L1_gnn_in['W1_s'], 'L1_gnn_W1_v': _L1_gnn_in['W1_v'], 'L1_gnn_W2_s': _L1_gnn_in['W2_s'], 'L1_gnn_W2_v': _L1_gnn_in['W2_v'], 'L1_mix_Wq': _L1_mix_in['Wq'], 'L1_mix_Wk': _L1_mix_in['Wk'], 'L1_mix_Wv': _L1_mix_in['Wv'], 'L1_mix_Wo': _L1_mix_in['Wo'], 'L1_mix_omega_q': _L1_mix_in['omega_q'], 'L1_mix_omega_k': _L1_mix_in['omega_k'], 'L1_ffn_router_w': _L1_ffn_in['router_w'], 'L1_ffn_w_gate': _L1_ffn_in['w_gate'], 'L1_ffn_w_up': _L1_ffn_in['w_up'], 'L1_ffn_w_down': _L1_ffn_in['w_down']}

def reference(x, src, dst, edge_attr_20, edge_attr_3, edge_weight, L0_gnn_W_l, L0_gnn_W_r, L0_gnn_att, L0_gnn_bias, L0_mix_W_qkv, L0_mix_W_out, L0_mix_b_out, L0_ffn_Wr, L0_ffn_br, L0_ffn_W1, L0_ffn_b1, L0_ffn_W2, L0_ffn_b2, L1_gnn_W_in2f_s, L1_gnn_W_in2f_v, L1_gnn_Wf1, L1_gnn_bf1, L1_gnn_Wf2, L1_gnn_bf2, L1_gnn_W1_s, L1_gnn_W1_v, L1_gnn_W2_s, L1_gnn_W2_v, L1_mix_Wq, L1_mix_Wk, L1_mix_Wv, L1_mix_Wo, L1_mix_omega_q, L1_mix_omega_k, L1_ffn_router_w, L1_ffn_w_gate, L1_ffn_w_up, L1_ffn_w_down):
    import jax
    import jax.numpy as jnp

    def _L0_gnn_ref(x, edge_index, W_l, W_r, att, bias):
        import jax, jax.numpy as jnp
        import numpy as np
        N, E, D, H = (1250, 20000, 512, 8)
        C = D // H
        n = x.shape[0]
        self_idx = jnp.arange(n, dtype=edge_index.dtype)
        src = jnp.concatenate([edge_index[0], self_idx])
        dst = jnp.concatenate([edge_index[1], self_idx])
        x_l = (x @ W_l).reshape(n, H, C)
        x_r = (x @ W_r).reshape(n, H, C)
        m = jax.nn.leaky_relu(x_l[src] + x_r[dst], negative_slope=0.2)
        alpha = jnp.einsum('ehc,hc->eh', m, att)
        amax = jax.lax.stop_gradient(jax.ops.segment_max(alpha, dst, num_segments=n))
        ea = jnp.exp(alpha - amax[dst])
        denom = jax.ops.segment_sum(ea, dst, num_segments=n)
        w = ea / jnp.maximum(denom[dst], 1e-16)
        out = jax.ops.segment_sum(w[:, :, None] * x_l[src], dst, num_segments=n)
        out = out.reshape(n, H * C) + bias
        return jax.nn.elu(out) + x

    def _L0_mix_ref(x, W_qkv, W_out, b_out):
        import jax, jax.numpy as jnp
        import numpy as np
        DIM = 512
        NUM_HEADS = 8
        HEAD_DIM = DIM // NUM_HEADS
        EPS = 1e-06

        def _feature_map(x):
            return jax.nn.elu(x) + 1.0
        B, N, C = x.shape
        H, D = (NUM_HEADS, HEAD_DIM)
        qkv = x @ W_qkv
        qkv = qkv.reshape(B, N, 3, H, D).transpose(2, 0, 3, 1, 4)
        q, k, v = (qkv[0], qkv[1], qkv[2])
        q_phi = _feature_map(q)
        k_phi = _feature_map(k)
        KV = jnp.einsum('bhnd,bhne->bhde', k_phi, v)
        K_sum = k_phi.sum(axis=2)
        denom = jnp.einsum('bhnd,bhd->bhn', q_phi, K_sum)[..., None] + EPS
        out = jnp.einsum('bhnd,bhde->bhne', q_phi, KV) / denom
        out = out.transpose(0, 2, 1, 3).reshape(B, N, C)
        return out @ W_out + b_out

    def _L0_ffn_ref(x, Wr, br, W1, b1, W2, b2):
        import jax, jax.numpy as jnp
        import numpy as np
        B, S, H, E, F = (4, 256, 512, 8, 512)
        b, s, h = x.shape
        xt = x.reshape(-1, h)
        logits = xt @ Wr + br
        probs = jax.nn.softmax(logits, axis=-1)
        G = jnp.max(probs, axis=-1)
        idx = jnp.argmax(probs, axis=-1)
        h1 = jax.nn.relu(jnp.einsum('nh,ehf->nef', xt, W1) + b1)
        eo = jnp.einsum('nef,efh->neh', h1, W2) + b2
        Eout = jnp.take_along_axis(eo, idx[:, None, None], axis=1)[:, 0, :]
        y = G[:, None] * Eout
        return y.reshape(b, s, h)

    def _L1_gnn_ref(x, idx_i, idx_j, f_ij, rcut_ij, r_ij, W_in2f_s, W_in2f_v, Wf1, bf1, Wf2, bf2, W1_s, W1_v, W2_s, W2_v):
        import jax, jax.numpy as jnp
        import numpy as np
        N_ATOMS = 625
        N_EDGES = 6250
        C = 128
        F = 128
        N_RBF = 20
        LOG2 = float(np.log(2.0))
        Y0 = float(1.0 / np.sqrt(4.0 * np.pi))
        Y1_SCALE = float(np.sqrt(3.0 / (4.0 * np.pi)))

        def shifted_softplus(x):
            return jax.nn.softplus(x) - LOG2

        def _forward(x, idx_i, idx_j, f_ij, rcut_ij, r_ij, W_in2f_s, W_in2f_v, Wf1, bf1, Wf2, bf2, W1_s, W1_v, W2_s, W2_v):
            n = x.shape[0]
            e = r_ij.shape[0]
            xs = x[:, :C] @ (W_in2f_s / np.sqrt(C))
            xv = jnp.einsum('nci,cf->nfi', x[:, C:].reshape(n, C, 3), W_in2f_v) / np.sqrt(C)
            sj = xs[idx_j]
            vj = xv[idx_j]
            u = r_ij / jnp.linalg.norm(r_ij, axis=-1, keepdims=True)
            Yv = Y1_SCALE * u
            o0a = sj * Y0
            o0b = jnp.einsum('efi,ei->ef', vj, Yv) / np.sqrt(3.0)
            s2 = jnp.stack([o0a, o0b], axis=-1).reshape(e, 2 * F)
            ova = sj[:, :, None] * Yv[:, None, :]
            ovb = vj * Y0
            v2 = jnp.stack([ova, ovb], axis=2)
            w1 = jnp.cross(vj, Yv[:, None, :]) / np.sqrt(2.0)
            ax, ay, az = (vj[..., 0], vj[..., 1], vj[..., 2])
            bx, by, bz = (Yv[:, None, 0], Yv[:, None, 1], Yv[:, None, 2])
            t = jnp.stack([(ax * by + ay * bx) / np.sqrt(2.0), (ay * bz + az * by) / np.sqrt(2.0), (2.0 * az * bz - ax * bx - ay * by) / np.sqrt(6.0), (az * bx + ax * bz) / np.sqrt(2.0), (ax * bx - ay * by) / np.sqrt(2.0)], axis=-1)
            h = shifted_softplus(f_ij @ Wf1 + bf1)
            W = (h @ Wf2 + bf2) * rcut_ij[:, None]
            m_s = s2 * W[:, :2 * F]
            m_v = (v2.reshape(e, 2 * F, 3) * W[:, 2 * F:4 * F, None]).reshape(e, 6 * F)
            m_w = (w1 * W[:, 4 * F:5 * F, None]).reshape(e, 3 * F)
            m_t = (t * W[:, 5 * F:6 * F, None]).reshape(e, 5 * F)
            x_ij = jnp.concatenate([m_s, m_v, m_w, m_t], axis=1)
            agg = jax.ops.segment_sum(x_ij, idx_i, num_segments=n)
            S = agg[:, :2 * F] @ (W1_s / np.sqrt(2 * F))
            V = jnp.einsum('nmi,mc->nci', agg[:, 2 * F:8 * F].reshape(n, 2 * F, 3), W1_v) / np.sqrt(2 * F)
            S = shifted_softplus(S)
            S = S @ (W2_s / np.sqrt(C))
            V = jnp.einsum('nci,cd->ndi', V, W2_v) / np.sqrt(C)
            return jnp.concatenate([S, V.reshape(n, 3 * C)], axis=1)
        return _forward(x, idx_i, idx_j, f_ij, rcut_ij, r_ij, W_in2f_s, W_in2f_v, Wf1, bf1, Wf2, bf2, W1_s, W1_v, W2_s, W2_v)

    def _L1_mix_ref(x, Wq, Wk, Wv, Wo, omega_q, omega_k):
        import jax, jax.numpy as jnp
        import numpy as np
        import math
        E = 512
        H = 8
        D = E // H
        M = 64
        EPS = 1e-08
        CLAMP_MAX = 50.0

        def _make_omega(key):
            w = jax.random.normal(key, (D, M), dtype=jnp.float32) / np.sqrt(D)
            q, _ = jnp.linalg.qr(w)
            return q

        def _positive_random_feature_map(v, omega):
            f = jnp.minimum(v @ omega, CLAMP_MAX)
            l2 = jnp.maximum(jnp.linalg.norm(v, axis=-1, keepdims=True), EPS)
            norm_term = jnp.maximum(jnp.exp(-0.5 * l2 * l2), EPS)
            return norm_term * jnp.exp(f)
        B, S, _ = x.shape
        scale = 1.0 / np.sqrt(D)

        def heads(y):
            return y.reshape(B, S, H, D).transpose(0, 2, 1, 3)
        Q = heads(x @ Wq) * scale
        K = heads(x @ Wk) * scale
        V = heads(x @ Wv)
        Q_phi = _positive_random_feature_map(Q, omega_q)
        K_phi = _positive_random_feature_map(K, omega_k)
        KV = jnp.einsum('bhsm,bhsd->bhmd', K_phi, V)
        QKV = jnp.einsum('bhsm,bhmd->bhsd', Q_phi, KV)
        K_ones = K_phi.sum(axis=2)
        QK_ones = jnp.einsum('bhsm,bhm->bhs', Q_phi, K_ones)
        attn = QKV / QK_ones[..., None]
        out = attn.transpose(0, 2, 1, 3).reshape(B, S, E)
        return out @ Wo

    def _L1_ffn_ref(x, router_w, w_gate, w_up, w_down):
        import jax, jax.numpy as jnp
        import numpy as np
        B, S, D, H, E, K = (2, 256, 512, 1024, 8, 2)

        def _moe(x, router_w, w_gate, w_up, w_down):
            bsz, seq, d = x.shape
            flat = x.reshape(-1, d)
            logits = flat @ router_w.T
            topk_vals, topk_idx = jax.lax.top_k(logits, K)
            topk_w = jax.nn.softmax(topk_vals, axis=-1)
            s = flat.shape[0]
            dense_w = jnp.zeros((s, E), dtype=flat.dtype).at[jnp.arange(s)[:, None], topk_idx].add(topk_w)
            g = jnp.einsum('sd,edh->esh', flat, w_gate)
            u = jnp.einsum('sd,edh->esh', flat, w_up)
            y = jnp.einsum('esh,ehd->esd', jax.nn.silu(g) * u, w_down)
            out = jnp.einsum('esd,se->sd', y, dense_w)
            return out.reshape(bsz, seq, d)
        return _moe(x, router_w, w_gate, w_up, w_down)
    edge_index = jnp.stack([src, dst])
    xn = _layernorm(x, axis=-1)
    x = x + _L0_gnn_ref(xn, edge_index, L0_gnn_W_l, L0_gnn_W_r, L0_gnn_att, L0_gnn_bias) + _L0_mix_ref(xn[None], L0_mix_W_qkv, L0_mix_W_out, L0_mix_b_out)[0]
    x = x + _L0_ffn_ref(_layernorm(x, axis=-1)[None], L0_ffn_Wr, L0_ffn_br, L0_ffn_W1, L0_ffn_b1, L0_ffn_W2, L0_ffn_b2)[0]
    xn = _layernorm(x, axis=-1)
    x = x + _L1_gnn_ref(xn, src, dst, edge_attr_20, edge_weight, edge_attr_3, L1_gnn_W_in2f_s, L1_gnn_W_in2f_v, L1_gnn_Wf1, L1_gnn_bf1, L1_gnn_Wf2, L1_gnn_bf2, L1_gnn_W1_s, L1_gnn_W1_v, L1_gnn_W2_s, L1_gnn_W2_v) + _L1_mix_ref(xn[None], L1_mix_Wq, L1_mix_Wk, L1_mix_Wv, L1_mix_Wo, L1_mix_omega_q, L1_mix_omega_k)[0]
    x = x + _L1_ffn_ref(_layernorm(x, axis=-1)[None], L1_ffn_router_w, L1_ffn_w_gate, L1_ffn_w_up, L1_ffn_w_down)[0]
    return x

_drawn_inputs = setup_inputs


def setup_inputs(seed=0):
    import zlib

    import numpy as np

    out = dict(_drawn_inputs(seed))
    spreads = {'L0_gnn_bias': (0.0, 0.1),
     'L0_ffn_br': (0.0, 0.1),
     'L0_ffn_b1': (0.0, 0.352),
     'L0_ffn_b2': (0.0, 0.1)}
    factors = {'L0_mix_W_qkv': 4.084,
     'L0_mix_W_out': 4.508,
     'L1_mix_Wq': 8.0,
     'L1_mix_Wk': 8.0,
     'L1_mix_omega_q': 8.0,
     'L1_mix_omega_k': 8.0}
    for name, (base, spread) in spreads.items():
        noise = np.random.default_rng([zlib.crc32(name.encode()), seed]).standard_normal(out[name].shape)
        drawn = base * np.exp(spread * noise) if base else spread * noise
        out[name] = jnp.asarray(drawn.astype(out[name].dtype))
    for name, factor in factors.items():
        out[name] = (out[name] * factor).astype(out[name].dtype)
    return out
```

```python
from contextlib import ExitStack

import numpy as np

import concourse.bass as bass
from concourse import mybir
from concourse.bass import IndirectOffsetOnAxis, ds

ALU = mybir.AluOpType
ACT = mybir.ActivationFunctionType
AX = mybir.AxisListType
F32 = mybir.dt.float32
BF16 = mybir.dt.bfloat16
I32 = mybir.dt.int32
U32 = mybir.dt.uint32

P = 128
N, D, H = 1250, 512, 8
HD = D // H
NT, TR = 10, 125
KC = D // P
E = 40000
ER = E // TR
CHN = 2 * TR
NCH = N // CHN
BATCH = 5
GROUP = 512
Q = GROUP // P
BIG = 1e30
PAD_ROW = 999.0


def n_groups(edges):
    g = (edges + NT * (GROUP - 1)) // GROUP
    return g + g % 2


G0, G1 = n_groups(E + N), n_groups(E)
REC0, REC1 = 4, 26
F_RBF = 20


class Order:

    def __init__(self, eng, sem, base=0):
        self.eng, self.sem, self.base, self.n = eng, sem, base, 0

    def mark(self, ins):
        ins.then_inc(self.sem, 1)
        self.n += 1

    def settle(self):
        self.eng.wait_ge(self.sem, self.base + self.n)

    def link(self, ins):
        self.mark(ins)
        self.settle()


def wait_apart(eng, sem, value, passed):
    eng.wait_ge(sem, value)
    eng.sem_inc(passed, 1)


class Stage:
    used = set()

    def __init__(self, nc, name):
        self.nc, self.name, self.ctx = nc, name, ExitStack()

    def __enter__(self):
        return self

    def __exit__(self, *x):
        return self.ctx.__exit__(*x)

    def sb(self, name, shape, dt=F32):
        return self.ctx.enter_context(self.nc.sbuf_tensor(f"{self.name}_{name}", shape, dt))

    def ps(self, name, banks=1, dt=F32):
        n = banks * (512 if dt == F32 else 1024)
        return self.ctx.enter_context(self.nc.psum_tensor(f"{self.name}_{name}", [P, n], dt))

    def sem(self, name):
        sem = self.ctx.enter_context(self.nc.semaphore(f"{self.name}_{name}"))
        Stage.used.add(sem.num)
        return sem

    def pool_dma_sem(self, name):
        return self.nc.alloc_semaphore(f"{self.name}_{name}")

    def block(self):
        return self.nc.Block()


def clear_semaphores(nc):
    with nc.Block() as block:
        @block.gpsimd
        def _(pool):
            first = last = None
            for n in sorted(Stage.used) + [-1]:
                if last is not None and n != last + 1:
                    pool.sem_clear(range(first, last + 1))
                    first = None
                if first is None:
                    first = n
                last = n
    Stage.used.clear()


def mid(ap, axis, count):
    a = ap.unsqueeze(axis)
    shape = list(a.shape)
    shape[axis] = count
    return a.broadcast_to(shape)


def constants(nc, m, x):
    with Stage(nc, "const") as s:
        row_i = s.sb("row_i", [P, P], I32)
        col_i = s.sb("col_i", [P, 1], I32)
        iotas, order, loaded = s.sem("iotas"), s.sem("order"), s.sem("x_loaded")
        with s.block() as block:
            @block.sync
            def _(sp):
                sp.dma_start(m.X[:], x.rearrange("(t p) d -> p t d", p=TR)).then_inc(loaded, 16)
                sp.wait_ge(loaded, 16)

            @block.gpsimd
            def _(pool):
                nc.gpsimd.iota(row_i[:], [[1, P]], 0, 0).then_inc(iotas, 1)
                nc.gpsimd.iota(col_i[:], [[0, 1]], 0, 1).then_inc(iotas, 1)

            @block.vector
            def _(dve):
                o = Order(dve, order)
                o.mark(nc.vector.memset(m.ones[:], 1.0))
                dve.wait_ge(iotas, 2)
                o.mark(nc.vector.tensor_copy(m.iota_row[:], row_i[:]))
                o.link(nc.vector.tensor_copy(m.iota_col[:], col_i[:]))
                o.mark(nc.vector.tensor_scalar(m.ident[:], m.iota_row[:], m.iota_col[:, 0:1], None, ALU.is_equal))
                o.mark(nc.vector.tensor_scalar(m.ident_b[:], m.iota_row[:], m.iota_col[:, 0:1], None, ALU.is_equal))
                o.mark(nc.vector.tensor_scalar(m.above[:], m.iota_row[:], m.iota_col[:, 0:1], None, ALU.is_gt))


def sort_edges(nc, m, name, groups, rec, rec_dram, tile_row, load_list, n_loads, fill_rest, n_self):
    T = ER + n_self
    n_batches = T // BATCH
    positions = groups * GROUP
    W = BATCH * NT
    with Stage(nc, name) as s:
        key_i = s.sb("key_i", [TR, T], I32)
        other_i = s.sb("other_i", [TR, T], I32)
        recs = s.sb("recs", [TR, T, rec])
        key = s.sb("key", [TR, T])
        tile_of = s.sb("tile_of", [TR, T])
        row_of = s.sb("row_of", [TR, T])
        tile_hot = s.sb("tile_hot", [TR, T, NT], BF16)
        zeros = s.sb("zeros", [TR, P], BF16)
        row_hot = s.sb("row_hot", [TR, 2, BATCH, TR], BF16)
        row_hot_t = s.sb("row_hot_t", [TR, BATCH, TR], BF16)
        before = s.sb("before", [TR, BATCH, TR], BF16)
        hist = s.sb("hist", [TR, NT])
        sizes_i = s.sb("sizes_i", [TR, NT], I32)
        sizes = s.sb("sizes", [TR, NT])
        zrow = s.sb("zrow", [TR, NT])
        starts = s.sb("starts", [TR, NT])
        base = s.sb("base", [TR, NT])
        g_iota_i = s.sb("g_iota_i", [1, groups], I32)
        g_iota = s.sb("g_iota", [1, groups])
        g_tile = s.sb("g_tile", [1, groups])
        snap_i = s.sb("snap_i", [TR, BATCH + 1, NT], I32)
        low_i = s.sb("low_i", [TR, BATCH + 1, NT], I32)
        snap_hi = s.sb("snap_hi", [TR, BATCH + 1, NT], BF16)
        snap_lo = s.sb("snap_lo", [TR, BATCH + 1, NT], BF16)
        picked = s.sb("picked", [TR, BATCH, NT])
        place_f = s.sb("place_f", [TR, BATCH])
        place = s.sb("place", [TR, 2, BATCH], U32)
        staged = s.sb("staged", [TR, 2, BATCH, rec])
        pads = s.sb("pads", [P, 8, rec])
        rest = s.sb("rest", [TR, T * (REC1 - 2)]) if rec == REC1 else None
        hist_p = s.ps("hist_p")[0:TR, 0:NT]
        sums_p = s.ps("sums_p")[0:TR, 0:2 * NT].rearrange("p (k a) -> p k a", k=2)
        row_hot_p = s.ps("row_hot_p", 1, BF16)[0:TR, 0:BATCH * P].rearrange("p (j e) -> p j e", j=BATCH)
        same_p = s.ps("same_p", 2)[0:TR, :].rearrange("p (j e) -> p j e", e=P)
        snap_p = s.ps("snap_p")[0:TR, 0:(BATCH + 1) * NT].rearrange("p (j a) -> p j a", a=NT)
        rank_p = s.ps("rank_p")[0:TR, 0:BATCH * NT].rearrange("p (j a) -> p j a", a=NT)

        loaded, self_ids, padded = s.sem("loaded"), s.sem("self_ids"), s.sem("padded")
        pads_made = s.sem("pads_made")
        prep, hot_made, hist_added = s.sem("prep"), s.sem("hot_made"), s.sem("hist_added")
        hist_done, sums_done, fields = s.sem("hist_done"), s.sem("sums_done"), s.sem("fields")
        hot2_made, turned, turned_kept = s.sem("hot2_made"), s.sem("turned"), s.sem("turned_kept")
        snap_added, snap_split, same_done = s.sem("snap_added"), s.sem("snap_split"), s.sem("same_done")
        before_made, ranked, chain = s.sem("before_made"), s.sem("ranked"), s.sem("chain")
        placed, staged_full, hist_kept = s.sem("placed"), s.sem("staged_full"), s.sem("hist_kept")
        scattered = [s.pool_dma_sem(f"scattered{b}") for b in range(2)]
        past, act_past = s.sem("past"), s.sem("act_past")
        first_dram = nc.dram_tensor(f"{name}_first", [2, rec], F32).ap()

        with s.block() as block:
            @block.sync
            def _(sp):
                for dst, src in load_list(key_i, other_i, rest):
                    sp.dma_start(dst, src).then_inc(loaded, 16)
                sp.wait_ge(pads_made, 1)
                chunks = positions // (P * 8)
                for k in range(chunks):
                    sp.dma_start(rec_dram[k * P * 8:(k + 1) * P * 8, :].rearrange("(p j) w -> p j w", p=P),
                                 pads[:]).then_inc(padded, 16)
                left = positions - chunks * P * 8
                if left:
                    sp.dma_start(rec_dram[chunks * P * 8:positions, :].rearrange("(p j) w -> p j w", p=P),
                                 pads[:, 0:left // P, :]).then_inc(padded, 16)
                sp.wait_ge(loaded, 16 * n_loads)
                sp.wait_ge(padded, 16 * ((positions + P * 8 - 1) // (P * 8)))

            @block.gpsimd
            def _(pool):
                nc.gpsimd.iota(g_iota_i[:], [[1, groups]], 0, 0).then_inc(self_ids, 1)
                if n_self:
                    nc.gpsimd.iota(key_i[:, ER:T], [[TR, n_self]], 0, 1).then_inc(self_ids, 1)
                    nc.gpsimd.iota(other_i[:, ER:T], [[TR, n_self]], 0, 1).then_inc(self_ids, 1)
                chunks = (positions + P * 8 - 1) // (P * 8)
                pool.wait_ge(padded, 16 * chunks)
                for b in range(2):
                    nc.gpsimd.dma_start(first_dram[b:b + 1, :], pads[0:1, 0, :]).then_inc(scattered[b], 16)
                with pool.Fori(0, n_batches // 2) as i:
                    for b in range(2):
                        pool.wait_ge(placed, i * 2 + (b + 1))
                        wait_apart(pool, staged_full, i * 2 + (b + 1), past)
                        for j in range(BATCH):
                            nc.gpsimd.indirect_dma_start(
                                out=rec_dram[:, :], out_offset=IndirectOffsetOnAxis(ap=place[:, b, j:j + 1], axis=0),
                                in_=staged[:, b, j, :], in_offset=None).then_inc(scattered[b], 16)
                for b in range(2):
                    pool.wait_ge(scattered[b], 16 + 8 * T)

            @block.vector
            def _(dve):
                o = Order(dve, prep)
                o.mark(nc.vector.memset(zeros[:], 0.0))
                o.link(nc.vector.memset(pads[:], 0.0))
                if rec == REC1:
                    o.link(nc.vector.memset(pads[:, :, 2:5], 1.0))
                    nc.vector.memset(pads[:, :, 1:2], PAD_ROW).then_inc(pads_made, 1)
                else:
                    o.link(nc.vector.memset(recs[:], 0.0))
                    nc.vector.memset(pads[:, :, 1:3], PAD_ROW * TR).then_inc(pads_made, 1)
                o.mark(nc.vector.memset(zrow[:], 0.0))
                dve.wait_ge(loaded, 16 * n_loads)
                dve.wait_ge(self_ids, 3 if n_self else 1)
                o.mark(nc.vector.tensor_copy(g_iota[:], g_iota_i[:]))
                o.link(nc.vector.tensor_copy(key[:], key_i[:]))
                o.link(nc.vector.tensor_scalar(tile_of[:], key[:], float(TR), None, ALU.is_ge))
                for k in range(2, NT):
                    o.link(nc.vector.scalar_tensor_tensor(out=tile_of[:], in0=key[:], scalar=float(TR * k), in1=tile_of[:],
                                                          op0=ALU.is_ge, op1=ALU.add))
                o.link(nc.vector.scalar_tensor_tensor(out=row_of[:], in0=tile_of[:], scalar=-float(TR), in1=key[:],
                                                      op0=ALU.mult, op1=ALU.add))
                o.mark(nc.vector.tensor_tensor(tile_hot[:], mid(tile_of[:], 2, NT),
                                               mid(m.iota_row[0:TR, 0:NT], 1, T), ALU.is_equal))
                o.mark(nc.vector.tensor_copy(recs[:].bitcast(I32)[:, :, 0], other_i[:]))
                o.settle()
                o.link(nc.vector.tensor_copy(recs[:, :, 1], row_of[:]))
                fill_rest(key, rest, recs).then_inc(fields, 1)

                def hots(buf, t0):
                    return nc.vector.tensor_tensor(row_hot[:, buf], mid(m.iota_row[0:TR, 0:TR], 1, BATCH),
                                                   mid(row_of[:, ds(t0, BATCH)], 2, TR), ALU.is_equal)

                with dve.Fori(0, n_batches // 2) as i:
                    for b in range(2):
                        dve.wait_ge(hist_added, i * 2 + (b + 1))
                        hots(b, i * (2 * BATCH) + b * BATCH).then_inc(hot_made, 1)
                dve.wait_ge(hist_done, 1)
                nc.vector.tensor_copy(hist[:], hist_p).then_inc(hist_kept, 1)
                dve.wait_ge(sums_done, 1)
                o.link(nc.vector.tensor_scalar(sizes[:], sums_p[:, 1], float(GROUP - 1), None, ALU.add))
                o.link(nc.vector.tensor_copy(sizes_i[:], sizes[:]))
                o.link(nc.vector.tensor_scalar(sizes_i[:], sizes_i[:], 9, None, ALU.arith_shift_right))
                o.link(nc.vector.tensor_copy(sizes[:], sizes_i[:]))
                o.link(nc.vector.tensor_tensor_scan(starts[:], sizes[:], zrow[:], 0.0, ALU.add, ALU.add))
                o.link(nc.vector.tensor_tensor(starts[:], starts[:], sizes[:], ALU.subtract))
                o.link(nc.vector.scalar_tensor_tensor(out=base[:], in0=starts[:], scalar=float(GROUP), in1=sums_p[:, 0],
                                                      op0=ALU.mult, op1=ALU.add))
                o.link(nc.vector.tensor_scalar(g_tile[:], g_iota[:], starts[0:1, 1:2], None, ALU.is_ge))
                for k in range(2, NT):
                    o.link(nc.vector.scalar_tensor_tensor(out=g_tile[:], in0=g_iota[:], scalar=starts[0:1, k:k + 1],
                                                          in1=g_tile[:], op0=ALU.is_ge, op1=ALU.add))
                o.mark(nc.vector.tensor_copy(tile_row[0:1, 0:groups], g_tile[:]))
                o.link(nc.vector.tensor_copy(snap_i[:, BATCH], base[:]))
                o.link(nc.vector.tensor_scalar(low_i[:, BATCH], snap_i[:, BATCH], 255, None, ALU.bitwise_and))
                o.mark(nc.vector.tensor_copy(snap_lo[:, BATCH], low_i[:, BATCH]))
                o.settle()
                nc.vector.tensor_tensor(snap_hi[:, BATCH], snap_i[:, BATCH], low_i[:, BATCH],
                                        ALU.subtract).then_inc(snap_split, 1)

                with dve.Fori(0, n_batches // 2) as i:
                    for b in range(2):
                        n = i * 2 + b
                        c = Order(dve, chain, n * 5)
                        hots(b, i * (2 * BATCH) + b * BATCH).then_inc(hot2_made, 1)
                        dve.wait_ge(snap_added, n + 1)
                        c.link(nc.vector.tensor_copy(snap_i[:], snap_p))
                        c.link(nc.vector.tensor_scalar(low_i[:], snap_i[:], 255, None, ALU.bitwise_and))
                        c.link(nc.vector.tensor_copy(snap_lo[:], low_i[:]))
                        nc.vector.tensor_tensor(snap_hi[:], snap_i[:], low_i[:], ALU.subtract).then_inc(snap_split, 1)
                        dve.wait_ge(same_done, n + 1)
                        nc.vector.tensor_tensor(before[:], same_p[:, 0:BATCH, 0:TR], mid(m.above[0:TR, 0:TR], 1, BATCH),
                                                ALU.mult).then_inc(before_made, 1)
                        dve.wait_ge(ranked, n + 1)
                        c.link(nc.vector.tensor_tensor(picked[:], rank_p,
                                                       tile_hot[:, ds(i * (2 * BATCH) + b * BATCH, BATCH), :], ALU.mult))
                        c.link(nc.vector.tensor_reduce(place_f[:], picked[:], AX.X, ALU.add))
                        dve.wait_ge(scattered[b], i * (16 * BATCH) + 16)
                        nc.vector.tensor_copy(place[:, b], place_f[:]).then_inc(placed, 1)

            @block.scalar
            def _(act):
                act.wait_ge(fields, 1)
                with act.Fori(0, n_batches // 2) as i:
                    for b in range(2):
                        n = i * 2 + b
                        act.wait_ge(turned, n + 1)
                        nc.scalar.copy(row_hot_t[:], row_hot_p[:, :, 0:TR]).then_inc(turned_kept, 1)
                        wait_apart(act, scattered[b], i * (16 * BATCH) + 16, act_past)
                        nc.scalar.copy(staged[:, b], recs[:, ds(i * (2 * BATCH) + b * BATCH, BATCH), :]
                                       ).then_inc(staged_full, 1)

            @block.tensor
            def _(pe):
                pe.wait_ge(prep, 1)
                nc.tensor.matmul(hist_p, zeros[:, 0:TR], zeros[:, 0:NT], start=True, stop=False,
                                 skip_group_check=True).then_inc(hist_added, 2)
                with pe.Fori(0, n_batches // 2) as i:
                    for b in range(2):
                        pe.wait_ge(hot_made, i * 2 + (b + 1))
                        for j in range(BATCH):
                            last = nc.tensor.matmul(hist_p, row_hot[:, b, j],
                                                    tile_hot[:, i * (2 * BATCH) + (b * BATCH + j), :],
                                                    start=False, stop=False, skip_group_check=True)
                        last.then_inc(hist_added, 1)
                nc.tensor.matmul(hist_p, zeros[:, 0:TR], zeros[:, 0:NT], start=False, stop=True,
                                 skip_group_check=True).then_inc(hist_done, 1)
                pe.wait_ge(hist_kept, 1)
                nc.tensor.matmul(sums_p[:, 0], m.above[0:TR, 0:TR], hist[:], start=True, stop=True)
                nc.tensor.matmul(sums_p[:, 1], m.ones[0:TR, 0:TR], hist[:], start=True, stop=True).then_inc(sums_done, 1)
                with pe.Fori(0, n_batches // 2) as i:
                    for b in range(2):
                        n = i * 2 + b
                        col = [i * (2 * BATCH) + (b * BATCH + j) for j in range(BATCH)]
                        pe.wait_ge(hot2_made, n + 1)
                        for j in range(BATCH):
                            last = nc.tensor.transpose(row_hot_p[:, j, 0:TR], row_hot[:, b, j], m.ident_b[0:TR, 0:TR])
                        last.then_inc(turned, 1)
                        pe.wait_ge(snap_split, n + 1)
                        for j in range(BATCH + 1):
                            nc.tensor.matmul(snap_p[:, j], m.ident_b[0:TR, 0:TR], snap_hi[:, BATCH], start=(j == 0),
                                             stop=False, skip_group_check=True)
                            last = nc.tensor.matmul(snap_p[:, j], m.ident_b[0:TR, 0:TR], snap_lo[:, BATCH], start=False,
                                                    stop=(j == 0), skip_group_check=True)
                            for k in range(j):
                                last = nc.tensor.matmul(snap_p[:, j], row_hot[:, b, k], tile_hot[:, col[k], :],
                                                        start=False, stop=(k == j - 1), skip_group_check=True)
                        last.then_inc(snap_added, 1)
                        pe.wait_ge(turned_kept, n + 1)
                        for j in range(BATCH):
                            last = nc.tensor.matmul(same_p[:, j, 0:TR], row_hot_t[:, j], row_hot_t[:, j],
                                                    start=True, stop=True, skip_group_check=True)
                        last.then_inc(same_done, 1)
                        pe.wait_ge(snap_split, n + 2)
                        pe.wait_ge(before_made, n + 1)
                        for j in range(BATCH):
                            nc.tensor.matmul(rank_p[:, j], row_hot_t[:, j], snap_hi[:, j], start=(j == 0), stop=False,
                                             skip_group_check=True)
                            nc.tensor.matmul(rank_p[:, j], row_hot_t[:, j], snap_lo[:, j], start=False, stop=False,
                                             skip_group_check=True)
                            last = nc.tensor.matmul(rank_p[:, j], before[:, j], tile_hot[:, col[j], :], start=False,
                                                    stop=True, skip_group_check=True)
                        last.then_inc(ranked, 1)


def layer_norm(nc, m, name, src_cols):
    with Stage(nc, name) as s:
        stats = s.sb("stats", [TR, NT, 6])
        mv = s.sb("mv", [TR, NT, 2])
        rstd = s.sb("rstd", [TR, NT])
        turned_p = [s.ps(f"turned_p{b}") for b in range(2)]
        order, normed, turned, kept = s.sem("order"), s.sem("normed"), s.sem("turned"), s.sem("kept")
        var_made, std_made = s.sem("var_made"), s.sem("std_made")
        with s.block() as block:
            @block.vector
            def _(dve):
                o = Order(dve, order)
                for t in range(NT):
                    o.mark(nc.vector.bn_stats(stats[:, t], m.X[:, t]))
                o.settle()
                for t in range(NT):
                    o.mark(nc.vector.bn_aggr(mv[:, t], stats[:, t]))
                o.settle()
                nc.vector.tensor_scalar(rstd[:], mv[:, :, 1], 1e-5, None, ALU.add).then_inc(var_made, 1)
                dve.wait_ge(std_made, 1)
                o.link(nc.vector.reciprocal(rstd[:], rstd[:]))
                for t in range(NT):
                    nc.vector.tensor_scalar(m.XN[:, t], m.X[:, t], mv[:, t, 0:1], rstd[:, t:t + 1],
                                            ALU.subtract, ALU.mult).then_inc(normed, 1)

            @block.tensor
            def _(pe):
                for t in range(NT):
                    pe.wait_ge(normed, t + 1)
                    if t >= 2:
                        pe.wait_ge(kept, t - 1)
                    for c in range(KC):
                        last = nc.tensor.transpose(turned_p[t % 2][:, c * P:c * P + TR], m.XN[:, t, src_cols(c)],
                                                   m.ident[0:TR, 0:TR])
                    last.then_inc(turned, 1)

            @block.scalar
            def _(act):
                act.wait_ge(var_made, 1)
                nc.scalar.activation(rstd[:], rstd[:], ACT.Sqrt).then_inc(std_made, 1)
                for t in range(NT):
                    act.wait_ge(turned, t + 1)
                    nc.scalar.copy(m.XT[:, :, t * TR:(t + 1) * TR],
                                   turned_p[t % 2][:].rearrange("p (c n) -> p c n", c=KC)[:, :, 0:TR]).then_inc(kept, 1)


def plain(c):
    return slice(c * P, (c + 1) * P)


def by_component(c):
    return slice(0, P) if c == 0 else slice(P + c - 1, D, 3)


def chunk_rows(w, cols):
    return [w[cols(c), :] for c in range(KC)]


def attention(nc, m, name, wq, wk, wv, wo, bias=None, omegas=None):
    with Stage(nc, name) as s:
        Wq, Wk, Wv, Wo = (s.sb(n, [P, KC, D]) for n in ("Wq", "Wk", "Wv", "Wo"))
        bo = s.sb("bo", [1, D])
        QT = s.sb("QT", [P, KC, N])
        KV = s.sb("KV", [P, KC, P + 2])
        om = s.sb("om", [P, 2, P])
        pair = s.sb("pair", [P, 2])
        pair_rows = s.sb("pair_rows", [P, P])
        t1 = s.sb("t1", [P, 2, D])
        t2 = s.sb("t2", [P, 2, D])
        t3 = s.sb("t3", [P, 2, D])
        t4 = s.sb("t4", [P, 2, D])
        kt = s.sb("kt", [P, 2, KC, TR])
        kt2 = s.sb("kt2", [P, 2, KC, TR])
        kphi = s.sb("kphi", [TR, 2, D])
        vt = s.sb("vt", [TR, 2, KC, P + 1])
        den = s.sb("den", [TR, NT, H])
        att = s.sb("att", [TR, 2, D])
        att_t = s.sb("att_t", [P, 2, KC, TR])
        A = [s.ps(f"A{b}") for b in range(2)]
        B = [s.ps(f"B{b}") for b in range(2)]
        C = s.ps("C", 2)
        S = [s.ps(f"S{b}") for b in range(2)]
        loaded, ready = s.sem("loaded"), s.sem("ready")
        q_done, q_kept, f_done, f_kept = s.sem("q_done"), s.sem("q_kept"), s.sem("f_done"), s.sem("f_kept")
        q_exp, q_phi = s.sem("q_exp"), s.sem("q_phi")
        k_done, k_kept, kf_done, k_pre, k_exp, k_phi = (s.sem(n) for n in ("k_done", "k_kept", "kf_done", "k_pre", "k_exp", "k_phi"))
        v_done, v_kept, kv_added = s.sem("v_done"), s.sem("v_kept"), s.sem("kv_added")
        kv_ready, o_done, o_norm, o_turned, o_kept, y_done, y_added = (
            s.sem(n) for n in ("kv_ready", "o_done", "o_norm", "o_turned", "o_kept", "y_done", "y_added"))
        order, aorder = s.sem("order"), s.sem("aorder")
        loads = [(W[:, c], rows) for W, ws in ((Wq, wq), (Wk, wk), (Wv, wv), (Wo, wo)) for c, rows in enumerate(ws)]
        if bias is not None:
            loads.append((bo[:], bias))
        if omegas is not None:
            for k, w in enumerate(omegas):
                for h in range(2):
                    loads.append((om[h * HD:(h + 1) * HD, k, h * HD:(h + 1) * HD], w))
        n_loads = 16 * len(loads)
        n_q = NCH * 2
        L1 = omegas is not None

        with s.block() as block:
            @block.sync
            def _(sp):
                if L1:
                    sp.wait_ge(ready, 1)
                for dst, src in loads:
                    sp.dma_start(dst, src).then_inc(loaded, 16)
                sp.wait_ge(loaded, n_loads)

            @block.tensor
            def _(pe):
                pe.wait_ge(loaded, n_loads)
                pe.wait_ge(ready, 4)
                for n in range(n_q):
                    c, g = n // 2, n % 2
                    nodes = slice(c * CHN, (c + 1) * CHN)
                    if n >= 2:
                        pe.wait_ge(q_kept if L1 else q_phi, n - 1)
                    for j in range(2):
                        hp = 2 * g + j
                        for k in range(KC):
                            last = nc.tensor.matmul(A[n % 2][:, j * 256:j * 256 + CHN], Wq[:, k, hp * P:(hp + 1) * P],
                                                    m.XT[:, k, nodes], start=(k == 0), stop=(k == KC - 1))
                    last.then_inc(q_done, 1)
                    if L1:
                        pe.wait_ge(q_kept, n + 1)
                        if n >= 2:
                            pe.wait_ge(q_phi, n - 1)
                        q = t1[:, n % 2].rearrange("p (j n) -> p j n", j=2)
                        q2 = t2[:, n % 2].rearrange("p (j n) -> p j n", j=2)
                        for j in range(2):
                            nc.tensor.matmul(B[n % 2][:, j * 256:j * 256 + CHN], om[:, 0], q[:, j, 0:CHN],
                                             start=True, stop=True)
                            last = nc.tensor.matmul(S[n % 2][:, j * 256:j * 256 + CHN], pair_rows[:],
                                                    q2[:, j, 0:CHN], start=True, stop=True)
                        last.then_inc(f_done, 1)
                pe.wait_ge(q_phi, n_q)
                for t in range(NT):
                    rows = slice(t * TR, (t + 1) * TR)
                    if L1:
                        if t >= 2:
                            pe.wait_ge(k_kept, t - 1)
                        for j in range(KC):
                            for k in range(KC):
                                last = nc.tensor.matmul(A[t % 2][:, j * P:j * P + TR], Wk[:, k, j * P:(j + 1) * P],
                                                        m.XT[:, k, rows], start=(k == 0), stop=(k == KC - 1))
                        last.then_inc(k_done, 1)
                        pe.wait_ge(k_kept, t + 1)
                        if t >= 2:
                            pe.wait_ge(k_phi, t - 1)
                        for j in range(KC):
                            last = nc.tensor.matmul(S[t % 2][0:TR, j * P:(j + 1) * P], kt[:, t % 2, j], om[:, 1],
                                                    start=True, stop=True)
                        for j in range(KC):
                            last = nc.tensor.matmul(B[1][0:TR, 2 * j:2 * j + 2], kt2[:, t % 2, j], pair[:],
                                                    start=(j == 0), stop=(j == KC - 1), skip_group_check=True)
                        last.then_inc(kf_done, 1)
                    else:
                        if t >= 2:
                            pe.wait_ge(k_phi, t - 1)
                        for k in range(KC):
                            last = nc.tensor.matmul(S[t % 2][0:TR, :], m.XT[:, k, rows], Wk[:, k], start=(k == 0),
                                                    stop=(k == KC - 1))
                        last.then_inc(kf_done, 1)
                    if t >= 1:
                        pe.wait_ge(v_kept, t)
                    for k in range(KC):
                        last = nc.tensor.matmul(B[0][0:TR, :], m.XT[:, k, rows], Wv[:, k], start=(k == 0),
                                                stop=(k == KC - 1))
                    last.then_inc(v_done, 1)
                    pe.wait_ge(k_phi, t + 1)
                    pe.wait_ge(v_kept, t + 1)
                    for j in range(KC):
                        bank, off = j // 2, (j % 2) * (P + 1)
                        last = nc.tensor.matmul(C[:, bank * 512 + off:bank * 512 + off + P + 1], kphi[:, t % 2, j * P:(j + 1) * P],
                                                vt[:, t % 2, j], start=(t == 0 and j % 2 == 0), stop=(t == NT - 1),
                                                skip_group_check=True)
                    last.then_inc(kv_added, 1)
                pe.wait_ge(kv_ready, 1)
                for t in range(NT + 1):
                    if t < NT:
                        rows = slice(t * TR, (t + 1) * TR)
                        if t >= 1:
                            pe.wait_ge(o_norm, t)
                        for j in range(KC):
                            bank, off = j // 2, (j % 2) * (P + 2)
                            last = nc.tensor.matmul(C[0:TR, bank * 512 + off:bank * 512 + off + P + 2], QT[:, j, rows],
                                                    KV[:, j], start=True, stop=True, skip_group_check=True)
                        last.then_inc(o_done, 1)
                    if t >= 1:
                        u = t - 1
                        if u >= 2:
                            pe.wait_ge(o_kept, u - 1)
                        pe.wait_ge(o_norm, u + 1)
                        for j in range(KC):
                            last = nc.tensor.transpose(A[u % 2][:, j * P:j * P + TR], att[:, u % 2, j * P:(j + 1) * P],
                                                       m.ident[0:TR, 0:TR])
                        last.then_inc(o_turned, 1)
                        pe.wait_ge(o_kept, u + 1)
                        if u >= 2:
                            pe.wait_ge(y_added, u - 1)
                        for k in range(KC):
                            last = nc.tensor.matmul(B[u % 2][0:TR, :], att_t[:, u % 2, k], Wo[:, k], start=(k == 0),
                                                    stop=(k == KC - 1 and bias is None))
                        if bias is not None:
                            last = nc.tensor.matmul(B[u % 2][0:TR, :], m.ones[0:1, 0:TR], bo[:], start=False, stop=True)
                        last.then_inc(y_done, 1)

            @block.scalar
            def _(act):
                o = Order(act, aorder)
                for n in range(n_q):
                    c, g = n // 2, n % 2
                    nodes = slice(c * CHN, (c + 1) * CHN)
                    v = lambda x: x[:, n % 2].rearrange("p (j n) -> p j n", j=2)[:, :, 0:CHN]
                    w = lambda x: x[n % 2][:].rearrange("p (j n) -> p j n", j=2)[:, :, 0:CHN]
                    if L1:
                        act.wait_ge(q_done, n + 1)
                        if n >= 2:
                            act.wait_ge(q_phi, n - 1)
                        o.mark(nc.scalar.activation(v(t1), w(A), ACT.Copy, scale=HD ** -0.5))
                        o.settle()
                        nc.scalar.activation(v(t2), v(t1), ACT.Square).then_inc(q_kept, 1)
                        act.wait_ge(f_kept, n + 1)
                        nc.scalar.activation(v(t3), v(t3), ACT.Exp).then_inc(q_exp, 1)
                        nc.scalar.activation(v(t4), v(t4), ACT.Exp).then_inc(q_exp, 1)
                    else:
                        act.wait_ge(f_kept, n + 1)
                        nc.scalar.activation(v(t1), v(t1), ACT.Exp).then_inc(q_exp, 1)
                for t in range(NT):
                    if L1:
                        act.wait_ge(k_done, t + 1)
                        if t >= 2:
                            act.wait_ge(kf_done, t - 1)
                        x = A[t % 2][:].rearrange("p (j n) -> p j n", j=KC)[:, :, 0:TR]
                        o.mark(nc.scalar.activation(kt[:, t % 2], x, ACT.Copy, scale=HD ** -0.5))
                        o.settle()
                        nc.scalar.activation(kt2[:, t % 2], kt[:, t % 2], ACT.Square).then_inc(k_kept, 1)
                        act.wait_ge(k_pre, t + 1)
                        nc.scalar.activation(t3[0:TR, t % 2, 0:H], t3[0:TR, t % 2, 0:H], ACT.Exp).then_inc(k_exp, 1)
                        nc.scalar.activation(t1[0:TR, t % 2], t1[0:TR, t % 2], ACT.Exp).then_inc(k_exp, 1)
                    else:
                        act.wait_ge(k_pre, t + 1)
                        nc.scalar.activation(t1[0:TR, t % 2], t1[0:TR, t % 2], ACT.Exp).then_inc(k_exp, 1)
                    act.wait_ge(v_done, t + 1)
                    if t >= 2:
                        act.wait_ge(kv_added, t - 1)
                    nc.scalar.copy(vt[:, t % 2, :, 0:P], B[0][0:TR, :].rearrange("p (j n) -> p j n", j=KC)
                                   ).then_inc(v_kept, 1)
                for t in range(NT):
                    act.wait_ge(o_turned, t + 1)
                    if t >= 2:
                        act.wait_ge(y_done, t - 1)
                    nc.scalar.copy(att_t[:, t % 2], A[t % 2][:].rearrange("p (j n) -> p j n", j=KC)[:, :, 0:TR]
                                   ).then_inc(o_kept, 1)

            @block.vector
            def _(dve):
                o = Order(dve, order)
                nc.vector.memset(om[:], 0.0).then_inc(ready, 1)
                o.mark(nc.vector.memset(KV[:], 0.0))
                nc.vector.memset(vt[:], 1.0).then_inc(ready, 1)
                o.link(nc.vector.tensor_scalar(pair[:, 1:2], m.iota_col[:, 0:1], float(HD), None, ALU.is_ge))
                o.link(nc.vector.tensor_scalar(pair[:, 0:1], m.iota_col[:, 0:1], float(HD), None, ALU.is_lt))
                nc.vector.tensor_scalar(pair_rows[:, 0:HD], m.ones[:, 0:HD], pair[:, 0:1], None, ALU.mult).then_inc(ready, 1)
                nc.vector.tensor_scalar(pair_rows[:, HD:P], m.ones[:, 0:HD], pair[:, 1:2], None, ALU.mult).then_inc(ready, 1)
                for n in range(n_q):
                    c, g = n // 2, n % 2
                    nodes = slice(c * CHN, (c + 1) * CHN)
                    v = lambda x: x[:, n % 2].rearrange("p (j n) -> p j n", j=2)[:, :, 0:CHN]
                    w = lambda x: x[n % 2][:].rearrange("p (j n) -> p j n", j=2)[:, :, 0:CHN]
                    out = QT[:, 2 * g:2 * g + 2, nodes]
                    if L1:
                        dve.wait_ge(f_done, n + 1)
                        if n >= 2:
                            o.settle()
                        o.mark(nc.vector.tensor_scalar(v(t3), w(B), 50.0, None, ALU.min))
                        nc.vector.tensor_scalar(v(t4), w(S), 1e-16, -0.5, ALU.max, ALU.mult).then_inc(f_kept, 1)
                        dve.wait_ge(q_exp, 2 * n + 2)
                        nc.vector.scalar_tensor_tensor(out=out, in0=v(t4), scalar=1e-8, in1=v(t3), op0=ALU.max,
                                                       op1=ALU.mult).then_inc(q_phi, 1)
                    else:
                        dve.wait_ge(q_done, n + 1)
                        if n >= 2:
                            dve.wait_ge(q_phi, n - 1)
                        nc.vector.tensor_scalar(v(t1), w(A), 0.0, None, ALU.min).then_inc(f_kept, 1)
                        dve.wait_ge(q_exp, n + 1)
                        nc.vector.scalar_tensor_tensor(out=out, in0=w(A), scalar=0.0, in1=v(t1), op0=ALU.max,
                                                       op1=ALU.add).then_inc(q_phi, 1)
                dve.wait_ge(q_phi, n_q)
                for t in range(NT):
                    dve.wait_ge(kf_done, t + 1)
                    f, k = S[t % 2][0:TR, :], kphi[:, t % 2]
                    if t >= 2:
                        dve.wait_ge(k_phi, t - 1)
                        dve.wait_ge(kv_added, t - 1)
                    if L1:
                        o.mark(nc.vector.tensor_scalar(t1[0:TR, t % 2], f, 50.0, None, ALU.min))
                        nc.vector.tensor_scalar(t3[0:TR, t % 2, 0:H], B[1][0:TR, 0:H], 1e-16, -0.5, ALU.max,
                                                ALU.mult).then_inc(k_pre, 1)
                        dve.wait_ge(k_exp, 2 * t + 2)
                        o.link(nc.vector.tensor_scalar(t4[0:TR, t % 2, 0:H], t3[0:TR, t % 2, 0:H], 1e-8, None, ALU.max))
                        nc.vector.tensor_tensor(k.rearrange("p (h d) -> p h d", h=H),
                                                t1[0:TR, t % 2].rearrange("p (h d) -> p h d", h=H),
                                                mid(t4[0:TR, t % 2, 0:H], 2, HD), ALU.mult).then_inc(k_phi, 1)
                    else:
                        nc.vector.tensor_scalar(t1[0:TR, t % 2], f, 0.0, None, ALU.min).then_inc(k_pre, 1)
                        dve.wait_ge(k_exp, t + 1)
                        nc.vector.scalar_tensor_tensor(out=k, in0=f, scalar=0.0, in1=t1[0:TR, t % 2], op0=ALU.max,
                                                       op1=ALU.add).then_inc(k_phi, 1)
                dve.wait_ge(kv_added, NT)
                for j in range(KC):
                    off = (j // 2) * 512 + (j % 2) * (P + 1)
                    for h in range(2):
                        r = slice(h * HD, (h + 1) * HD)
                        o.mark(nc.vector.tensor_copy(KV[r, j, r], C[r, off + h * HD:off + (h + 1) * HD]))
                        last = nc.vector.tensor_copy(KV[r, j, P + h:P + h + 1], C[r, off + P:off + P + 1])
                        if j == KC - 1 and h == 1:
                            last.then_inc(kv_ready, 1)
                        else:
                            o.mark(last)
                o.settle()
                for t in range(NT):
                    dve.wait_ge(o_done, t + 1)
                    if t >= 2:
                        dve.wait_ge(o_turned, t - 1)
                    for b in range(2):
                        x = C[0:TR, b * 512:b * 512 + 2 * (P + 2)].rearrange("p (j n) -> p j n", j=2)
                        dn = den[:, t, 4 * b:4 * b + 4].rearrange("p (j h) -> p j h", j=2)
                        o.link(nc.vector.tensor_scalar(dn, x[:, :, P:P + 2], 0.0 if L1 else 1e-6, None, ALU.add))
                    o.link(nc.vector.reciprocal(den[:, t], den[:, t]))
                    for b in range(2):
                        x = C[0:TR, b * 512:b * 512 + 2 * (P + 2)].rearrange("p (j n) -> p j n", j=2)[:, :, 0:P]
                        for j in range(2):
                            hs = 4 * b + 2 * j
                            last = nc.vector.tensor_tensor(
                                att[:, t % 2, hs * HD:(hs + 2) * HD].rearrange("p (h d) -> p h d", h=2),
                                x[:, j].rearrange("p (h d) -> p h d", h=2), mid(den[:, t, hs:hs + 2], 2, HD), ALU.mult)
                            if b == 1 and j == 1:
                                last.then_inc(o_norm, 1)
                            else:
                                o.mark(last)
                    if t >= 1:
                        dve.wait_ge(y_done, t)
                        nc.vector.tensor_tensor(m.X[:, t - 1], m.X[:, t - 1], B[(t - 1) % 2][0:TR, :],
                                                ALU.add).then_inc(y_added, 1)
                dve.wait_ge(y_done, NT)
                nc.vector.tensor_tensor(m.X[:, NT - 1], m.X[:, NT - 1], B[(NT - 1) % 2][0:TR, :],
                                        ALU.add).then_inc(y_added, 1)


def node_table(nc, m, name, weights, blocks, scale, table, keep):
    with Stage(nc, name) as s:
        Ws = [s.sb(f"W{k}", [P, len(w), w[0].shape[1]]) for k, w in enumerate(weights)]
        rows_sb = s.sb("rows", [TR, 2, D])
        out_p = [s.ps(f"out_p{b}") for b in range(2)]
        keep_p = [s.ps(f"keep_p{b}") for b in range(2)]
        loaded, done, copied, stored = s.sem("loaded"), s.sem("done"), s.sem("copied"), [s.sem(f"stored{b}") for b in range(2)]
        keep_done, kept = s.sem("keep_done"), s.sem("kept")
        loads = [(W[:, c], rows) for W, ws in zip(Ws, weights) for c, rows in enumerate(ws)]
        with s.block() as block:
            @block.sync
            def _(sp):
                for dst, src in loads:
                    sp.dma_start(dst, src).then_inc(loaded, 16)
                for t in range(NT):
                    sp.wait_ge(copied, t + 1)
                    sp.dma_start(table[t * TR:(t + 1) * TR, :], rows_sb[:, t % 2]).then_inc(stored[t % 2], 16)
                for b in range(2):
                    sp.wait_ge(stored[b], 16 * NT // 2)

            @block.tensor
            def _(pe):
                pe.wait_ge(loaded, 16 * len(loads))
                for t in range(NT):
                    rows = slice(t * TR, (t + 1) * TR)
                    if t >= 2:
                        pe.wait_ge(copied, t - 1)
                    for cols, pairs in blocks:
                        for i, (c, w, k) in enumerate(pairs):
                            last = nc.tensor.matmul(out_p[t % 2][0:TR, cols], m.XT[:, c, rows], Ws[w][:, k],
                                                    start=(i == 0), stop=(i == len(pairs) - 1), skip_group_check=True)
                    last.then_inc(done, 1)
                    if keep is not None:
                        if t >= 2:
                            pe.wait_ge(kept, t - 1)
                        for k in range(KC):
                            last = nc.tensor.matmul(keep_p[t % 2][0:TR, :], m.XT[:, k, rows], Ws[1][:, k],
                                                    start=(k == 0), stop=(k == KC - 1))
                        last.then_inc(keep_done, 1)

            @block.scalar
            def _(act):
                for t in range(NT):
                    act.wait_ge(done, t + 1)
                    if t >= 2:
                        act.wait_ge(stored[t % 2], 16 * (t // 2))
                    nc.scalar.activation(rows_sb[:, t % 2], out_p[t % 2][0:TR, :], ACT.Copy, scale=scale).then_inc(copied, 1)

            @block.vector
            def _(dve):
                if keep is not None:
                    for t in range(NT):
                        dve.wait_ge(keep_done, t + 1)
                        nc.vector.tensor_copy(keep[:, t], keep_p[t % 2][0:TR, :]).then_inc(kept, 1)


def edge_scores(nc, m, XR, att_w, XL_dram, rec_dram, alpha_dram):
    with Stage(nc, "scores") as s:
        recs = s.sb("recs", [P, G0, Q * REC0])
        alpha = s.sb("alpha", [P, G0, Q * H])
        att = s.sb("att", [P, D])
        att_r = s.sb("att_r", [1, D])
        idx = s.sb("idx", [P, 2, Q], U32)
        xl = s.sb("xl", [P, 2, Q * D])
        hot = s.sb("hot", [P, 2, Q, TR])
        past = s.sem("past")
        hot_t = s.sb("hot_t", [TR, 2, Q, P])
        z = s.sb("z", [P, Q * D])
        z2 = s.sb("z2", [P, Q * D])
        turned_p = s.ps("turned_p")
        z_p = s.ps("z_p", Q)
        att_p = s.ps("att_p")
        loaded, att_done, att_kept = s.sem("loaded"), s.sem("att_done"), s.sem("att_kept")
        gathered = [s.pool_dma_sem(f"gathered{b}") for b in range(2)]
        idx_ready, hot_made, turned, kept = s.sem("idx_ready"), s.sem("hot_made"), s.sem("turned"), s.sem("kept")
        z_done, z_read, chain, stored = s.sem("z_done"), s.sem("z_read"), s.sem("chain"), s.sem("stored")
        scored = [s.sem(f"scored{b}") for b in range(2)]
        with s.block() as block:
            @block.sync
            def _(sp):
                sp.dma_start(att_r[:], att_w.rearrange("h c -> (h c)").unsqueeze(0)).then_inc(loaded, 16)
                sp.dma_start(recs[:], rec_dram.rearrange("(g p q) w -> p g (q w)", p=P, q=Q)).then_inc(loaded, 16)
                for b in range(2):
                    sp.wait_ge(scored[b], G0 // 2 + 1)
                sp.dma_start(alpha_dram.rearrange("(g p q) h -> p g (q h)", p=P, q=Q), alpha[:]).then_inc(stored, 16)
                sp.wait_ge(stored, 16)

            @block.gpsimd
            def _(pool):
                pool.wait_ge(loaded, 32)
                with pool.Fori(0, G0 // 2) as i:
                    for b in range(2):
                        rows = recs[:, i * 2 + b, :].rearrange("p (q w) -> p q w", w=REC0)
                        pool.wait_ge(scored[b], i + 1)
                        nc.gpsimd.tensor_copy(idx[:, b], rows.bitcast(U32)[:, :, 0]).then_inc(idx_ready, 1)
                        wait_apart(pool, idx_ready, i * 2 + (b + 1), past)
                        for q in range(Q):
                            nc.gpsimd.indirect_dma_start(
                                out=xl[:, b, q * D:(q + 1) * D], out_offset=None, in_=XL_dram[:, :],
                                in_offset=IndirectOffsetOnAxis(ap=idx[:, b, q:q + 1], axis=0)).then_inc(gathered[b], 16)

            @block.vector
            def _(dve):
                dve.sem_inc(z_read, 1)
                for b in range(2):
                    dve.sem_inc(scored[b], 1)
                dve.wait_ge(att_done, 1)
                nc.vector.tensor_copy(att[:], att_p[:]).then_inc(att_kept, 1)
                dve.wait_ge(att_kept, 1)
                dve.wait_ge(loaded, 32)
                with dve.Fori(0, G0 // 2) as i:
                    for b in range(2):
                        n = i * 2 + b
                        c = Order(dve, chain, n * 2)
                        rows = recs[:, n, :].rearrange("p (q w) -> p q w", w=REC0)
                        nc.vector.tensor_tensor(hot[:, b], mid(m.iota_row[:, 0:TR], 1, Q), mid(rows[:, :, 1], 2, TR),
                                                ALU.is_equal).then_inc(hot_made, 1)
                        dve.wait_ge(z_done, n + 1)
                        dve.wait_ge(gathered[b], i * (16 * Q) + 16 * Q)
                        nc.vector.tensor_tensor(z[:], z_p[:], xl[:, b], ALU.add).then_inc(z_read, 1)
                        dve.wait_ge(z_read, n + 2)
                        c.link(nc.vector.scalar_tensor_tensor(out=z2[:], in0=z[:], scalar=0.2, in1=z[:], op0=ALU.mult,
                                                              op1=ALU.max))
                        c.link(nc.vector.tensor_tensor(z[:].rearrange("p (q d) -> p q d", q=Q),
                                                       z2[:].rearrange("p (q d) -> p q d", q=Q), mid(att[:], 1, Q), ALU.mult))
                        nc.vector.tensor_reduce(alpha[:, n, :], z[:].rearrange("p (k d) -> p k d", d=HD), AX.X,
                                                ALU.add).then_inc(scored[b], 1)
                        dve.wait_ge(scored[b], i + 2)

            @block.scalar
            def _(act):
                with act.Fori(0, G0 // 2) as i:
                    for b in range(2):
                        n = i * 2 + b
                        act.wait_ge(turned, n + 1)
                        nc.scalar.copy(hot_t[:, b], turned_p[0:TR, :].rearrange("p (q e) -> p q e", q=Q)).then_inc(kept, 1)

            @block.tensor
            def _(pe):
                pe.wait_ge(loaded, 32)
                nc.tensor.matmul(att_p[:], m.ones[0:1, :], att_r[:], start=True, stop=True).then_inc(att_done, 1)
                with pe.Fori(0, G0 // 2) as i:
                    for b in range(2):
                        n = i * 2 + b
                        pe.wait_ge(hot_made, n + 1)
                        for q in range(Q):
                            last = nc.tensor.transpose(turned_p[0:TR, q * P:(q + 1) * P], hot[:, b, q], m.ident[:])
                        last.then_inc(turned, 1)
                        tile = nc.tensor.value_load(m.tile0[0:1, ds(n, 1)], min_val=0, max_val=NT - 1)
                        pe.wait_ge(kept, n + 1)
                        pe.wait_ge(z_read, n + 1)
                        for q in range(Q):
                            last = nc.tensor.matmul(z_p[:, q * D:(q + 1) * D], hot_t[:, b, q], XR[:, tile, :],
                                                    start=True, stop=True)
                        last.then_inc(z_done, 1)


def edge_weights(nc, m, rec_dram, alpha_dram, weight_dram):
    L = G0 * GROUP // P
    with Stage(nc, "weights") as s:
        a = s.sb("a", [P, L, H])
        recs = s.sb("recs", [P, L, REC0])
        mx = s.sb("mx", [P, L, H])
        bw = s.sb("bw", [P, L])
        cut_f = s.sb("cut_f", [P, L])
        cut_b = s.sb("cut_b", [P, L])
        at_first = s.sb("at_first", [P, L])
        at_last = s.sb("at_last", [P, L])
        ends = s.sb("ends", [P, 4, H])
        rows = s.sb("rows", [H, 4, P])
        cut = s.sb("cut", [H, 4, P])
        run = s.sb("run", [H, 2, P])
        carry = s.sb("carry", [H, 2, P])
        carried = s.sb("carried", [P, 2, H])
        ends_p, back_p = s.ps("ends_p"), s.ps("back_p")
        loaded, order, ends_made, ends_turned = s.sem("loaded"), s.sem("order"), s.sem("ends_made"), s.sem("ends_turned")
        carry_made, carry_turned, shifted, expd, stored = (s.sem(n) for n in ("carry_made", "carry_turned", "shifted", "expd", "stored"))
        with s.block() as block:
            @block.sync
            def _(sp):
                sp.dma_start(a[:], alpha_dram.rearrange("(p l) h -> p l h", p=P)).then_inc(loaded, 16)
                sp.dma_start(recs[:], rec_dram.rearrange("(p l) w -> p l w", p=P)).then_inc(loaded, 16)
                sp.wait_ge(loaded, 32)
                sp.wait_ge(expd, 1)
                sp.dma_start(weight_dram.rearrange("(p l) h -> p l h", p=P), a[:]).then_inc(stored, 16)
                sp.wait_ge(stored, 16)

            @block.vector
            def _(dve):
                o = Order(dve, order)
                node = recs[:, :, 2]

                def penalty(out, x, y):
                    o.link(nc.vector.tensor_tensor(out, x, y, ALU.is_equal))
                    o.link(nc.vector.tensor_scalar(out, out, BIG, -BIG, ALU.mult, ALU.add))

                dve.wait_ge(loaded, 32)
                o.mark(nc.vector.memset(cut_f[:], -BIG))
                o.mark(nc.vector.memset(cut_b[:], -BIG))
                o.mark(nc.vector.memset(cut[:], -BIG))
                o.mark(nc.vector.memset(carry[:], -BIG))
                o.settle()
                penalty(cut_f[:, 1:L], node[:, 1:L], node[:, 0:L - 1])
                o.link(nc.vector.tensor_copy(cut_b[:, 0:L - 1], cut_f[:, 1:L]))
                for h in range(H):
                    o.mark(nc.vector.tensor_tensor_scan(mx[:, :, h], cut_f[:], a[:, :, h], -BIG, ALU.add, ALU.max))
                o.settle()
                o.mark(nc.vector.tensor_copy(ends[:, 0], mx[:, L - 1]))
                for h in range(H):
                    o.link(nc.vector.tensor_tensor_scan(bw[:, ::-1], cut_b[:, ::-1], a[:, ::-1, h], -BIG, ALU.add, ALU.max))
                    o.mark(nc.vector.tensor_copy(ends[:, 1, h:h + 1], bw[:, 0:1]))
                    o.link(nc.vector.tensor_tensor(mx[:, :, h], mx[:, :, h], bw[:], ALU.max))
                o.mark(nc.vector.tensor_copy(ends[:, 2], node[:, 0:1].broadcast_to([P, H])))
                o.mark(nc.vector.tensor_copy(ends[:, 3], node[:, L - 1:L].broadcast_to([P, H])))
                o.settle()
                nc.vector.memset(bw[:, 0:1], 0.0).then_inc(ends_made, 1)
                dve.wait_ge(ends_turned, 1)
                o.link(nc.vector.tensor_copy(rows[:], ends_p[0:H, :].rearrange("p (k n) -> p k n", k=4)))
                first, last_ = rows[:, 2], rows[:, 3]
                penalty(cut[:, 0, 1:P], first[:, 1:P], last_[:, 0:P - 1])
                o.link(nc.vector.tensor_copy(cut[:, 1, 0:P - 1], cut[:, 0, 1:P]))
                penalty(cut[:, 2], first, last_)
                o.link(nc.vector.tensor_tensor(cut[:, 3], cut[:, 2], cut[:, 1], ALU.min))
                o.link(nc.vector.tensor_tensor(cut[:, 2], cut[:, 2], cut[:, 0], ALU.min))
                o.mark(nc.vector.tensor_tensor_scan(run[:, 0], cut[:, 2], rows[:, 0], -BIG, ALU.add, ALU.max))
                o.link(nc.vector.tensor_tensor_scan(run[:, 1, ::-1], cut[:, 3, ::-1], rows[:, 1, ::-1], -BIG,
                                                    ALU.add, ALU.max))
                o.mark(nc.vector.tensor_tensor(carry[:, 0, 1:P], run[:, 0, 0:P - 1], cut[:, 0, 1:P], ALU.add))
                o.mark(nc.vector.tensor_tensor(carry[:, 1, 0:P - 1], run[:, 1, 1:P], cut[:, 1, 0:P - 1], ALU.add))
                o.settle()
                nc.vector.memset(run[:, 0, 0:1], 0.0).then_inc(carry_made, 1)
                dve.wait_ge(carry_turned, 1)
                o.link(nc.vector.tensor_copy(carried[:], back_p[:, 0:2 * H].rearrange("p (k h) -> p k h", k=2)))
                for out, j in ((at_first, 0), (at_last, L - 1)):
                    o.link(nc.vector.tensor_scalar(out[:], node, recs[:, j, 2:3], None, ALU.is_equal))
                    o.link(nc.vector.tensor_scalar(out[:], out[:], BIG, -BIG, ALU.mult, ALU.add))
                for k, pen in enumerate((at_first, at_last)):
                    for h in range(H):
                        o.mark(nc.vector.scalar_tensor_tensor(out=mx[:, :, h], in0=pen[:], scalar=carried[:, k, h:h + 1],
                                                              in1=mx[:, :, h], op0=ALU.add, op1=ALU.max))
                    o.settle()
                nc.vector.tensor_tensor(a[:], a[:], mx[:], ALU.subtract).then_inc(shifted, 1)

            @block.tensor
            def _(pe):
                pe.wait_ge(ends_made, 1)
                for k in range(4):
                    last = nc.tensor.transpose(ends_p[0:H, k * P:(k + 1) * P], ends[:, k], m.ident[:])
                last.then_inc(ends_turned, 1)
                pe.wait_ge(carry_made, 1)
                for k in range(2):
                    last = nc.tensor.transpose(back_p[:, k * H:(k + 1) * H], carry[:, k], m.ident[0:H, 0:H])
                last.then_inc(carry_turned, 1)

            @block.scalar
            def _(act):
                act.wait_ge(shifted, 1)
                nc.scalar.activation(a[:], a[:], ACT.Exp).then_inc(expd, 1)


def edge_sums(nc, m, bias, XL_dram, rec_dram, weight_dram):
    W = D + H
    with Stage(nc, "sums") as s:
        recs = s.sb("recs", [P, G0, Q * REC0])
        wts = s.sb("wts", [P, G0, Q * H])
        idx = s.sb("idx", [P, 2, Q], U32)
        xl = s.sb("xl", [P, 2, Q * D])
        msg = s.sb("msg", [P, 2, Q, W])
        hot = s.sb("hot", [P, 2, Q, TR])
        past = s.sem("past")
        acc = s.sb("acc", [TR, NT, W])
        bias_r = s.sb("bias_r", [1, D])
        g1 = s.sb("g1", [TR, 2, D])
        sum_p = [s.ps(f"sum_p{b}", 2) for b in range(2)]
        bias_p = s.ps("bias_p")
        loaded, acc_zero, bias_done = s.sem("loaded"), s.sem("acc_zero"), s.sem("bias_done")
        gathered = [s.pool_dma_sem(f"gathered{b}") for b in range(2)]
        idx_ready, summed, added = s.sem("idx_ready"), s.sem("summed"), s.sem("added")
        msg_made = [s.sem(f"msg_made{b}") for b in range(2)]
        order, pre, expd = s.sem("order"), s.sem("pre"), s.sem("expd")
        with s.block() as block:
            @block.sync
            def _(sp):
                sp.dma_start(bias_r[:], bias.unsqueeze(0)).then_inc(loaded, 16)
                sp.dma_start(recs[:], rec_dram.rearrange("(g p q) w -> p g (q w)", p=P, q=Q)).then_inc(loaded, 16)
                sp.dma_start(wts[:], weight_dram.rearrange("(g p q) h -> p g (q h)", p=P, q=Q)).then_inc(loaded, 16)
                sp.wait_ge(loaded, 48)

            @block.gpsimd
            def _(pool):
                pool.wait_ge(loaded, 48)
                with pool.Fori(0, G0 // 2) as i:
                    for b in range(2):
                        rows = recs[:, i * 2 + b, :].rearrange("p (q w) -> p q w", w=REC0)
                        pool.wait_ge(msg_made[b], i * 3 + 1)
                        nc.gpsimd.tensor_copy(idx[:, b], rows.bitcast(U32)[:, :, 0]).then_inc(idx_ready, 1)
                        wait_apart(pool, idx_ready, i * 2 + (b + 1), past)
                        for q in range(Q):
                            nc.gpsimd.indirect_dma_start(
                                out=xl[:, b, q * D:(q + 1) * D], out_offset=None, in_=XL_dram[:, :],
                                in_offset=IndirectOffsetOnAxis(ap=idx[:, b, q:q + 1], axis=0)).then_inc(gathered[b], 16)

            @block.vector
            def _(dve):
                for b in range(2):
                    dve.sem_inc(msg_made[b], 1)
                nc.vector.memset(acc[:], 0.0).then_inc(acc_zero, 1)
                dve.wait_ge(acc_zero, 1)
                dve.wait_ge(loaded, 48)
                with dve.Fori(0, G0 // 2) as i:
                    for b in range(2):
                        n = i * 2 + b
                        rows = recs[:, n, :].rearrange("p (q w) -> p q w", w=REC0)
                        w = wts[:, n, :]
                        nc.vector.tensor_tensor(hot[:, b], mid(m.iota_row[:, 0:TR], 1, Q), mid(rows[:, :, 1], 2, TR),
                                                ALU.is_equal).then_inc(msg_made[b], 1)
                        nc.vector.tensor_copy(msg[:, b, :, D:W], w.rearrange("p (q h) -> p q h", q=Q)).then_inc(msg_made[b], 1)
                        dve.wait_ge(gathered[b], i * (16 * Q) + 16 * Q)
                        nc.vector.tensor_tensor(
                            msg[:, b, :, 0:D].rearrange("p q (h d) -> p q h d", h=H),
                            xl[:, b].rearrange("p (q h d) -> p q h d", q=Q, h=H),
                            mid(w.rearrange("p (q h) -> p q h", q=Q), 3, HD), ALU.mult).then_inc(msg_made[b], 1)
                        tile = nc.vector.value_load(m.tile0[0:1, ds(n, 1)], min_val=0, max_val=NT - 1)
                        dve.wait_ge(summed, n + 1)
                        nc.vector.tensor_tensor(acc[:, tile, :], acc[:, tile, :], sum_p[b][0:TR, 0:W],
                                                ALU.add).then_inc(added, 1)
                        dve.wait_ge(added, n + 1)
                o = Order(dve, order)
                for t in range(NT):
                    den = acc[:, t, D:W]
                    o.mark(nc.vector.tensor_scalar(den, den, 1e-16, None, ALU.max))
                o.settle()
                o.link(nc.vector.reciprocal(acc[:, :, D:W], acc[:, :, D:W]))
                dve.wait_ge(bias_done, 1)
                for t in range(NT):
                    x = acc[:, t, 0:D]
                    o.link(nc.vector.tensor_tensor(x.rearrange("p (h d) -> p h d", h=H), x.rearrange("p (h d) -> p h d", h=H),
                                                   mid(acc[:, t, D:W], 2, HD), ALU.mult))
                    o.link(nc.vector.tensor_tensor(x, x, bias_p[0:TR, :], ALU.add))
                    if t >= 2:
                        o.settle()
                    nc.vector.tensor_scalar(g1[:, t % 2], x, 0.0, None, ALU.min).then_inc(pre, 1)
                    o.mark(nc.vector.tensor_scalar(x, x, 0.0, -1.0, ALU.max, ALU.add))
                    o.mark(nc.vector.tensor_tensor(m.X[:, t], m.X[:, t], m.XN[:, t], ALU.add))
                    o.settle()
                    dve.wait_ge(expd, t + 1)
                    o.link(nc.vector.tensor_tensor(x, x, g1[:, t % 2], ALU.add))
                    o.link(nc.vector.tensor_tensor(m.X[:, t], m.X[:, t], x, ALU.add))

            @block.scalar
            def _(act):
                for t in range(NT):
                    act.wait_ge(pre, t + 1)
                    nc.scalar.activation(g1[:, t % 2], g1[:, t % 2], ACT.Exp).then_inc(expd, 1)

            @block.tensor
            def _(pe):
                pe.wait_ge(loaded, 48)
                nc.tensor.matmul(bias_p[:], m.ones[0:1, :], bias_r[:], start=True, stop=True).then_inc(bias_done, 1)
                with pe.Fori(0, G0 // 2) as i:
                    for b in range(2):
                        n = i * 2 + b
                        pe.wait_ge(msg_made[b], i * 3 + 4)
                        for q in range(Q):
                            nc.tensor.matmul(sum_p[b][0:TR, 0:D], hot[:, b, q], msg[:, b, q, 0:D], start=(q == 0),
                                             stop=(q == Q - 1))
                            last = nc.tensor.matmul(sum_p[b][0:TR, D:W], hot[:, b, q], msg[:, b, q, D:W],
                                                    start=(q == 0), stop=(q == Q - 1))
                        last.then_inc(summed, 1)


def experts(nc, m, name, n_out, gated, w1s, w2, route, n_exp, b1=None, b2=None):
    F = w1s[0].shape[2]
    FC = F // P
    n1 = len(w1s)
    with Stage(nc, name) as s:
        W1 = [[s.sb(f"W1_{k}_{b}", [P, KC, F]) for k in range(n1)] for b in range(2)]
        W2 = [s.sb(f"W2_{b}", [P, FC, D]) for b in range(2)]
        b2_r = [s.sb(f"b2_{b}", [1, D]) for b in range(2)] if b2 is not None else None
        b1_c = s.sb("b1_c", [P, n_exp, FC]) if b1 is not None else None
        hid = s.sb("hid", [P, 2, FC, CHN])
        gate = s.sb("gate", [P, 2, CHN])
        Wr = s.sb("Wr", [P, KC, n_exp])
        r_rows = s.sb("r_rows", [n_exp, D]) if gated else None
        br = s.sb("br", [1, n_exp])
        wts = s.sb("wts", [TR, NT, n_exp])
        tmp = [s.sb(f"tmp{k}", [TR, NT, n_exp]) for k in range(3)]
        small = s.sb("small", [TR, 6, NT])
        cur = s.sb("cur", [TR, 2, NT])
        up_p = [[s.ps(f"up_p{k}_{b}") for b in range(2)] for k in range(n1)]
        y_p = [s.ps(f"y_p{b}") for b in range(2)]
        log_p = s.ps("log_p")
        r_loaded = s.sem("r_loaded")
        w_loaded = [s.sem(f"w_loaded{b}") for b in range(2)]
        r_turned, r_kept, logged, shifted, expd, routed = (s.sem(n) for n in ("r_turned", "r_kept", "logged", "shifted", "expd", "routed"))
        up_done, gate_made, hid_made, y_added, cur_made, order = (
            s.sem(n) for n in ("up_done", "gate_made", "hid_made", "y_added", "cur_made", "order"))
        y_done = [s.sem(f"y_done{b}") for b in range(2)]
        act_past = s.sem("act_past")
        b1_rows = s.sb("b1_rows", [n_exp * FC, P]) if b1 is not None else None
        n_up = NCH * FC
        per_load = 16 * (n1 + 1 + (b2 is not None))
        n_route = 16 * (route.n_loads + (b1 is not None))

        with s.block() as block:
            @block.sync
            def _(sp):
                route.load(sp, r_loaded, Wr, r_rows, br)
                if b1 is not None:
                    sp.dma_start(b1_rows[:], b1.rearrange("e (c p) -> (e c) p", p=P)).then_inc(r_loaded, 16)
                with sp.Fori(0, n_exp // 2) as i:
                    for b in range(2):
                        e = i * 2 + b
                        sp.wait_ge(y_done[b], i * NT + 1)
                        for k in range(n1):
                            sp.dma_start(W1[b][k][:], w1s[k][e].rearrange("(c p) f -> p c f", p=P)).then_inc(w_loaded[b], 16)
                        sp.dma_start(W2[b][:], w2[e].rearrange("(c p) f -> p c f", p=P)).then_inc(w_loaded[b], 16)
                        if b2 is not None:
                            sp.dma_start(b2_r[b][:], b2[e].unsqueeze(0)).then_inc(w_loaded[b], 16)
                sp.wait_ge(r_loaded, n_route)

            @block.tensor
            def _(pe):
                for b in range(2):
                    pe.sem_inc(y_done[b], 1)
                pe.wait_ge(r_loaded, n_route)
                if gated:
                    for c in range(KC):
                        last = nc.tensor.transpose(y_p[0][:, c * n_exp:(c + 1) * n_exp], r_rows[:, c * P:(c + 1) * P],
                                                   m.ident[0:n_exp, 0:n_exp])
                    last.then_inc(r_turned, 1)
                    pe.wait_ge(r_kept, 1)
                else:
                    nc.tensor.transpose(y_p[0][:, 0:n_exp * FC], b1_rows[:],
                                        m.ident[0:n_exp * FC, 0:n_exp * FC]).then_inc(r_turned, 1)
                for t in range(NT):
                    for k in range(KC):
                        last = nc.tensor.matmul(log_p[0:TR, t * n_exp:(t + 1) * n_exp], m.XT[:, k, t * TR:(t + 1) * TR],
                                                Wr[:, k], start=(k == 0), stop=(k == KC - 1 and gated), skip_group_check=True)
                    if not gated:
                        last = nc.tensor.matmul(log_p[0:TR, t * n_exp:(t + 1) * n_exp], m.ones[0:1, 0:TR], br[:],
                                                start=False, stop=True, skip_group_check=True)
                last.then_inc(logged, 1)
                with pe.Fori(0, n_exp // 2) as i:
                    for b in range(2):
                        e = i * 2 + b
                        pe.wait_ge(w_loaded[b], i * per_load + per_load)
                        for c in range(NCH):
                            for f in range(FC):
                                n = c * FC + f
                                pe.wait_ge(hid_made, e * n_up + (n + 1))
                                for w in range(n1):
                                    for k in range(KC):
                                        last = nc.tensor.matmul(up_p[w][n % 2][:, 0:CHN], W1[b][w][:, k, f * P:(f + 1) * P],
                                                                m.XT[:, k, c * CHN:(c + 1) * CHN], start=(k == 0),
                                                                stop=(k == KC - 1))
                                last.then_inc(up_done, 1)
                            pe.wait_ge(hid_made, e * n_up + ((c + 1) * FC + 2))
                            for r in range(2):
                                t = 2 * c + r
                                pe.wait_ge(y_added, e * NT + (t + 1))
                                for f in range(FC):
                                    last = nc.tensor.matmul(y_p[t % 2][0:TR, :], hid[:, c % 2, f, r * TR:(r + 1) * TR],
                                                            W2[b][:, f], start=(f == 0), stop=(f == FC - 1 and b2 is None))
                                if b2 is not None:
                                    last = nc.tensor.matmul(y_p[t % 2][0:TR, :], m.ones[0:1, 0:TR], b2_r[b][:],
                                                            start=False, stop=True)
                                last.then_inc(y_done[b], 1)

            @block.scalar
            def _(act):
                route.act(act, shifted, expd, tmp, small)
                if not gated:
                    act.sem_inc(hid_made, 2)
                    act.wait_ge(r_kept, 1)
                with act.Fori(0, n_exp // 2) as i:
                    for b in range(2):
                        e = i * 2 + b
                        for c in range(NCH):
                            for f in range(FC):
                                n = c * FC + f
                                if not gated:
                                    wait_apart(act, up_done, e * n_up + (n + 1), act_past)
                                else:
                                    act.wait_ge(up_done, e * n_up + (n + 1))
                                if gated:
                                    act.wait_ge(hid_made, e * n_up + (n + 1))
                                    nc.scalar.activation(gate[:, n % 2], up_p[0][n % 2][:, 0:CHN], ACT.Silu
                                                         ).then_inc(gate_made, 1)
                                else:
                                    nc.scalar.activation(hid[:, c % 2, f], up_p[0][n % 2][:, 0:CHN], ACT.Relu,
                                                         bias=b1_c[:, e, f:f + 1]
                                                         ).then_inc(hid_made, 1)

            @block.vector
            def _(dve):
                o = Order(dve, order)
                if gated:
                    dve.sem_inc(hid_made, 2)
                dve.wait_ge(r_turned, 1)
                if gated:
                    nc.vector.tensor_copy(Wr[:], y_p[0][:, 0:KC * n_exp].rearrange("p (c e) -> p c e", c=KC)).then_inc(r_kept, 1)
                else:
                    nc.vector.tensor_copy(b1_c[:], y_p[0][:, 0:n_exp * FC].rearrange("p (e c) -> p e c", c=FC)
                                          ).then_inc(r_kept, 1)
                    dve.wait_ge(r_kept, 1)
                dve.sem_inc(y_added, 2)
                dve.wait_ge(logged, 1)
                route.weigh(nc, dve, o, log_p[0:TR, 0:NT * n_exp].rearrange("p (t e) -> p t e", t=NT), wts, tmp, small,
                            shifted, expd)
                o.settle()
                with dve.Fori(0, n_exp // 2) as i:
                    for b in range(2):
                        e = i * 2 + b
                        nc.vector.tensor_copy(cur[:, b], wts[:, :, e]).then_inc(cur_made, 1)
                        dve.wait_ge(cur_made, e + 1)
                        for c in range(NCH):
                            if gated:
                                for f in range(FC):
                                    n = c * FC + f
                                    dve.wait_ge(gate_made, e * n_up + (n + 1))
                                    nc.vector.tensor_tensor(hid[:, c % 2, f], gate[:, n % 2], up_p[1][n % 2][:, 0:CHN],
                                                            ALU.mult).then_inc(hid_made, 1)
                            for r in range(2):
                                t = 2 * c + r
                                dve.wait_ge(y_done[b], i * NT + (t + 2))
                                nc.vector.scalar_tensor_tensor(out=m.X[:, t], in0=y_p[t % 2][0:TR, :],
                                                               scalar=cur[:, b, t:t + 1], in1=m.X[:, t], op0=ALU.mult,
                                                               op1=ALU.add).then_inc(y_added, 1)


def first_of(nc, o, hit, out, taken):
    o.link(nc.vector.tensor_copy(out[:, :, 0], hit[:, :, 0]))
    o.link(nc.vector.tensor_copy(taken, hit[:, :, 0]))
    for e in range(1, out.shape[2]):
        o.link(nc.vector.tensor_tensor(out[:, :, e], hit[:, :, e], taken, ALU.is_gt))
        o.link(nc.vector.tensor_tensor(taken, taken, hit[:, :, e], ALU.max))


class Top1:
    n_loads = 2

    def __init__(self, Wr, br):
        self.Wr, self.br = Wr, br

    def load(self, sp, sem, Wr, r_rows, br):
        sp.dma_start(Wr[:], self.Wr.rearrange("(c p) e -> p c e", p=P)).then_inc(sem, 16)
        sp.dma_start(br[:], self.br.unsqueeze(0)).then_inc(sem, 16)

    def act(self, act, shifted, expd, tmp, small):
        act.wait_ge(shifted, 1)
        act.activation(tmp[1][:], tmp[0][:], ACT.Exp).then_inc(expd, 1)

    def weigh(self, nc, dve, o, logits, wts, tmp, small, shifted, expd):
        n = logits.shape[2]
        o.link(nc.vector.tensor_reduce(small[:, 0], logits, AX.X, ALU.max))
        nc.vector.tensor_tensor(tmp[0][:], logits, mid(small[:, 0], 2, n), ALU.subtract).then_inc(shifted, 1)
        dve.wait_ge(expd, 1)
        o.mark(nc.vector.tensor_reduce(small[:, 1], tmp[1][:], AX.X, ALU.add))
        o.link(nc.vector.tensor_reduce(small[:, 2], tmp[1][:], AX.X, ALU.max))
        o.mark(nc.vector.tensor_tensor(tmp[0][:], tmp[1][:], mid(small[:, 2], 2, n), ALU.is_ge))
        o.mark(nc.vector.reciprocal(small[:, 1], small[:, 1]))
        o.settle()
        o.link(nc.vector.tensor_tensor(small[:, 3], small[:, 1], small[:, 2], ALU.mult))
        first_of(nc, o, tmp[0], tmp[2], small[:, 4])
        o.link(nc.vector.tensor_tensor(wts[:], tmp[2][:], mid(small[:, 3], 2, n), ALU.mult))


class Top2:
    n_loads = 1

    def __init__(self, router):
        self.router = router

    def load(self, sp, sem, Wr, r_rows, br):
        sp.dma_start(r_rows[:], self.router).then_inc(sem, 16)

    def act(self, act, shifted, expd, tmp, small):
        act.wait_ge(shifted, 1)
        act.activation(small[:, 2], small[:, 2], ACT.Exp).then_inc(expd, 1)

    def weigh(self, nc, dve, o, logits, wts, tmp, small, shifted, expd):
        n = logits.shape[2]
        o.link(nc.vector.tensor_reduce(small[:, 0], logits, AX.X, ALU.max))
        o.link(nc.vector.tensor_tensor(tmp[0][:], logits, mid(small[:, 0], 2, n), ALU.is_ge))
        first_of(nc, o, tmp[0], tmp[1], small[:, 4])
        o.link(nc.vector.scalar_tensor_tensor(out=tmp[2][:], in0=tmp[1][:], scalar=-BIG, in1=logits, op0=ALU.mult,
                                              op1=ALU.add))
        o.link(nc.vector.tensor_reduce(small[:, 1], tmp[2][:], AX.X, ALU.max))
        o.link(nc.vector.tensor_tensor(tmp[0][:], tmp[2][:], mid(small[:, 1], 2, n), ALU.is_ge))
        first_of(nc, o, tmp[0], tmp[2], small[:, 4])
        nc.vector.tensor_tensor(small[:, 2], small[:, 1], small[:, 0], ALU.subtract).then_inc(shifted, 1)
        dve.wait_ge(expd, 1)
        o.link(nc.vector.tensor_scalar(small[:, 3], small[:, 2], 1.0, None, ALU.add))
        o.link(nc.vector.reciprocal(small[:, 3], small[:, 3]))
        o.link(nc.vector.tensor_tensor(small[:, 2], small[:, 2], small[:, 3], ALU.mult))
        o.link(nc.vector.tensor_tensor(tmp[1][:], tmp[1][:], mid(small[:, 3], 2, n), ALU.mult))
        o.link(nc.vector.tensor_tensor(tmp[2][:], tmp[2][:], mid(small[:, 2], 2, n), ALU.mult))
        o.link(nc.vector.tensor_tensor(wts[:], tmp[1][:], tmp[2][:], ALU.add))


F1 = 128
Y0 = float(1.0 / np.sqrt(4.0 * np.pi))
Y1 = float(np.sqrt(3.0 / (4.0 * np.pi)))
MW = 9 * F1


def convolution(nc, m, Wf1, bf1, Wf2, bf2, W1_s, W1_v, W2_s, W2_v, table, rec_dram):
    with Stage(nc, "conv") as s:
        agg = s.sb("agg", [TR, NT, 8 * F1])
        conv_edges(nc, m, agg, Wf1, bf1, Wf2, bf2, table, rec_dram)
        conv_nodes(nc, m, agg, W1_s, W1_v, W2_s, W2_v)


def conv_edges(nc, m, agg, Wf1, bf1, Wf2, bf2, table, rec_dram):
    with Stage(nc, "edges") as s:
        recs = s.sb("recs", [P, G1, Q * REC1])
        wf1 = s.sb("wf1", [F_RBF, F1])
        wf2_in = s.sb("wf2_in", [P, 4 * F1])
        wf2 = s.sb("wf2", [P, 4, F1])
        bf1_c = s.sb("bf1_c", [P, 1])
        bf2_in = s.sb("bf2_in", [3, 4 * F1])
        bf2_r = s.sb("bf2_r", [3, 4 * F1])
        bf2_k = [s.sb(f"bf2_k{k}", [3, 4 * F1], BF16) for k in range(3)]
        bf2_s = s.sb("bf2_s", [3, 4 * F1], BF16)
        ones_b = s.sb("ones_b", [3, P], BF16)
        part = s.sb("part", [3, 3])
        norm = s.sb("norm", [P, G1 * Q])
        idx = s.sb("idx", [P, 2, Q], U32)
        rows_g = s.sb("rows_g", [P, 2, Q, D])
        hot = s.sb("hot", [P, 2, Q, TR])
        past = s.sem("past")
        fs = s.sb("fs", [P, Q, F_RBF])
        ft = s.sb("ft", [F_RBF, Q * P])
        ab = s.sb("ab", [P, Q * P])
        hx = s.sb("hx", [P, Q * P])
        half = s.sb("half", [P, 1])
        ht = s.sb("ht", [P, Q * P])
        msg = s.sb("msg", [P, Q, MW])
        dot = s.sb("dot", [P, Q, F1])
        vy = s.sb("vy", [P, Q, 3, F1])
        f_p = s.ps("f_p")
        h_p = s.ps("h_p")
        w_p = s.ps("w_p", 4)
        sum_p = s.ps("sum_p", 2)
        names = ("loaded", "prep", "sq_made", "norm_made", "idx_ready", "hot_made", "f_staged", "f_turned", "f_kept",
                 "h_done", "h_ln", "h_made", "w_done", "c_made", "vector_made", "msg_made", "summed",
                 "added", "chain", "rows_used0", "rows_used1", "aorder")
        S = {n: s.sem(n) for n in names}
        root_made, act_past = s.sem("root_made"), s.sem("act_past")
        (loaded, prep, sq_made, norm_made, idx_ready, hot_made, f_staged, f_turned, f_kept, h_done, h_ln,
         h_made, w_done, c_made, vector_made, msg_made, summed, added, chain, used0, used1, aorder) = (S[n] for n in names)
        rows_used = [used0, used1]
        gathered = [s.pool_dma_sem(f"gathered{b}") for b in range(2)]
        rec4 = recs[:].rearrange("p g (q w) -> p g q w", q=Q)
        recf = recs[:].rearrange("p g (q w) -> p (g q) w", q=Q)
        n_loads = 4 + 3

        with s.block() as block:
            @block.sync
            def _(sp):
                sp.dma_start(recs[:], rec_dram.rearrange("(g p q) w -> p g (q w)", p=P, q=Q)).then_inc(loaded, 16)
                sp.dma_start(wf1[:], Wf1).then_inc(loaded, 16)
                sp.dma_start(wf2_in[:], Wf2[:, 0:4 * F1]).then_inc(loaded, 16)
                sp.dma_start(bf1_c[:], bf1.rearrange("(p o) -> p o", o=1)).then_inc(loaded, 16)
                for k in range(3):
                    sp.dma_start(bf2_in[k:k + 1, :], bf2[0:4 * F1].unsqueeze(0)).then_inc(loaded, 16)
                sp.wait_ge(loaded, 16 * n_loads)

            @block.gpsimd
            def _(pool):
                pool.wait_ge(loaded, 16 * n_loads)
                with pool.Fori(0, G1 // 2) as i:
                    for b in range(2):
                        rows = recs[:, i * 2 + b, :].rearrange("p (q w) -> p q w", q=Q)
                        pool.wait_ge(rows_used[b], i + 1)
                        nc.gpsimd.tensor_copy(idx[:, b], rows.bitcast(U32)[:, :, 0]).then_inc(idx_ready, 1)
                        wait_apart(pool, idx_ready, i * 2 + (b + 1), past)
                        for q in range(Q):
                            nc.gpsimd.indirect_dma_start(
                                out=rows_g[:, b, q, :], out_offset=None, in_=table[:, :],
                                in_offset=IndirectOffsetOnAxis(ap=idx[:, b, q:q + 1], axis=0)).then_inc(gathered[b], 16)

            @block.vector
            def _(dve):
                o = Order(dve, prep)
                for b in range(2):
                    dve.sem_inc(rows_used[b], 1)
                o.mark(nc.vector.memset(agg[:], 0.0))
                o.mark(nc.vector.memset(ones_b[:], 1.0))
                o.mark(nc.vector.memset(half[:], 0.5))
                for k in range(3):
                    o.mark(nc.vector.tensor_scalar(part[:, k:k + 1], m.iota_col[0:3, 0:1], float(k), None, ALU.is_equal))
                dve.wait_ge(loaded, 16 * n_loads)
                for slot, off in ((0, 2 * F1), (1, 0), (2, 1), (3, 2 * F1 + 1)):
                    pick = slice(off, off - off % 2 + 2 * F1, 2)
                    o.mark(nc.vector.tensor_copy(wf2[:, slot], wf2_in[:, pick]))
                    o.mark(nc.vector.tensor_copy(bf2_r[:, slot * F1:(slot + 1) * F1], bf2_in[:, pick]))
                o.settle()
                for k in range(3):
                    o.link(nc.vector.tensor_copy(bf2_k[k][:], bf2_r[:]))
                    if k < 2:
                        o.link(nc.vector.tensor_tensor(bf2_r[:], bf2_r[:], bf2_k[k][:], ALU.subtract))
                o.link(nc.vector.tensor_scalar(bf2_s[:], bf2_k[0][:], part[:, 0:1], None, ALU.mult))
                for k in (1, 2):
                    o.link(nc.vector.scalar_tensor_tensor(out=bf2_s[:], in0=bf2_k[k][:], scalar=part[:, k:k + 1],
                                                          in1=bf2_s[:], op0=ALU.mult, op1=ALU.add))
                sq = vy[:].rearrange("p q i f -> p (q i f)")[:, 0:G1 * Q]
                o.link(nc.vector.tensor_tensor(norm[:], recf[:, :, 2], recf[:, :, 2], ALU.mult))
                for k in (3, 4):
                    o.link(nc.vector.tensor_tensor(sq, recf[:, :, k], recf[:, :, k], ALU.mult))
                    o.link(nc.vector.tensor_tensor(norm[:], norm[:], sq, ALU.add))
                nc.vector.memset(dot[:, 0, 0:1], 0.0).then_inc(sq_made, 1)
                dve.wait_ge(root_made, 1)
                o.link(nc.vector.reciprocal(norm[:], norm[:]))
                o.link(nc.vector.tensor_scalar(norm[:], norm[:], Y1, None, ALU.mult))
                nc.vector.tensor_tensor(recf[:, :, 2:5], recf[:, :, 2:5], mid(norm[:], 2, 3), ALU.mult).then_inc(norm_made, 1)
                dve.wait_ge(norm_made, 1)
                with dve.Fori(0, G1 // 2) as i:
                    for b in range(2):
                        n = i * 2 + b
                        c = Order(dve, chain, n * 5)
                        rec = recs[:, n, :].rearrange("p (q w) -> p q w", q=Q)
                        c.link(nc.vector.tensor_tensor(hot[:, b], mid(m.iota_row[:, 0:TR], 1, Q), mid(rec[:, :, 1], 2, TR),
                                                       ALU.is_equal))
                        nc.vector.tensor_tensor(hot[:, b], hot[:, b], mid(rec[:, :, 5], 2, TR), ALU.mult).then_inc(hot_made, 1)
                        dve.wait_ge(h_ln, n + 1)
                        nc.vector.scalar_tensor_tensor(out=ht[:], in0=hx[:], scalar=0.0, in1=ab[:], op0=ALU.max,
                                                       op1=ALU.add).then_inc(h_made, 1)
                        dve.wait_ge(gathered[b], i * (16 * Q) + 16 * Q)
                        v = rows_g[:, b, :, F1:D].rearrange("p q (i f) -> p q i f", i=3)
                        wp = w_p[:].rearrange("p (q k f) -> p q k f", q=Q, k=4)
                        c.link(nc.vector.tensor_tensor(vy[:], v, mid(rec[:, :, 2:5], 3, F1), ALU.mult))
                        c.link(nc.vector.tensor_tensor(dot[:], vy[:, :, 0], vy[:, :, 1], ALU.add))
                        c.link(nc.vector.tensor_tensor(dot[:], dot[:], vy[:, :, 2], ALU.add))
                        dve.wait_ge(w_done, n + 1)
                        nc.vector.tensor_tensor(msg[:, :, 0:2 * F1].rearrange("p q (k f) -> p q k f", k=2),
                                                mid(rows_g[:, b, :, 0:F1], 2, 2), wp[:, :, 0:2], ALU.mult).then_inc(c_made, 1)
                        c.mark(nc.vector.tensor_tensor(msg[:, :, 2 * F1:3 * F1], dot[:], wp[:, :, 2], ALU.mult))
                        nc.vector.tensor_tensor(msg[:, :, 6 * F1:9 * F1].rearrange("p q (i f) -> p q i f", i=3), v,
                                                mid(wp[:, :, 3], 2, 3), ALU.mult).then_inc(rows_used[b], 1)
                        tile = nc.vector.value_load(m.tile1[0:1, ds(n, 1)], min_val=0, max_val=NT - 1)
                        dve.wait_ge(summed, n + 1)
                        nc.vector.tensor_tensor(agg[:, tile, :], agg[:, tile, :], sum_p[0:TR, :], ALU.add).then_inc(added, 1)
                        dve.wait_ge(added, n + 1)

            @block.scalar
            def _(act):
                act.wait_ge(sq_made, 1)
                nc.scalar.activation(norm[:], norm[:], ACT.Sqrt).then_inc(root_made, 1)
                act.wait_ge(norm_made, 1)
                with act.Fori(0, G1 // 2) as i:
                    for b in range(2):
                        n = i * 2 + b
                        rec = recs[:, n, :].rearrange("p (q w) -> p q w", q=Q)
                        nc.scalar.copy(fs[:], rec[:, :, 6:6 + F_RBF]).then_inc(f_staged, 1)
                        act.wait_ge(f_turned, n + 1)
                        nc.scalar.copy(ft[:], f_p[0:F_RBF, :]).then_inc(f_kept, 1)
                        act.wait_ge(h_done, n + 1)
                        a = Order(act, aorder, n * 3)
                        a.link(nc.scalar.activation(hx[:], h_p[:], ACT.Identity, bias=bf1_c[:, 0:1]))
                        a.link(nc.scalar.activation(ab[:], hx[:], ACT.Abs))
                        a.link(nc.scalar.activation(ab[:], ab[:], ACT.Exp, scale=-1.0))
                        nc.scalar.activation(ab[:], ab[:], ACT.Ln, bias=half[:, 0:1], scale=0.5).then_inc(h_ln, 1)
                        wait_apart(act, c_made, n + 1, act_past)
                        for q in range(Q):
                            for k in range(3):
                                last = nc.scalar.activation(msg[:, q, (3 + k) * F1:(4 + k) * F1], msg[:, q, 0:F1], ACT.Copy,
                                                            scale=rec[:, q, 2 + k:3 + k])
                        last.then_inc(vector_made, 1)

            @block.tensor
            def _(pe):
                pe.wait_ge(norm_made, 1)
                with pe.Fori(0, G1 // 2) as i:
                    for b in range(2):
                        n = i * 2 + b
                        pe.wait_ge(f_staged, n + 1)
                        for q in range(Q):
                            last = nc.tensor.transpose(f_p[0:F_RBF, q * P:(q + 1) * P], fs[:, q], m.ident[:])
                        last.then_inc(f_turned, 1)
                        pe.wait_ge(f_kept, n + 1)
                        nc.tensor.matmul(h_p[:], wf1[:], ft[:], start=True, stop=True).then_inc(h_done, 1)
                        pe.wait_ge(h_made, n + 1)
                        for q in range(Q):
                            nc.tensor.matmul(w_p[:, q * 512:(q + 1) * 512], ht[:, q * P:(q + 1) * P],
                                             wf2[:].rearrange("p k f -> p (k f)"), start=True, stop=False)
                            last = nc.tensor.matmul(w_p[:, q * 512:(q + 1) * 512], ones_b[:], bf2_s[:], start=False, stop=True)
                        last.then_inc(w_done, 1)
                        pe.wait_ge(hot_made, n + 1)
                        pe.wait_ge(rows_used[b], i + 2)
                        pe.wait_ge(vector_made, n + 1)
                        for k in range(2):
                            for q in range(Q):
                                last = nc.tensor.matmul(sum_p[0:TR, k * 512:(k + 1) * 512], hot[:, b, q],
                                                        msg[:, q, F1 + k * 512:F1 + (k + 1) * 512], start=(q == 0),
                                                        stop=(q == Q - 1))
                        last.then_inc(summed, 1)


def conv_nodes(nc, m, agg, W1_s, W1_v, W2_s, W2_v):
    with Stage(nc, "nodes") as s:
        w1 = s.sb("w1", [P, 4, F1])
        w2 = s.sb("w2", [P, 2, F1])
        agg_t = s.sb("agg_t", [P, 8, TR])
        u = s.sb("u", [P, 4, TR])
        ab = s.sb("ab", [P, TR])
        half = s.sb("half", [P, 1])
        t_p = s.ps("t_p", 2)
        u_p = s.ps("u_p")
        y_p = s.ps("y_p")
        names = ("loaded", "prep", "turned", "kept", "u_done", "u_ln", "u_made", "y_done", "added", "aorder")
        loaded, prep, turned, kept, u_done, u_ln, u_made, y_done, added, aorder = (s.sem(n) for n in names)
        with s.block() as block:
            @block.sync
            def _(sp):
                for k, w in enumerate((W1_s[0:2 * F1:2, :], W1_s[1:2 * F1:2, :], W1_v[0:2 * F1:2, :], W1_v[1:2 * F1:2, :])):
                    sp.dma_start(w1[:, k], w).then_inc(loaded, 16)
                for k, w in enumerate((W2_s, W2_v)):
                    sp.dma_start(w2[:, k], w).then_inc(loaded, 16)
                sp.wait_ge(loaded, 96)

            @block.vector
            def _(dve):
                dve.wait_ge(loaded, 96)
                r = (2 * F1) ** -0.5
                for k, f in enumerate((Y0 * r, 3.0 ** -0.5 * r, r, Y0 * r)):
                    nc.vector.tensor_scalar(w1[:, k], w1[:, k], f, None, ALU.mult).then_inc(prep, 1)
                nc.vector.memset(half[:], 0.5).then_inc(prep, 1)
                nc.vector.tensor_scalar(w2[:], w2[:], F1 ** -0.5, None, ALU.mult).then_inc(prep, 1)
                for t in range(NT):
                    dve.wait_ge(u_ln, t + 1)
                    nc.vector.scalar_tensor_tensor(out=u[:, 0], in0=u[:, 0], scalar=0.0, in1=ab[:], op0=ALU.max,
                                                   op1=ALU.add).then_inc(u_made, 1)
                    dve.wait_ge(y_done, t + 1)
                    nc.vector.tensor_tensor(m.X[:, t, 0:F1], m.X[:, t, 0:F1], y_p[0:TR, 0:F1], ALU.add).then_inc(added, 1)
                    x = m.X[:, t, F1:D].rearrange("p (d i) -> p i d", i=3)
                    nc.vector.tensor_tensor(x, x, y_p[0:TR, F1:D].rearrange("p (i d) -> p i d", i=3), ALU.add
                                            ).then_inc(added, 1)

            @block.scalar
            def _(act):
                act.wait_ge(prep, 6)
                for t in range(NT):
                    act.wait_ge(turned, t + 1)
                    nc.scalar.copy(agg_t[:], t_p[:].rearrange("p (k n) -> p k n", k=8)[:, :, 0:TR]).then_inc(kept, 1)
                    act.wait_ge(u_done, t + 1)
                    a = Order(act, aorder, 3 * t)
                    a.link(nc.scalar.copy(u[:], u_p[:, 0:4 * TR].rearrange("p (k n) -> p k n", k=4)))
                    a.link(nc.scalar.activation(ab[:], u[:, 0], ACT.Abs))
                    a.link(nc.scalar.activation(ab[:], ab[:], ACT.Exp, scale=-1.0))
                    nc.scalar.activation(ab[:], ab[:], ACT.Ln, bias=half[:, 0:1], scale=0.5).then_inc(u_ln, 1)

            @block.tensor
            def _(pe):
                pe.wait_ge(prep, 6)
                for t in range(NT):
                    for k in range(8):
                        last = nc.tensor.transpose(t_p[:, k * P:k * P + TR], agg[:, t, k * F1:(k + 1) * F1],
                                                   m.ident[0:TR, 0:TR])
                    last.then_inc(turned, 1)
                    pe.wait_ge(kept, t + 1)
                    nc.tensor.matmul(u_p[:, 0:TR], w1[:, 0], agg_t[:, 0], start=True, stop=False, skip_group_check=True)
                    nc.tensor.matmul(u_p[:, 0:TR], w1[:, 1], agg_t[:, 1], start=False, stop=True, skip_group_check=True)
                    vec = u_p[:, TR:4 * TR]
                    nc.tensor.matmul(vec, w1[:, 2], agg_t[:, 2:5].rearrange("p k n -> p (k n)"), start=False, stop=False,
                                     skip_group_check=True)
                    nc.tensor.matmul(vec, w1[:, 3], agg_t[:, 5:8].rearrange("p k n -> p (k n)"), start=False, stop=True,
                                     skip_group_check=True).then_inc(u_done, 1)
                    pe.wait_ge(u_made, t + 1)
                    if t >= 1:
                        pe.wait_ge(added, 2 * t)
                    for k in range(4):
                        last = nc.tensor.matmul(y_p[0:TR, k * F1:(k + 1) * F1], u[:, k], w2[:, min(k, 1)],
                                                start=True, stop=True, skip_group_check=True)
                    last.then_inc(y_done, 1)


def store(nc, m, out):
    with Stage(nc, "store") as s:
        stored = s.sem("stored")
        with s.block() as block:
            @block.sync
            def _(sp):
                sp.dma_start(out.rearrange("(t p) d -> p t d", p=TR), m.X[:]).then_inc(stored, 16)
                sp.wait_ge(stored, 16)


class Memory:

    def __init__(self, s):
        self.X = s.sb("X", [TR, NT, D])
        self.XN = s.sb("XN", [TR, NT, D])
        self.XT = s.sb("XT", [P, KC, N])
        self.iota_row = s.sb("iota_row", [P, P])
        self.iota_col = s.sb("iota_col", [P, 1])
        self.ident = s.sb("ident", [P, P])
        self.ident_b = s.sb("ident_b", [P, P], BF16)
        self.above = s.sb("above", [P, P])
        self.ones = s.sb("ones", [P, P])
        self.tile0 = s.sb("tile0", [1, G0], I32)
        self.tile1 = s.sb("tile1", [1, G1], I32)


def gps_kernel(nc, i, out, stop=99):
    rec0 = nc.dram_tensor("rec0", [G0 * GROUP, REC0], F32).ap()
    rec1 = nc.dram_tensor("rec1", [G1 * GROUP, REC1], F32).ap()
    XL = nc.dram_tensor("XL", [N, D], F32).ap()
    T1 = nc.dram_tensor("T1", [N, D], F32).ap()
    alpha = nc.dram_tensor("alpha", [G0 * GROUP, H], F32).ap()
    weight = nc.dram_tensor("weight", [G0 * GROUP, H], F32).ap()
    by_row = lambda v: v.rearrange("(p t) -> p t", p=TR)

    Stage.used.clear()
    with Stage(nc, "all") as s:
        m = Memory(s)
        constants(nc, m, i["x"])

        sort_edges(nc, m, "sort0", G0, REC0, rec0, m.tile0,
                   lambda key, other, rest: [(key[:, 0:ER], by_row(i["dst"])), (other[:, 0:ER], by_row(i["src"]))], 2,
                   lambda key, rest, recs: nc.vector.tensor_copy(recs[:, :, 2], key[:]), N // TR)

        def loads1(key, other, rest):
            return [(key[:], by_row(i["src"])), (other[:], by_row(i["dst"])),
                    (rest[:, 0:3 * ER], i["edge_attr_3"].rearrange("(p t) c -> p (t c)", p=TR)),
                    (rest[:, 3 * ER:4 * ER], by_row(i["edge_weight"])),
                    (rest[:, 4 * ER:24 * ER], i["edge_attr_20"].rearrange("(p t) c -> p (t c)", p=TR))]

        def fill1(key, rest, recs):
            nc.vector.tensor_copy(recs[:, :, 2:5], rest[:, 0:3 * ER].rearrange("p (t c) -> p t c", c=3))
            nc.vector.tensor_copy(recs[:, :, 5], rest[:, 3 * ER:4 * ER])
            return nc.vector.tensor_copy(recs[:, :, 6:26], rest[:, 4 * ER:24 * ER].rearrange("p (t c) -> p t c", c=F_RBF))

        sort_edges(nc, m, "sort1", G1, REC1, rec1, m.tile1, loads1, 5, fill1, 0)

        layer_norm(nc, m, "norm0", plain)
        wqkv = i["L0_mix_W_qkv"]
        if stop >= 1:
            part = lambda k: [wqkv[c * P:(c + 1) * P, k * D:(k + 1) * D] for c in range(KC)]
            attention(nc, m, "mix0", part(0), part(1), part(2), chunk_rows(i["L0_mix_W_out"], plain),
                      bias=i["L0_mix_b_out"].unsqueeze(0))
        if stop >= 2:
            with Stage(nc, "gat") as g:
                XR = g.sb("XR", [TR, NT, D])
                node_table(nc, m, "lr", [chunk_rows(i["L0_gnn_W_l"], plain), chunk_rows(i["L0_gnn_W_r"], plain)],
                           [(slice(0, D), [(c, 0, c) for c in range(KC)])], 1.0, XL, XR)
                edge_scores(nc, m, XR, i["L0_gnn_att"], XL, rec0, alpha)
            edge_weights(nc, m, rec0, alpha, weight)
            edge_sums(nc, m, i["L0_gnn_bias"], XL, rec0, weight)
        if stop >= 3:
            layer_norm(nc, m, "norm1", plain)
            experts(nc, m, "moe0", D, False, [i["L0_ffn_W1"]], i["L0_ffn_W2"], Top1(i["L0_ffn_Wr"], i["L0_ffn_br"]), 8,
                    b1=i["L0_ffn_b1"], b2=i["L0_ffn_b2"])
        clear_semaphores(nc)
        if stop >= 4:
            layer_norm(nc, m, "norm2", by_component)
            sc, vc = i["L1_gnn_W_in2f_s"], i["L1_gnn_W_in2f_v"]
            node_table(nc, m, "t1", [[sc, vc]], [(slice(c * P, (c + 1) * P), [(c, 0, min(c, 1))]) for c in range(KC)],
                       F1 ** -0.5, T1, None)
            rows = lambda n: chunk_rows(i[n], by_component)
            attention(nc, m, "mix1", rows("L1_mix_Wq"), rows("L1_mix_Wk"), rows("L1_mix_Wv"),
                      chunk_rows(i["L1_mix_Wo"], plain), omegas=(i["L1_mix_omega_q"], i["L1_mix_omega_k"]))
        if stop >= 5:
            convolution(nc, m, i["L1_gnn_Wf1"], i["L1_gnn_bf1"], i["L1_gnn_Wf2"], i["L1_gnn_bf2"], i["L1_gnn_W1_s"],
                        i["L1_gnn_W1_v"], i["L1_gnn_W2_s"], i["L1_gnn_W2_v"], T1, rec1)
        if stop >= 6:
            layer_norm(nc, m, "norm3", plain)
            experts(nc, m, "moe1", D, True, [i["L1_ffn_w_gate"], i["L1_ffn_w_up"]], i["L1_ffn_w_down"],
                    Top2(i["L1_ffn_router_w"]), 8)
        store(nc, m, out)


def kernel(**inputs):
    import numpy as _np
    from concourse import bacc as _bacc
    from concourse.bass_utils import run_bass_kernel_spmd as _run

    nc = _bacc.Bacc("TRN2", target_bir_lowering=False, num_devices=1)
    arrays, aps = {}, {}
    for name, value in inputs.items():
        a = _np.ascontiguousarray(value)
        arrays[f"in_{name}"] = a
        aps[name] = nc.dram_tensor(f"in_{name}", a.shape, mybir.dt.from_np(a.dtype), kind="ExternalInput").ap()
    out = nc.dram_tensor("out", (N, D), F32, kind="ExternalOutput").ap()
    gps_kernel(nc, aps, out)
    r = _run(nc, [arrays], core_ids=[0])
    return r.results[0]["out"]
```

```python
from contextlib import ExitStack

import numpy as np

import concourse.bass as bass
from concourse import mybir
from concourse.bass import IndirectOffsetOnAxis, ds

ALU = mybir.AluOpType
ACT = mybir.ActivationFunctionType
AX = mybir.AxisListType
F32 = mybir.dt.float32
BF16 = mybir.dt.bfloat16
I32 = mybir.dt.int32
U32 = mybir.dt.uint32

P = 128
N, D, H = 1250, 512, 8
HD = D // H
NT, TR = 10, 125
KC = D // P
E = 40000
ER = E // TR
CHN = 2 * TR
NCH = N // CHN
BATCH = 5
GROUP = 512
Q = GROUP // P
BIG = 1e30
PAD_ROW = 999.0


def n_groups(edges):
    g = (edges + NT * (GROUP - 1)) // GROUP
    return g + g % 2


G0, G1 = n_groups(E + N), n_groups(E)
REC0, REC1 = 4, 26
F_RBF = 20


class Order:

    def __init__(self, eng, sem, base=0):
        self.eng, self.sem, self.base, self.n = eng, sem, base, 0

    def mark(self, ins):
        ins.then_inc(self.sem, 1)
        self.n += 1

    def settle(self):
        self.eng.wait_ge(self.sem, self.base + self.n)

    def link(self, ins):
        self.mark(ins)
        self.settle()


def wait_apart(eng, sem, value, passed):
    eng.wait_ge(sem, value)
    eng.sem_inc(passed, 1)


class Stage:
    used = set()

    def __init__(self, nc, name):
        self.nc, self.name, self.ctx = nc, name, ExitStack()

    def __enter__(self):
        return self

    def __exit__(self, *x):
        return self.ctx.__exit__(*x)

    def sb(self, name, shape, dt=F32):
        return self.ctx.enter_context(self.nc.sbuf_tensor(f"{self.name}_{name}", shape, dt))

    def ps(self, name, banks=1, dt=F32):
        n = banks * (512 if dt == F32 else 1024)
        return self.ctx.enter_context(self.nc.psum_tensor(f"{self.name}_{name}", [P, n], dt))

    def sem(self, name):
        sem = self.ctx.enter_context(self.nc.semaphore(f"{self.name}_{name}"))
        Stage.used.add(sem.num)
        return sem

    def pool_dma_sem(self, name):
        return self.nc.alloc_semaphore(f"{self.name}_{name}")

    def block(self):
        return self.nc.Block()


def at(i, c):
    return i * 2 + c, c % 2, i + c // 2


def clear_semaphores(nc):
    with nc.Block() as block:
        @block.gpsimd
        def _(pool):
            first = last = None
            for n in sorted(Stage.used) + [-1]:
                if last is not None and n != last + 1:
                    pool.sem_clear(range(first, last + 1))
                    first = None
                if first is None:
                    first = n
                last = n
    Stage.used.clear()


def mid(ap, axis, count):
    a = ap.unsqueeze(axis)
    shape = list(a.shape)
    shape[axis] = count
    return a.broadcast_to(shape)


def constants(nc, m, x):
    with Stage(nc, "const") as s:
        row_i = s.sb("row_i", [P, P], I32)
        col_i = s.sb("col_i", [P, 1], I32)
        iotas, order, loaded = s.sem("iotas"), s.sem("order"), s.sem("x_loaded")
        with s.block() as block:
            @block.sync
            def _(sp):
                sp.dma_start(m.X[:], x.rearrange("(t p) d -> p t d", p=TR)).then_inc(loaded, 16)
                sp.wait_ge(loaded, 16)

            @block.gpsimd
            def _(pool):
                nc.gpsimd.iota(row_i[:], [[1, P]], 0, 0).then_inc(iotas, 1)
                nc.gpsimd.iota(col_i[:], [[0, 1]], 0, 1).then_inc(iotas, 1)

            @block.vector
            def _(dve):
                o = Order(dve, order)
                o.mark(nc.vector.memset(m.ones[:], 1.0))
                dve.wait_ge(iotas, 2)
                o.mark(nc.vector.tensor_copy(m.iota_row[:], row_i[:]))
                o.link(nc.vector.tensor_copy(m.iota_col[:], col_i[:]))
                o.mark(nc.vector.tensor_scalar(m.ident[:], m.iota_row[:], m.iota_col[:, 0:1], None, ALU.is_equal))
                o.mark(nc.vector.tensor_scalar(m.ident_b[:], m.iota_row[:], m.iota_col[:, 0:1], None, ALU.is_equal))
                o.mark(nc.vector.tensor_scalar(m.above[:], m.iota_row[:], m.iota_col[:, 0:1], None, ALU.is_gt))


def sort_edges(nc, m, name, groups, rec, rec_dram, tile_row, load_list, n_loads, fill_rest, n_self):
    T = ER + n_self
    n_batches = T // BATCH
    positions = groups * GROUP
    W = BATCH * NT
    with Stage(nc, name) as s:
        key_i = s.sb("key_i", [TR, T], I32)
        other_i = s.sb("other_i", [TR, T], I32)
        recs = s.sb("recs", [TR, T, rec])
        key = s.sb("key", [TR, T])
        tile_of = s.sb("tile_of", [TR, T])
        row_of = s.sb("row_of", [TR, T])
        tile_hot = s.sb("tile_hot", [TR, T, NT], BF16)
        zeros = s.sb("zeros", [TR, P], BF16)
        row_hot = s.sb("row_hot", [TR, 2, BATCH, TR], BF16)
        row_hot_t = s.sb("row_hot_t", [TR, BATCH, TR], BF16)
        before = s.sb("before", [TR, BATCH, TR], BF16)
        hist = s.sb("hist", [TR, NT])
        sizes_i = s.sb("sizes_i", [TR, NT], I32)
        sizes = s.sb("sizes", [TR, NT])
        zrow = s.sb("zrow", [TR, NT])
        starts = s.sb("starts", [TR, NT])
        base = s.sb("base", [TR, NT])
        g_iota_i = s.sb("g_iota_i", [1, groups], I32)
        g_iota = s.sb("g_iota", [1, groups])
        g_tile = s.sb("g_tile", [1, groups])
        snap_i = s.sb("snap_i", [TR, BATCH + 1, NT], I32)
        low_i = s.sb("low_i", [TR, BATCH + 1, NT], I32)
        snap_hi = s.sb("snap_hi", [TR, BATCH + 1, NT], BF16)
        snap_lo = s.sb("snap_lo", [TR, BATCH + 1, NT], BF16)
        picked = s.sb("picked", [TR, BATCH, NT])
        place_f = s.sb("place_f", [TR, BATCH])
        place = s.sb("place", [TR, 2, BATCH], U32)
        staged = s.sb("staged", [TR, 2, BATCH, rec])
        pads = s.sb("pads", [P, 8, rec])
        rest = s.sb("rest", [TR, T * (REC1 - 2)]) if rec == REC1 else None
        hist_p = s.ps("hist_p")[0:TR, 0:NT]
        sums_p = s.ps("sums_p")[0:TR, 0:2 * NT].rearrange("p (k a) -> p k a", k=2)
        row_hot_p = s.ps("row_hot_p", 1, BF16)[0:TR, 0:BATCH * P].rearrange("p (j e) -> p j e", j=BATCH)
        same_p = s.ps("same_p", 2)[0:TR, :].rearrange("p (j e) -> p j e", e=P)
        snap_p = s.ps("snap_p")[0:TR, 0:(BATCH + 1) * NT].rearrange("p (j a) -> p j a", a=NT)
        rank_p = s.ps("rank_p")[0:TR, 0:BATCH * NT].rearrange("p (j a) -> p j a", a=NT)

        loaded, self_ids, padded = s.sem("loaded"), s.sem("self_ids"), s.sem("padded")
        pads_made = s.sem("pads_made")
        prep, hot_made, hist_added = s.sem("prep"), s.sem("hot_made"), s.sem("hist_added")
        hist_done, sums_done, fields = s.sem("hist_done"), s.sem("sums_done"), s.sem("fields")
        hot2_made, turned, turned_kept = s.sem("hot2_made"), s.sem("turned"), s.sem("turned_kept")
        snap_added, snap_split, same_done = s.sem("snap_added"), s.sem("snap_split"), s.sem("same_done")
        before_made, ranked, chain = s.sem("before_made"), s.sem("ranked"), s.sem("chain")
        placed, staged_full, hist_kept = s.sem("placed"), s.sem("staged_full"), s.sem("hist_kept")
        scattered = [s.pool_dma_sem(f"scattered{b}") for b in range(2)]
        past, act_past = s.sem("past"), s.sem("act_past")
        first_dram = nc.dram_tensor(f"{name}_first", [2, rec], F32).ap()

        with s.block() as block:
            @block.sync
            def _(sp):
                for dst, src in load_list(key_i, other_i, rest):
                    sp.dma_start(dst, src).then_inc(loaded, 16)
                sp.wait_ge(pads_made, 1)
                chunks = positions // (P * 8)
                for k in range(chunks):
                    sp.dma_start(rec_dram[k * P * 8:(k + 1) * P * 8, :].rearrange("(p j) w -> p j w", p=P),
                                 pads[:]).then_inc(padded, 16)
                left = positions - chunks * P * 8
                if left:
                    sp.dma_start(rec_dram[chunks * P * 8:positions, :].rearrange("(p j) w -> p j w", p=P),
                                 pads[:, 0:left // P, :]).then_inc(padded, 16)
                sp.wait_ge(loaded, 16 * n_loads)
                sp.wait_ge(padded, 16 * ((positions + P * 8 - 1) // (P * 8)))

            @block.gpsimd
            def _(pool):
                nc.gpsimd.iota(g_iota_i[:], [[1, groups]], 0, 0).then_inc(self_ids, 1)
                if n_self:
                    nc.gpsimd.iota(key_i[:, ER:T], [[TR, n_self]], 0, 1).then_inc(self_ids, 1)
                    nc.gpsimd.iota(other_i[:, ER:T], [[TR, n_self]], 0, 1).then_inc(self_ids, 1)
                chunks = (positions + P * 8 - 1) // (P * 8)
                pool.wait_ge(padded, 16 * chunks)
                for b in range(2):
                    nc.gpsimd.dma_start(first_dram[b:b + 1, :], pads[0:1, 0, :]).then_inc(scattered[b], 16)
                with pool.Fori(0, n_batches // 2) as i:
                    for b in range(2):
                        pool.wait_ge(placed, i * 2 + (b + 1))
                        wait_apart(pool, staged_full, i * 2 + (b + 1), past)
                        for j in range(BATCH):
                            nc.gpsimd.indirect_dma_start(
                                out=rec_dram[:, :], out_offset=IndirectOffsetOnAxis(ap=place[:, b, j:j + 1], axis=0),
                                in_=staged[:, b, j, :], in_offset=None).then_inc(scattered[b], 16)
                for b in range(2):
                    pool.wait_ge(scattered[b], 16 + 8 * T)

            @block.vector
            def _(dve):
                o = Order(dve, prep)
                o.mark(nc.vector.memset(zeros[:], 0.0))
                o.link(nc.vector.memset(pads[:], 0.0))
                if rec == REC1:
                    o.link(nc.vector.memset(pads[:, :, 2:5], 1.0))
                    nc.vector.memset(pads[:, :, 1:2], PAD_ROW).then_inc(pads_made, 1)
                else:
                    o.link(nc.vector.memset(recs[:], 0.0))
                    nc.vector.memset(pads[:, :, 1:3], PAD_ROW * TR).then_inc(pads_made, 1)
                o.mark(nc.vector.memset(zrow[:], 0.0))
                dve.wait_ge(loaded, 16 * n_loads)
                dve.wait_ge(self_ids, 3 if n_self else 1)
                o.mark(nc.vector.tensor_copy(g_iota[:], g_iota_i[:]))
                o.link(nc.vector.tensor_copy(key[:], key_i[:]))
                o.link(nc.vector.tensor_scalar(tile_of[:], key[:], float(TR), None, ALU.is_ge))
                for k in range(2, NT):
                    o.link(nc.vector.scalar_tensor_tensor(out=tile_of[:], in0=key[:], scalar=float(TR * k), in1=tile_of[:],
                                                          op0=ALU.is_ge, op1=ALU.add))
                o.link(nc.vector.scalar_tensor_tensor(out=row_of[:], in0=tile_of[:], scalar=-float(TR), in1=key[:],
                                                      op0=ALU.mult, op1=ALU.add))
                o.mark(nc.vector.tensor_tensor(tile_hot[:], mid(tile_of[:], 2, NT),
                                               mid(m.iota_row[0:TR, 0:NT], 1, T), ALU.is_equal))
                o.mark(nc.vector.tensor_copy(recs[:].bitcast(I32)[:, :, 0], other_i[:]))
                o.settle()
                o.link(nc.vector.tensor_copy(recs[:, :, 1], row_of[:]))
                fill_rest(key, rest, recs).then_inc(fields, 1)

                def hots(buf, t0):
                    return nc.vector.tensor_tensor(row_hot[:, buf], mid(m.iota_row[0:TR, 0:TR], 1, BATCH),
                                                   mid(row_of[:, ds(t0, BATCH)], 2, TR), ALU.is_equal)

                with dve.Fori(0, n_batches // 2) as i:
                    for b in range(2):
                        dve.wait_ge(hist_added, i * 2 + (b + 1))
                        hots(b, i * (2 * BATCH) + b * BATCH).then_inc(hot_made, 1)
                dve.wait_ge(hist_done, 1)
                nc.vector.tensor_copy(hist[:], hist_p).then_inc(hist_kept, 1)
                dve.wait_ge(sums_done, 1)
                o.link(nc.vector.tensor_scalar(sizes[:], sums_p[:, 1], float(GROUP - 1), None, ALU.add))
                o.link(nc.vector.tensor_copy(sizes_i[:], sizes[:]))
                o.link(nc.vector.tensor_scalar(sizes_i[:], sizes_i[:], 9, None, ALU.arith_shift_right))
                o.link(nc.vector.tensor_copy(sizes[:], sizes_i[:]))
                o.link(nc.vector.tensor_tensor_scan(starts[:], sizes[:], zrow[:], 0.0, ALU.add, ALU.add))
                o.link(nc.vector.tensor_tensor(starts[:], starts[:], sizes[:], ALU.subtract))
                o.link(nc.vector.scalar_tensor_tensor(out=base[:], in0=starts[:], scalar=float(GROUP), in1=sums_p[:, 0],
                                                      op0=ALU.mult, op1=ALU.add))
                o.link(nc.vector.tensor_scalar(g_tile[:], g_iota[:], starts[0:1, 1:2], None, ALU.is_ge))
                for k in range(2, NT):
                    o.link(nc.vector.scalar_tensor_tensor(out=g_tile[:], in0=g_iota[:], scalar=starts[0:1, k:k + 1],
                                                          in1=g_tile[:], op0=ALU.is_ge, op1=ALU.add))
                o.mark(nc.vector.tensor_copy(tile_row[0:1, 0:groups], g_tile[:]))
                o.link(nc.vector.tensor_copy(snap_i[:, BATCH], base[:]))
                o.link(nc.vector.tensor_scalar(low_i[:, BATCH], snap_i[:, BATCH], 255, None, ALU.bitwise_and))
                o.mark(nc.vector.tensor_copy(snap_lo[:, BATCH], low_i[:, BATCH]))
                o.settle()
                nc.vector.tensor_tensor(snap_hi[:, BATCH], snap_i[:, BATCH], low_i[:, BATCH],
                                        ALU.subtract).then_inc(snap_split, 1)

                with dve.Fori(0, n_batches // 2) as i:
                    for b in range(2):
                        n = i * 2 + b
                        c = Order(dve, chain, n * 5)
                        hots(b, i * (2 * BATCH) + b * BATCH).then_inc(hot2_made, 1)
                        dve.wait_ge(snap_added, n + 1)
                        c.link(nc.vector.tensor_copy(snap_i[:], snap_p))
                        c.link(nc.vector.tensor_scalar(low_i[:], snap_i[:], 255, None, ALU.bitwise_and))
                        c.link(nc.vector.tensor_copy(snap_lo[:], low_i[:]))
                        nc.vector.tensor_tensor(snap_hi[:], snap_i[:], low_i[:], ALU.subtract).then_inc(snap_split, 1)
                        dve.wait_ge(same_done, n + 1)
                        nc.vector.tensor_tensor(before[:], same_p[:, 0:BATCH, 0:TR], mid(m.above[0:TR, 0:TR], 1, BATCH),
                                                ALU.mult).then_inc(before_made, 1)
                        dve.wait_ge(ranked, n + 1)
                        c.link(nc.vector.tensor_tensor(picked[:], rank_p,
                                                       tile_hot[:, ds(i * (2 * BATCH) + b * BATCH, BATCH), :], ALU.mult))
                        c.link(nc.vector.tensor_reduce(place_f[:], picked[:], AX.X, ALU.add))
                        dve.wait_ge(scattered[b], i * (16 * BATCH) + 16)
                        nc.vector.tensor_copy(place[:, b], place_f[:]).then_inc(placed, 1)

            @block.scalar
            def _(act):
                act.wait_ge(fields, 1)
                with act.Fori(0, n_batches // 2) as i:
                    for b in range(2):
                        n = i * 2 + b
                        act.wait_ge(turned, n + 1)
                        nc.scalar.copy(row_hot_t[:], row_hot_p[:, :, 0:TR]).then_inc(turned_kept, 1)
                        wait_apart(act, scattered[b], i * (16 * BATCH) + 16, act_past)
                        nc.scalar.copy(staged[:, b], recs[:, ds(i * (2 * BATCH) + b * BATCH, BATCH), :]
                                       ).then_inc(staged_full, 1)

            @block.tensor
            def _(pe):
                pe.wait_ge(prep, 1)
                nc.tensor.matmul(hist_p, zeros[:, 0:TR], zeros[:, 0:NT], start=True, stop=False,
                                 skip_group_check=True).then_inc(hist_added, 2)
                with pe.Fori(0, n_batches // 2) as i:
                    for b in range(2):
                        pe.wait_ge(hot_made, i * 2 + (b + 1))
                        for j in range(BATCH):
                            last = nc.tensor.matmul(hist_p, row_hot[:, b, j],
                                                    tile_hot[:, i * (2 * BATCH) + (b * BATCH + j), :],
                                                    start=False, stop=False, skip_group_check=True)
                        last.then_inc(hist_added, 1)
                nc.tensor.matmul(hist_p, zeros[:, 0:TR], zeros[:, 0:NT], start=False, stop=True,
                                 skip_group_check=True).then_inc(hist_done, 1)
                pe.wait_ge(hist_kept, 1)
                nc.tensor.matmul(sums_p[:, 0], m.above[0:TR, 0:TR], hist[:], start=True, stop=True)
                nc.tensor.matmul(sums_p[:, 1], m.ones[0:TR, 0:TR], hist[:], start=True, stop=True).then_inc(sums_done, 1)
                with pe.Fori(0, n_batches // 2) as i:
                    for b in range(2):
                        n = i * 2 + b
                        col = [i * (2 * BATCH) + (b * BATCH + j) for j in range(BATCH)]
                        pe.wait_ge(hot2_made, n + 1)
                        for j in range(BATCH):
                            last = nc.tensor.transpose(row_hot_p[:, j, 0:TR], row_hot[:, b, j], m.ident_b[0:TR, 0:TR])
                        last.then_inc(turned, 1)
                        pe.wait_ge(snap_split, n + 1)
                        for j in range(BATCH + 1):
                            nc.tensor.matmul(snap_p[:, j], m.ident_b[0:TR, 0:TR], snap_hi[:, BATCH], start=(j == 0),
                                             stop=False, skip_group_check=True)
                            last = nc.tensor.matmul(snap_p[:, j], m.ident_b[0:TR, 0:TR], snap_lo[:, BATCH], start=False,
                                                    stop=(j == 0), skip_group_check=True)
                            for k in range(j):
                                last = nc.tensor.matmul(snap_p[:, j], row_hot[:, b, k], tile_hot[:, col[k], :],
                                                        start=False, stop=(k == j - 1), skip_group_check=True)
                        last.then_inc(snap_added, 1)
                        pe.wait_ge(turned_kept, n + 1)
                        for j in range(BATCH):
                            last = nc.tensor.matmul(same_p[:, j, 0:TR], row_hot_t[:, j], row_hot_t[:, j],
                                                    start=True, stop=True, skip_group_check=True)
                        last.then_inc(same_done, 1)
                        pe.wait_ge(snap_split, n + 2)
                        pe.wait_ge(before_made, n + 1)
                        for j in range(BATCH):
                            nc.tensor.matmul(rank_p[:, j], row_hot_t[:, j], snap_hi[:, j], start=(j == 0), stop=False,
                                             skip_group_check=True)
                            nc.tensor.matmul(rank_p[:, j], row_hot_t[:, j], snap_lo[:, j], start=False, stop=False,
                                             skip_group_check=True)
                            last = nc.tensor.matmul(rank_p[:, j], before[:, j], tile_hot[:, col[j], :], start=False,
                                                    stop=True, skip_group_check=True)
                        last.then_inc(ranked, 1)


def layer_norm(nc, m, name, src_cols):
    with Stage(nc, name) as s:
        stats = s.sb("stats", [TR, NT, 6])
        mv = s.sb("mv", [TR, NT, 2])
        rstd = s.sb("rstd", [TR, NT])
        turned_p = [s.ps(f"turned_p{b}") for b in range(2)]
        order, normed, turned, kept = s.sem("order"), s.sem("normed"), s.sem("turned"), s.sem("kept")
        var_made, std_made = s.sem("var_made"), s.sem("std_made")
        with s.block() as block:
            @block.vector
            def _(dve):
                o = Order(dve, order)
                for t in range(NT):
                    o.mark(nc.vector.bn_stats(stats[:, t], m.X[:, t]))
                o.settle()
                for t in range(NT):
                    o.mark(nc.vector.bn_aggr(mv[:, t], stats[:, t]))
                o.settle()
                nc.vector.tensor_scalar(rstd[:], mv[:, :, 1], 1e-5, None, ALU.add).then_inc(var_made, 1)
                dve.wait_ge(std_made, 1)
                o.link(nc.vector.reciprocal(rstd[:], rstd[:]))
                for t in range(NT):
                    nc.vector.tensor_scalar(m.XN[:, t], m.X[:, t], mv[:, t, 0:1], rstd[:, t:t + 1],
                                            ALU.subtract, ALU.mult).then_inc(normed, 1)

            @block.tensor
            def _(pe):
                for t in range(NT):
                    pe.wait_ge(normed, t + 1)
                    if t >= 2:
                        pe.wait_ge(kept, t - 1)
                    for c in range(KC):
                        last = nc.tensor.transpose(turned_p[t % 2][:, c * P:c * P + TR], m.XN[:, t, src_cols(c)],
                                                   m.ident[0:TR, 0:TR])
                    last.then_inc(turned, 1)

            @block.scalar
            def _(act):
                act.wait_ge(var_made, 1)
                nc.scalar.activation(rstd[:], rstd[:], ACT.Sqrt).then_inc(std_made, 1)
                for t in range(NT):
                    act.wait_ge(turned, t + 1)
                    nc.scalar.copy(m.XT[:, :, t * TR:(t + 1) * TR],
                                   turned_p[t % 2][:].rearrange("p (c n) -> p c n", c=KC)[:, :, 0:TR]).then_inc(kept, 1)


def plain(c):
    return slice(c * P, (c + 1) * P)


def by_component(c):
    return slice(0, P) if c == 0 else slice(P + c - 1, D, 3)


def chunk_rows(w, cols):
    return [w[cols(c), :] for c in range(KC)]


def attention(nc, m, name, wq, wk, wv, wo, bias=None, omegas=None):
    with Stage(nc, name) as s:
        Wq, Wk, Wv, Wo = (s.sb(n, [P, KC, D]) for n in ("Wq", "Wk", "Wv", "Wo"))
        bo = s.sb("bo", [1, D])
        QT = s.sb("QT", [P, KC, N])
        KV = s.sb("KV", [P, KC, P + 2])
        om = s.sb("om", [P, 2, P])
        pair = s.sb("pair", [P, 2])
        pair_rows = s.sb("pair_rows", [P, P])
        t1 = s.sb("t1", [P, 2, D])
        t2 = s.sb("t2", [P, 2, D])
        t3 = s.sb("t3", [P, 2, D])
        t4 = s.sb("t4", [P, 2, D])
        kt = s.sb("kt", [P, 2, KC, TR])
        kt2 = s.sb("kt2", [P, 2, KC, TR])
        kphi = s.sb("kphi", [TR, 2, D])
        vt = s.sb("vt", [TR, 2, KC, P + 1])
        den = s.sb("den", [TR, NT, H])
        att = s.sb("att", [TR, 2, D])
        att_t = s.sb("att_t", [P, 2, KC, TR])
        A = [s.ps(f"A{b}") for b in range(2)]
        B = [s.ps(f"B{b}") for b in range(2)]
        C = s.ps("C", 2)
        S = [s.ps(f"S{b}") for b in range(2)]
        loaded, ready = s.sem("loaded"), s.sem("ready")
        q_done, q_kept, f_done, f_kept = s.sem("q_done"), s.sem("q_kept"), s.sem("f_done"), s.sem("f_kept")
        q_exp, q_phi = s.sem("q_exp"), s.sem("q_phi")
        k_done, k_kept, kf_done, k_pre, k_exp, k_phi = (s.sem(n) for n in ("k_done", "k_kept", "kf_done", "k_pre", "k_exp", "k_phi"))
        v_done, v_kept, kv_added = s.sem("v_done"), s.sem("v_kept"), s.sem("kv_added")
        kv_ready, o_done, o_norm, o_turned, o_kept, y_done, y_added = (
            s.sem(n) for n in ("kv_ready", "o_done", "o_norm", "o_turned", "o_kept", "y_done", "y_added"))
        order, aorder = s.sem("order"), s.sem("aorder")
        loads = [(W[:, c], rows) for W, ws in ((Wq, wq), (Wk, wk), (Wv, wv), (Wo, wo)) for c, rows in enumerate(ws)]
        if bias is not None:
            loads.append((bo[:], bias))
        if omegas is not None:
            for k, w in enumerate(omegas):
                for h in range(2):
                    loads.append((om[h * HD:(h + 1) * HD, k, h * HD:(h + 1) * HD], w))
        n_loads = 16 * len(loads)
        n_q = NCH * 2
        L1 = omegas is not None

        with s.block() as block:
            @block.sync
            def _(sp):
                if L1:
                    sp.wait_ge(ready, 1)
                for dst, src in loads:
                    sp.dma_start(dst, src).then_inc(loaded, 16)
                sp.wait_ge(loaded, n_loads)

            @block.tensor
            def _(pe):
                pe.wait_ge(loaded, n_loads)
                pe.wait_ge(ready, 4)
                for n in range(n_q):
                    c, g = n // 2, n % 2
                    nodes = slice(c * CHN, (c + 1) * CHN)
                    if n >= 2:
                        pe.wait_ge(q_kept if L1 else q_phi, n - 1)
                    for j in range(2):
                        hp = 2 * g + j
                        for k in range(KC):
                            last = nc.tensor.matmul(A[n % 2][:, j * 256:j * 256 + CHN], Wq[:, k, hp * P:(hp + 1) * P],
                                                    m.XT[:, k, nodes], start=(k == 0), stop=(k == KC - 1))
                    last.then_inc(q_done, 1)
                    if L1:
                        pe.wait_ge(q_kept, n + 1)
                        if n >= 2:
                            pe.wait_ge(q_phi, n - 1)
                        q = t1[:, n % 2].rearrange("p (j n) -> p j n", j=2)
                        q2 = t2[:, n % 2].rearrange("p (j n) -> p j n", j=2)
                        for j in range(2):
                            nc.tensor.matmul(B[n % 2][:, j * 256:j * 256 + CHN], om[:, 0], q[:, j, 0:CHN],
                                             start=True, stop=True)
                            last = nc.tensor.matmul(S[n % 2][:, j * 256:j * 256 + CHN], pair_rows[:],
                                                    q2[:, j, 0:CHN], start=True, stop=True)
                        last.then_inc(f_done, 1)
                pe.wait_ge(q_phi, n_q)
                for t in range(NT):
                    rows = slice(t * TR, (t + 1) * TR)
                    if L1:
                        if t >= 2:
                            pe.wait_ge(k_kept, t - 1)
                        for j in range(KC):
                            for k in range(KC):
                                last = nc.tensor.matmul(A[t % 2][:, j * P:j * P + TR], Wk[:, k, j * P:(j + 1) * P],
                                                        m.XT[:, k, rows], start=(k == 0), stop=(k == KC - 1))
                        last.then_inc(k_done, 1)
                        pe.wait_ge(k_kept, t + 1)
                        if t >= 2:
                            pe.wait_ge(k_phi, t - 1)
                        for j in range(KC):
                            last = nc.tensor.matmul(S[t % 2][0:TR, j * P:(j + 1) * P], kt[:, t % 2, j], om[:, 1],
                                                    start=True, stop=True)
                        for j in range(KC):
                            last = nc.tensor.matmul(B[1][0:TR, 2 * j:2 * j + 2], kt2[:, t % 2, j], pair[:],
                                                    start=(j == 0), stop=(j == KC - 1), skip_group_check=True)
                        last.then_inc(kf_done, 1)
                    else:
                        if t >= 2:
                            pe.wait_ge(k_phi, t - 1)
                        for k in range(KC):
                            last = nc.tensor.matmul(S[t % 2][0:TR, :], m.XT[:, k, rows], Wk[:, k], start=(k == 0),
                                                    stop=(k == KC - 1))
                        last.then_inc(kf_done, 1)
                    if t >= 1:
                        pe.wait_ge(v_kept, t)
                    for k in range(KC):
                        last = nc.tensor.matmul(B[0][0:TR, :], m.XT[:, k, rows], Wv[:, k], start=(k == 0),
                                                stop=(k == KC - 1))
                    last.then_inc(v_done, 1)
                    pe.wait_ge(k_phi, t + 1)
                    pe.wait_ge(v_kept, t + 1)
                    for j in range(KC):
                        bank, off = j // 2, (j % 2) * (P + 1)
                        last = nc.tensor.matmul(C[:, bank * 512 + off:bank * 512 + off + P + 1], kphi[:, t % 2, j * P:(j + 1) * P],
                                                vt[:, t % 2, j], start=(t == 0 and j % 2 == 0), stop=(t == NT - 1),
                                                skip_group_check=True)
                    last.then_inc(kv_added, 1)
                pe.wait_ge(kv_ready, 1)
                for t in range(NT + 1):
                    if t < NT:
                        rows = slice(t * TR, (t + 1) * TR)
                        if t >= 1:
                            pe.wait_ge(o_norm, t)
                        for j in range(KC):
                            bank, off = j // 2, (j % 2) * (P + 2)
                            last = nc.tensor.matmul(C[0:TR, bank * 512 + off:bank * 512 + off + P + 2], QT[:, j, rows],
                                                    KV[:, j], start=True, stop=True, skip_group_check=True)
                        last.then_inc(o_done, 1)
                    if t >= 1:
                        u = t - 1
                        if u >= 2:
                            pe.wait_ge(o_kept, u - 1)
                        pe.wait_ge(o_norm, u + 1)
                        for j in range(KC):
                            last = nc.tensor.transpose(A[u % 2][:, j * P:j * P + TR], att[:, u % 2, j * P:(j + 1) * P],
                                                       m.ident[0:TR, 0:TR])
                        last.then_inc(o_turned, 1)
                        pe.wait_ge(o_kept, u + 1)
                        if u >= 2:
                            pe.wait_ge(y_added, u - 1)
                        for k in range(KC):
                            last = nc.tensor.matmul(B[u % 2][0:TR, :], att_t[:, u % 2, k], Wo[:, k], start=(k == 0),
                                                    stop=(k == KC - 1 and bias is None))
                        if bias is not None:
                            last = nc.tensor.matmul(B[u % 2][0:TR, :], m.ones[0:1, 0:TR], bo[:], start=False, stop=True)
                        last.then_inc(y_done, 1)

            @block.scalar
            def _(act):
                o = Order(act, aorder)
                for n in range(n_q):
                    c, g = n // 2, n % 2
                    nodes = slice(c * CHN, (c + 1) * CHN)
                    v = lambda x: x[:, n % 2].rearrange("p (j n) -> p j n", j=2)[:, :, 0:CHN]
                    w = lambda x: x[n % 2][:].rearrange("p (j n) -> p j n", j=2)[:, :, 0:CHN]
                    if L1:
                        act.wait_ge(q_done, n + 1)
                        if n >= 2:
                            act.wait_ge(q_phi, n - 1)
                        o.mark(nc.scalar.activation(v(t1), w(A), ACT.Copy, scale=HD ** -0.5))
                        o.settle()
                        nc.scalar.activation(v(t2), v(t1), ACT.Square).then_inc(q_kept, 1)
                        act.wait_ge(f_kept, n + 1)
                        nc.scalar.activation(v(t3), v(t3), ACT.Exp).then_inc(q_exp, 1)
                        nc.scalar.activation(v(t4), v(t4), ACT.Exp).then_inc(q_exp, 1)
                    else:
                        act.wait_ge(f_kept, n + 1)
                        nc.scalar.activation(v(t1), v(t1), ACT.Exp).then_inc(q_exp, 1)
                for t in range(NT):
                    if L1:
                        act.wait_ge(k_done, t + 1)
                        if t >= 2:
                            act.wait_ge(kf_done, t - 1)
                        x = A[t % 2][:].rearrange("p (j n) -> p j n", j=KC)[:, :, 0:TR]
                        o.mark(nc.scalar.activation(kt[:, t % 2], x, ACT.Copy, scale=HD ** -0.5))
                        o.settle()
                        nc.scalar.activation(kt2[:, t % 2], kt[:, t % 2], ACT.Square).then_inc(k_kept, 1)
                        act.wait_ge(k_pre, t + 1)
                        nc.scalar.activation(t3[0:TR, t % 2, 0:H], t3[0:TR, t % 2, 0:H], ACT.Exp).then_inc(k_exp, 1)
                        nc.scalar.activation(t1[0:TR, t % 2], t1[0:TR, t % 2], ACT.Exp).then_inc(k_exp, 1)
                    else:
                        act.wait_ge(k_pre, t + 1)
                        nc.scalar.activation(t1[0:TR, t % 2], t1[0:TR, t % 2], ACT.Exp).then_inc(k_exp, 1)
                    act.wait_ge(v_done, t + 1)
                    if t >= 2:
                        act.wait_ge(kv_added, t - 1)
                    nc.scalar.copy(vt[:, t % 2, :, 0:P], B[0][0:TR, :].rearrange("p (j n) -> p j n", j=KC)
                                   ).then_inc(v_kept, 1)
                for t in range(NT):
                    act.wait_ge(o_turned, t + 1)
                    if t >= 2:
                        act.wait_ge(y_done, t - 1)
                    nc.scalar.copy(att_t[:, t % 2], A[t % 2][:].rearrange("p (j n) -> p j n", j=KC)[:, :, 0:TR]
                                   ).then_inc(o_kept, 1)

            @block.vector
            def _(dve):
                o = Order(dve, order)
                nc.vector.memset(om[:], 0.0).then_inc(ready, 1)
                o.mark(nc.vector.memset(KV[:], 0.0))
                nc.vector.memset(vt[:], 1.0).then_inc(ready, 1)
                o.link(nc.vector.tensor_scalar(pair[:, 1:2], m.iota_col[:, 0:1], float(HD), None, ALU.is_ge))
                o.link(nc.vector.tensor_scalar(pair[:, 0:1], m.iota_col[:, 0:1], float(HD), None, ALU.is_lt))
                nc.vector.tensor_scalar(pair_rows[:, 0:HD], m.ones[:, 0:HD], pair[:, 0:1], None, ALU.mult).then_inc(ready, 1)
                nc.vector.tensor_scalar(pair_rows[:, HD:P], m.ones[:, 0:HD], pair[:, 1:2], None, ALU.mult).then_inc(ready, 1)
                for n in range(n_q):
                    c, g = n // 2, n % 2
                    nodes = slice(c * CHN, (c + 1) * CHN)
                    v = lambda x: x[:, n % 2].rearrange("p (j n) -> p j n", j=2)[:, :, 0:CHN]
                    w = lambda x: x[n % 2][:].rearrange("p (j n) -> p j n", j=2)[:, :, 0:CHN]
                    out = QT[:, 2 * g:2 * g + 2, nodes]
                    if L1:
                        dve.wait_ge(f_done, n + 1)
                        if n >= 2:
                            o.settle()
                        o.mark(nc.vector.tensor_scalar(v(t3), w(B), 50.0, None, ALU.min))
                        nc.vector.tensor_scalar(v(t4), w(S), 1e-16, -0.5, ALU.max, ALU.mult).then_inc(f_kept, 1)
                        dve.wait_ge(q_exp, 2 * n + 2)
                        nc.vector.scalar_tensor_tensor(out=out, in0=v(t4), scalar=1e-8, in1=v(t3), op0=ALU.max,
                                                       op1=ALU.mult).then_inc(q_phi, 1)
                    else:
                        dve.wait_ge(q_done, n + 1)
                        if n >= 2:
                            dve.wait_ge(q_phi, n - 1)
                        nc.vector.tensor_scalar(v(t1), w(A), 0.0, None, ALU.min).then_inc(f_kept, 1)
                        dve.wait_ge(q_exp, n + 1)
                        nc.vector.scalar_tensor_tensor(out=out, in0=w(A), scalar=0.0, in1=v(t1), op0=ALU.max,
                                                       op1=ALU.add).then_inc(q_phi, 1)
                dve.wait_ge(q_phi, n_q)
                for t in range(NT):
                    dve.wait_ge(kf_done, t + 1)
                    f, k = S[t % 2][0:TR, :], kphi[:, t % 2]
                    if t >= 2:
                        dve.wait_ge(k_phi, t - 1)
                        dve.wait_ge(kv_added, t - 1)
                    if L1:
                        o.mark(nc.vector.tensor_scalar(t1[0:TR, t % 2], f, 50.0, None, ALU.min))
                        nc.vector.tensor_scalar(t3[0:TR, t % 2, 0:H], B[1][0:TR, 0:H], 1e-16, -0.5, ALU.max,
                                                ALU.mult).then_inc(k_pre, 1)
                        dve.wait_ge(k_exp, 2 * t + 2)
                        o.link(nc.vector.tensor_scalar(t4[0:TR, t % 2, 0:H], t3[0:TR, t % 2, 0:H], 1e-8, None, ALU.max))
                        nc.vector.tensor_tensor(k.rearrange("p (h d) -> p h d", h=H),
                                                t1[0:TR, t % 2].rearrange("p (h d) -> p h d", h=H),
                                                mid(t4[0:TR, t % 2, 0:H], 2, HD), ALU.mult).then_inc(k_phi, 1)
                    else:
                        nc.vector.tensor_scalar(t1[0:TR, t % 2], f, 0.0, None, ALU.min).then_inc(k_pre, 1)
                        dve.wait_ge(k_exp, t + 1)
                        nc.vector.scalar_tensor_tensor(out=k, in0=f, scalar=0.0, in1=t1[0:TR, t % 2], op0=ALU.max,
                                                       op1=ALU.add).then_inc(k_phi, 1)
                dve.wait_ge(kv_added, NT)
                for j in range(KC):
                    off = (j // 2) * 512 + (j % 2) * (P + 1)
                    for h in range(2):
                        r = slice(h * HD, (h + 1) * HD)
                        o.mark(nc.vector.tensor_copy(KV[r, j, r], C[r, off + h * HD:off + (h + 1) * HD]))
                        last = nc.vector.tensor_copy(KV[r, j, P + h:P + h + 1], C[r, off + P:off + P + 1])
                        if j == KC - 1 and h == 1:
                            last.then_inc(kv_ready, 1)
                        else:
                            o.mark(last)
                o.settle()
                for t in range(NT):
                    dve.wait_ge(o_done, t + 1)
                    if t >= 2:
                        dve.wait_ge(o_turned, t - 1)
                    for b in range(2):
                        x = C[0:TR, b * 512:b * 512 + 2 * (P + 2)].rearrange("p (j n) -> p j n", j=2)
                        dn = den[:, t, 4 * b:4 * b + 4].rearrange("p (j h) -> p j h", j=2)
                        o.link(nc.vector.tensor_scalar(dn, x[:, :, P:P + 2], 0.0 if L1 else 1e-6, None, ALU.add))
                    o.link(nc.vector.reciprocal(den[:, t], den[:, t]))
                    for b in range(2):
                        x = C[0:TR, b * 512:b * 512 + 2 * (P + 2)].rearrange("p (j n) -> p j n", j=2)[:, :, 0:P]
                        for j in range(2):
                            hs = 4 * b + 2 * j
                            last = nc.vector.tensor_tensor(
                                att[:, t % 2, hs * HD:(hs + 2) * HD].rearrange("p (h d) -> p h d", h=2),
                                x[:, j].rearrange("p (h d) -> p h d", h=2), mid(den[:, t, hs:hs + 2], 2, HD), ALU.mult)
                            if b == 1 and j == 1:
                                last.then_inc(o_norm, 1)
                            else:
                                o.mark(last)
                    if t >= 1:
                        dve.wait_ge(y_done, t)
                        nc.vector.tensor_tensor(m.X[:, t - 1], m.X[:, t - 1], B[(t - 1) % 2][0:TR, :],
                                                ALU.add).then_inc(y_added, 1)
                dve.wait_ge(y_done, NT)
                nc.vector.tensor_tensor(m.X[:, NT - 1], m.X[:, NT - 1], B[(NT - 1) % 2][0:TR, :],
                                        ALU.add).then_inc(y_added, 1)


def node_table(nc, m, name, weights, blocks, scale, table, keep, att_w=None):
    with Stage(nc, name) as s:
        Ws = [s.sb(f"W{k}", [P, len(w), w[0].shape[1]]) for k, w in enumerate(weights)]
        W = D if att_w is None else D + H
        rows_sb = s.sb("rows", [TR, 2, W])
        att = s.sb("att", [TR, D])
        att_r = s.sb("att_r", [1, D])
        y = s.sb("y", [TR, D])
        kept_rows = s.sb("kept_rows", [TR, 2, W])
        rest = s.sb("rest", [TR, 2, W])
        att_p = s.ps("att_p")
        order, full, att_done = s.sem("order"), s.sem("full"), s.sem("att_done")
        out_p = [s.ps(f"out_p{b}") for b in range(2)]
        keep_p = [s.ps(f"keep_p{b}") for b in range(2)]
        loaded, done, copied, stored = s.sem("loaded"), s.sem("done"), s.sem("copied"), [s.sem(f"stored{b}") for b in range(2)]
        keep_done, kept = s.sem("keep_done"), s.sem("kept")
        loads = [(W_[:, c], rows) for W_, ws in zip(Ws, weights) for c, rows in enumerate(ws)]
        if att_w is not None:
            loads.append((att_r[:], att_w.rearrange("h c -> (h c)").unsqueeze(0)))
        with s.block() as block:
            @block.sync
            def _(sp):
                for dst, src in loads:
                    sp.dma_start(dst, src).then_inc(loaded, 16)
                for t in range(NT):
                    sp.wait_ge(copied if att_w is None else full, t + 1)
                    sp.dma_start(table[t * TR:(t + 1) * TR, :], rows_sb[:, t % 2]).then_inc(stored[t % 2], 16)
                for b in range(2):
                    sp.wait_ge(stored[b], 16 * NT // 2)

            @block.tensor
            def _(pe):
                pe.wait_ge(loaded, 16 * len(loads))
                if att_w is not None:
                    nc.tensor.matmul(att_p[0:TR, :], m.ones[0:1, 0:TR], att_r[:], start=True, stop=True).then_inc(att_done, 1)
                for t in range(NT):
                    rows = slice(t * TR, (t + 1) * TR)
                    if t >= 2:
                        pe.wait_ge(copied, t - 1)
                    for cols, pairs in blocks:
                        for i, (c, w, k) in enumerate(pairs):
                            last = nc.tensor.matmul(out_p[t % 2][0:TR, cols], m.XT[:, c, rows], Ws[w][:, k],
                                                    start=(i == 0), stop=(i == len(pairs) - 1), skip_group_check=True)
                    last.then_inc(done, 1)
                    if keep is not None:
                        if t >= 2:
                            pe.wait_ge(kept, t - 1)
                        for k in range(KC):
                            last = nc.tensor.matmul(keep_p[t % 2][0:TR, :], m.XT[:, k, rows], Ws[1][:, k],
                                                    start=(k == 0), stop=(k == KC - 1))
                        last.then_inc(keep_done, 1)

            @block.scalar
            def _(act):
                for t in range(NT):
                    act.wait_ge(done, t + 1)
                    if t >= 2:
                        act.wait_ge(stored[t % 2], 16 * (t // 2))
                    nc.scalar.activation(rows_sb[:, t % 2, 0:D], out_p[t % 2][0:TR, :], ACT.Copy, scale=scale).then_inc(copied, 1)

            @block.vector
            def _(dve):
                if keep is None:
                    return
                o = Order(dve, order)
                dve.wait_ge(att_done, 1)
                o.link(nc.vector.tensor_copy(att[:], att_p[0:TR, :]))
                heads = lambda x: x.rearrange("p (h d) -> p h d", h=H)
                for t in range(NT):
                    dve.wait_ge(copied, t + 1)
                    o.link(nc.vector.tensor_tensor(y[:], rows_sb[:, t % 2, 0:D], att[:], ALU.mult))
                    nc.vector.tensor_reduce(rows_sb[:, t % 2, D:W], heads(y[:]), AX.X, ALU.add).then_inc(full, 1)
                    dve.wait_ge(full, t + 1)
                    row = kept_rows[:, t % 2]
                    dve.wait_ge(keep_done, t + 1)
                    nc.vector.tensor_copy(row[:, 0:D], keep_p[t % 2][0:TR, :]).then_inc(kept, 1)
                    dve.wait_ge(kept, t + 1)
                    o.link(nc.vector.tensor_tensor(y[:], row[:, 0:D], att[:], ALU.mult))
                    o.link(nc.vector.tensor_reduce(row[:, D:W], heads(y[:]), AX.X, ALU.add))
                    o.link(nc.vector.tensor_copy(keep[:, t, 0], row))
                    o.link(nc.vector.tensor_tensor(rest[:, 0], row, keep[:, t, 0], ALU.subtract))
                    o.link(nc.vector.tensor_copy(keep[:, t, 1], rest[:, 0]))
                    o.link(nc.vector.tensor_tensor(rest[:, 1], rest[:, 0], keep[:, t, 1], ALU.subtract))
                    o.link(nc.vector.tensor_copy(keep[:, t, 2], rest[:, 1]))


def edge_scores(nc, m, XR, att_w, XL_dram, rec_dram, alpha_dram):
    W = D + H
    with Stage(nc, "scores") as s:
        recs = s.sb("recs", [P, G0 + 1, Q * REC0])
        alpha = s.sb("alpha", [P, G0, Q * H])
        att = s.sb("att", [P, D])
        att_r = s.sb("att_r", [1, D])
        idx = s.sb("idx", [P, 2, Q], U32)
        xl = s.sb("xl", [P, 2, Q, W])
        hot = s.sb("hot", [P, 2, Q, TR], BF16)
        hot_t = s.sb("hot_t", [TR, 2, Q, P], BF16)
        past = s.sem("past")
        z = s.sb("z", [P, 2, Q, D])
        linear = s.sb("linear", [P, 2, Q, H])
        turned_p = s.ps("turned_p", 1, BF16)
        z_p = s.ps("z_p", Q)
        lin_p = s.ps("lin_p")
        att_p = s.ps("att_p")
        loaded, att_done, att_kept = s.sem("loaded"), s.sem("att_done"), s.sem("att_kept")
        gathered = [s.pool_dma_sem(f"gathered{b}") for b in range(2)]
        idx_ready, hot_made, turned, kept = s.sem("idx_ready"), s.sem("hot_made"), s.sem("turned"), s.sem("kept")
        z_done, z_relu, chain = s.sem("z_done"), s.sem("z_relu"), s.sem("chain")
        stored = s.sem("stored")
        rows_used = [s.sem(f"rows_used{b}") for b in range(2)]
        with s.block() as block:
            @block.sync
            def _(sp):
                sp.dma_start(att_r[:], att_w.rearrange("h c -> (h c)").unsqueeze(0)).then_inc(loaded, 16)
                sp.dma_start(recs[:, 0:G0], rec_dram.rearrange("(g p q) w -> p g (q w)", p=P, q=Q)).then_inc(loaded, 16)
                sp.wait_ge(chain, 3 * G0)
                sp.dma_start(alpha_dram.rearrange("(g p q) h -> p g (q h)", p=P, q=Q), alpha[:]).then_inc(stored, 16)
                sp.wait_ge(stored, 16)

            @block.gpsimd
            def _(pool):
                pool.wait_ge(loaded, 32)
                with pool.Fori(0, G0 // 2) as i:
                    for b in range(2):
                        rows = recs[:, i * 2 + b, :].rearrange("p (q w) -> p q w", w=REC0)
                        pool.wait_ge(rows_used[b], i + 1)
                        nc.gpsimd.tensor_copy(idx[:, b], rows.bitcast(U32)[:, :, 0]).then_inc(idx_ready, 1)
                        wait_apart(pool, idx_ready, i * 2 + (b + 1), past)
                        for q in range(Q):
                            nc.gpsimd.indirect_dma_start(
                                out=xl[:, b, q, :], out_offset=None, in_=XL_dram[:, :],
                                in_offset=IndirectOffsetOnAxis(ap=idx[:, b, q:q + 1], axis=0)).then_inc(gathered[b], 16)

            @block.vector
            def _(dve):
                for b in range(2):
                    dve.sem_inc(rows_used[b], 1)
                nc.vector.memset(recs[:, G0], 0.0)
                dve.wait_ge(att_done, 1)
                nc.vector.tensor_copy(att[:], att_p[:]).then_inc(att_kept, 1)
                dve.wait_ge(att_kept, 1)
                dve.wait_ge(loaded, 32)

                def hots(i, c):
                    n, b, k = at(i, c)
                    rows = recs[:, n, :].rearrange("p (q w) -> p q w", w=REC0)
                    nc.vector.tensor_tensor(hot[:, b], mid(m.iota_row[:, 0:TR], 1, Q), mid(rows[:, :, 1], 2, TR),
                                            ALU.is_equal).then_inc(hot_made, 1)

                def add(i, c):
                    n, b, k = at(i, c)
                    dve.wait_ge(z_done, n + 1)
                    dve.wait_ge(gathered[b], k * (16 * Q) + 16 * Q)
                    nc.vector.tensor_tensor(linear[:, b], lin_p[:, 0:Q * H].rearrange("p (q h) -> p q h", q=Q),
                                            xl[:, b, :, D:W], ALU.add)
                    nc.vector.tensor_tensor(z[:, b], z_p[:].rearrange("p (q d) -> p q d", q=Q), xl[:, b, :, 0:D],
                                            ALU.add).then_inc(rows_used[b], 1)
                    dve.wait_ge(rows_used[b], k + 2)

                def score(i, c):
                    n, b, k = at(i, c)
                    o = Order(dve, chain, n * 3)
                    dve.wait_ge(z_relu, n + 1)
                    o.link(nc.vector.tensor_tensor(z[:, b], z[:, b], mid(att[:], 1, Q), ALU.mult))
                    o.link(nc.vector.tensor_reduce(alpha[:, n, :], z[:, b].rearrange("p q (h d) -> p (q h) d", h=H), AX.X,
                                                   ALU.add))
                    o.link(nc.vector.scalar_tensor_tensor(out=alpha[:, n, :], in0=linear[:, b].rearrange("p q h -> p (q h)"),
                                                          scalar=0.2, in1=alpha[:, n, :], op0=ALU.mult, op1=ALU.add))

                hots(0, 0)
                hots(0, 1)
                add(0, 0)
                hots(0, 2)
                add(0, 1)
                hots(0, 3)
                score(0, 0)
                with dve.Fori(1, G0 // 2 - 1) as i:
                    for c in range(2):
                        add(i, c)
                        hots(i, c + 2)
                        score(i, c - 1)
                add(0, G0 - 2)
                score(0, G0 - 3)
                add(0, G0 - 1)
                score(0, G0 - 2)
                score(0, G0 - 1)

            @block.scalar
            def _(act):
                def keep(i, c):
                    n, b, k = at(i, c)
                    act.wait_ge(turned, n + 1)
                    nc.scalar.copy(hot_t[:, b], turned_p[0:TR, 0:Q * P].rearrange("p (q e) -> p q e", q=Q)).then_inc(kept, 1)

                def relu(i, c):
                    n, b, k = at(i, c)
                    act.wait_ge(rows_used[b], k + 2)
                    nc.scalar.activation(z[:, b], z[:, b], ACT.Relu, scale=0.8).then_inc(z_relu, 1)

                keep(0, 0)
                keep(0, 1)
                with act.Fori(0, G0 // 2 - 1) as i:
                    for c in range(2):
                        relu(i, c)
                        keep(i, c + 2)
                relu(0, G0 - 2)
                relu(0, G0 - 1)

            @block.tensor
            def _(pe):
                pe.wait_ge(loaded, 32)
                nc.tensor.matmul(att_p[:], m.ones[0:1, :], att_r[:], start=True, stop=True).then_inc(att_done, 1)

                def turn(i, c, first=False):
                    n, b, k = at(i, c)
                    pe.wait_ge(hot_made, n + 1)
                    if not first:
                        pe.wait_ge(kept, n)
                    for q in range(Q):
                        last = nc.tensor.transpose(turned_p[0:TR, q * P:(q + 1) * P], hot[:, b, q], m.ident_b[:])
                    last.then_inc(turned, 1)

                def spread(i, c, first=False):
                    n, b, k = at(i, c)
                    tile = nc.tensor.value_load(m.tile0[0:1, ds(n, 1)], min_val=0, max_val=NT - 1)
                    pe.wait_ge(kept, n + 1)
                    if not first:
                        _, other, before = at(i, c - 1)
                        pe.wait_ge(rows_used[other], before + 2)
                    for q in range(Q):
                        for part in range(3):
                            nc.tensor.matmul(z_p[:, q * D:(q + 1) * D], hot_t[:, b, q], XR[:, tile, part, 0:D],
                                             start=(part == 0), stop=(part == 2))
                            last = nc.tensor.matmul(lin_p[:, q * H:(q + 1) * H], hot_t[:, b, q], XR[:, tile, part, D:W],
                                                    start=(part == 0 and q == 0), stop=(part == 2), skip_group_check=True)
                    last.then_inc(z_done, 1)

                turn(0, 0, first=True)
                turn(0, 1)
                spread(0, 0, first=True)
                spread(0, 1)
                with pe.Fori(1, G0 // 2) as i:
                    for c in range(2):
                        turn(i, c)
                        spread(i, c)


def edge_weights(nc, m, rec_dram, alpha_dram, weight_dram):
    L = G0 * GROUP // P
    with Stage(nc, "weights") as s:
        a = s.sb("a", [P, L, H])
        recs = s.sb("recs", [P, L, REC0])
        mx = s.sb("mx", [P, L, H])
        bw = s.sb("bw", [P, L])
        cut_f = s.sb("cut_f", [P, L])
        cut_b = s.sb("cut_b", [P, L])
        at_first = s.sb("at_first", [P, L])
        at_last = s.sb("at_last", [P, L])
        ends = s.sb("ends", [P, 4, H])
        rows = s.sb("rows", [H, 4, P])
        cut = s.sb("cut", [H, 4, P])
        run = s.sb("run", [H, 2, P])
        carry = s.sb("carry", [H, 2, P])
        carried = s.sb("carried", [P, 2, H])
        ends_p, back_p = s.ps("ends_p"), s.ps("back_p")
        loaded, order, ends_made, ends_turned = s.sem("loaded"), s.sem("order"), s.sem("ends_made"), s.sem("ends_turned")
        carry_made, carry_turned, shifted, expd, stored = (s.sem(n) for n in ("carry_made", "carry_turned", "shifted", "expd", "stored"))
        with s.block() as block:
            @block.sync
            def _(sp):
                sp.dma_start(a[:], alpha_dram.rearrange("(p l) h -> p l h", p=P)).then_inc(loaded, 16)
                sp.dma_start(recs[:], rec_dram.rearrange("(p l) w -> p l w", p=P)).then_inc(loaded, 16)
                sp.wait_ge(loaded, 32)
                sp.wait_ge(expd, 1)
                sp.dma_start(weight_dram.rearrange("(p l) h -> p l h", p=P), a[:]).then_inc(stored, 16)
                sp.wait_ge(stored, 16)

            @block.vector
            def _(dve):
                o = Order(dve, order)
                node = recs[:, :, 2]

                def penalty(out, x, y):
                    o.link(nc.vector.tensor_tensor(out, x, y, ALU.is_equal))
                    o.link(nc.vector.tensor_scalar(out, out, BIG, -BIG, ALU.mult, ALU.add))

                dve.wait_ge(loaded, 32)
                o.mark(nc.vector.memset(cut_f[:], -BIG))
                o.mark(nc.vector.memset(cut_b[:], -BIG))
                o.mark(nc.vector.memset(cut[:], -BIG))
                o.mark(nc.vector.memset(carry[:], -BIG))
                o.settle()
                penalty(cut_f[:, 1:L], node[:, 1:L], node[:, 0:L - 1])
                o.link(nc.vector.tensor_copy(cut_b[:, 0:L - 1], cut_f[:, 1:L]))
                for h in range(H):
                    o.mark(nc.vector.tensor_tensor_scan(mx[:, :, h], cut_f[:], a[:, :, h], -BIG, ALU.add, ALU.max))
                o.settle()
                o.mark(nc.vector.tensor_copy(ends[:, 0], mx[:, L - 1]))
                for h in range(H):
                    o.link(nc.vector.tensor_tensor_scan(bw[:, ::-1], cut_b[:, ::-1], a[:, ::-1, h], -BIG, ALU.add, ALU.max))
                    o.mark(nc.vector.tensor_copy(ends[:, 1, h:h + 1], bw[:, 0:1]))
                    o.link(nc.vector.tensor_tensor(mx[:, :, h], mx[:, :, h], bw[:], ALU.max))
                o.mark(nc.vector.tensor_copy(ends[:, 2], node[:, 0:1].broadcast_to([P, H])))
                o.mark(nc.vector.tensor_copy(ends[:, 3], node[:, L - 1:L].broadcast_to([P, H])))
                o.settle()
                nc.vector.memset(bw[:, 0:1], 0.0).then_inc(ends_made, 1)
                dve.wait_ge(ends_turned, 1)
                o.link(nc.vector.tensor_copy(rows[:], ends_p[0:H, :].rearrange("p (k n) -> p k n", k=4)))
                first, last_ = rows[:, 2], rows[:, 3]
                penalty(cut[:, 0, 1:P], first[:, 1:P], last_[:, 0:P - 1])
                o.link(nc.vector.tensor_copy(cut[:, 1, 0:P - 1], cut[:, 0, 1:P]))
                penalty(cut[:, 2], first, last_)
                o.link(nc.vector.tensor_tensor(cut[:, 3], cut[:, 2], cut[:, 1], ALU.min))
                o.link(nc.vector.tensor_tensor(cut[:, 2], cut[:, 2], cut[:, 0], ALU.min))
                o.mark(nc.vector.tensor_tensor_scan(run[:, 0], cut[:, 2], rows[:, 0], -BIG, ALU.add, ALU.max))
                o.link(nc.vector.tensor_tensor_scan(run[:, 1, ::-1], cut[:, 3, ::-1], rows[:, 1, ::-1], -BIG,
                                                    ALU.add, ALU.max))
                o.mark(nc.vector.tensor_tensor(carry[:, 0, 1:P], run[:, 0, 0:P - 1], cut[:, 0, 1:P], ALU.add))
                o.mark(nc.vector.tensor_tensor(carry[:, 1, 0:P - 1], run[:, 1, 1:P], cut[:, 1, 0:P - 1], ALU.add))
                o.settle()
                nc.vector.memset(run[:, 0, 0:1], 0.0).then_inc(carry_made, 1)
                dve.wait_ge(carry_turned, 1)
                o.link(nc.vector.tensor_copy(carried[:], back_p[:, 0:2 * H].rearrange("p (k h) -> p k h", k=2)))
                for out, j in ((at_first, 0), (at_last, L - 1)):
                    o.link(nc.vector.tensor_scalar(out[:], node, recs[:, j, 2:3], None, ALU.is_equal))
                    o.link(nc.vector.tensor_scalar(out[:], out[:], BIG, -BIG, ALU.mult, ALU.add))
                for k, pen in enumerate((at_first, at_last)):
                    for h in range(H):
                        o.mark(nc.vector.scalar_tensor_tensor(out=mx[:, :, h], in0=pen[:], scalar=carried[:, k, h:h + 1],
                                                              in1=mx[:, :, h], op0=ALU.add, op1=ALU.max))
                    o.settle()
                nc.vector.tensor_tensor(a[:], a[:], mx[:], ALU.subtract).then_inc(shifted, 1)

            @block.tensor
            def _(pe):
                pe.wait_ge(ends_made, 1)
                for k in range(4):
                    last = nc.tensor.transpose(ends_p[0:H, k * P:(k + 1) * P], ends[:, k], m.ident[:])
                last.then_inc(ends_turned, 1)
                pe.wait_ge(carry_made, 1)
                for k in range(2):
                    last = nc.tensor.transpose(back_p[:, k * H:(k + 1) * H], carry[:, k], m.ident[0:H, 0:H])
                last.then_inc(carry_turned, 1)

            @block.scalar
            def _(act):
                act.wait_ge(shifted, 1)
                nc.scalar.activation(a[:], a[:], ACT.Exp).then_inc(expd, 1)


def edge_sums(nc, m, bias, XL_dram, rec_dram, weight_dram):
    W = D + H
    with Stage(nc, "sums") as s:
        recs = s.sb("recs", [P, G0, Q * REC0])
        wts = s.sb("wts", [P, G0, Q * H])
        idx = s.sb("idx", [P, 2, Q], U32)
        xl = s.sb("xl", [P, 2, Q, W])
        msg = s.sb("msg", [P, 2, Q, W])
        hot = s.sb("hot", [P, 2, Q, TR])
        past = s.sem("past")
        acc = s.sb("acc", [TR, NT, W])
        bias_r = s.sb("bias_r", [1, D])
        g1 = s.sb("g1", [TR, 2, D])
        sum_p = [s.ps(f"sum_p{b}", 2) for b in range(2)]
        bias_p = s.ps("bias_p")
        loaded, acc_zero, bias_done = s.sem("loaded"), s.sem("acc_zero"), s.sem("bias_done")
        gathered = [s.pool_dma_sem(f"gathered{b}") for b in range(2)]
        idx_ready, summed, added = s.sem("idx_ready"), s.sem("summed"), s.sem("added")
        msg_made = [s.sem(f"msg_made{b}") for b in range(2)]
        order, pre, expd = s.sem("order"), s.sem("pre"), s.sem("expd")
        with s.block() as block:
            @block.sync
            def _(sp):
                sp.dma_start(bias_r[:], bias.unsqueeze(0)).then_inc(loaded, 16)
                sp.dma_start(recs[:], rec_dram.rearrange("(g p q) w -> p g (q w)", p=P, q=Q)).then_inc(loaded, 16)
                sp.dma_start(wts[:], weight_dram.rearrange("(g p q) h -> p g (q h)", p=P, q=Q)).then_inc(loaded, 16)
                sp.wait_ge(loaded, 48)

            @block.gpsimd
            def _(pool):
                pool.wait_ge(loaded, 48)
                with pool.Fori(0, G0 // 2) as i:
                    for b in range(2):
                        rows = recs[:, i * 2 + b, :].rearrange("p (q w) -> p q w", w=REC0)
                        pool.wait_ge(msg_made[b], i * 3 + 1)
                        nc.gpsimd.tensor_copy(idx[:, b], rows.bitcast(U32)[:, :, 0]).then_inc(idx_ready, 1)
                        wait_apart(pool, idx_ready, i * 2 + (b + 1), past)
                        for q in range(Q):
                            nc.gpsimd.indirect_dma_start(
                                out=xl[:, b, q, :], out_offset=None, in_=XL_dram[:, :],
                                in_offset=IndirectOffsetOnAxis(ap=idx[:, b, q:q + 1], axis=0)).then_inc(gathered[b], 16)

            @block.vector
            def _(dve):
                for b in range(2):
                    dve.sem_inc(msg_made[b], 1)
                nc.vector.memset(acc[:], 0.0).then_inc(acc_zero, 1)
                dve.wait_ge(acc_zero, 1)
                dve.wait_ge(loaded, 48)

                def messages(i, c):
                        n, b, k = at(i, c)
                        rows = recs[:, n, :].rearrange("p (q w) -> p q w", w=REC0)
                        w = wts[:, n, :]
                        nc.vector.tensor_tensor(hot[:, b], mid(m.iota_row[:, 0:TR], 1, Q), mid(rows[:, :, 1], 2, TR),
                                                ALU.is_equal).then_inc(msg_made[b], 1)
                        nc.vector.tensor_copy(msg[:, b, :, D:W], w.rearrange("p (q h) -> p q h", q=Q)).then_inc(msg_made[b], 1)
                        dve.wait_ge(gathered[b], k * (16 * Q) + 16 * Q)
                        nc.vector.tensor_tensor(
                            msg[:, b, :, 0:D].rearrange("p q (h d) -> p q h d", h=H),
                            xl[:, b, :, 0:D].rearrange("p q (h d) -> p q h d", h=H),
                            mid(w.rearrange("p (q h) -> p q h", q=Q), 3, HD), ALU.mult).then_inc(msg_made[b], 1)

                def add(i, c):
                        n, b, k = at(i, c)
                        tile = nc.vector.value_load(m.tile0[0:1, ds(n, 1)], min_val=0, max_val=NT - 1)
                        dve.wait_ge(summed, n + 1)
                        nc.vector.tensor_tensor(acc[:, tile, :], acc[:, tile, :], sum_p[b][0:TR, 0:W],
                                                ALU.add).then_inc(added, 1)
                        dve.wait_ge(added, n + 1)

                messages(0, 0)
                messages(0, 1)
                add(0, 0)
                with dve.Fori(1, G0 // 2) as i:
                    for c in range(2):
                        messages(i, c)
                        add(i, c - 1)
                add(0, G0 - 1)
                o = Order(dve, order)
                for t in range(NT):
                    den = acc[:, t, D:W]
                    o.mark(nc.vector.tensor_scalar(den, den, 1e-16, None, ALU.max))
                o.settle()
                o.link(nc.vector.reciprocal(acc[:, :, D:W], acc[:, :, D:W]))
                dve.wait_ge(bias_done, 1)
                for t in range(NT):
                    x = acc[:, t, 0:D]
                    o.link(nc.vector.tensor_tensor(x.rearrange("p (h d) -> p h d", h=H), x.rearrange("p (h d) -> p h d", h=H),
                                                   mid(acc[:, t, D:W], 2, HD), ALU.mult))
                    o.link(nc.vector.tensor_tensor(x, x, bias_p[0:TR, :], ALU.add))
                    if t >= 2:
                        o.settle()
                    nc.vector.tensor_scalar(g1[:, t % 2], x, 0.0, None, ALU.min).then_inc(pre, 1)
                    o.mark(nc.vector.tensor_scalar(x, x, 0.0, -1.0, ALU.max, ALU.add))
                    o.mark(nc.vector.tensor_tensor(m.X[:, t], m.X[:, t], m.XN[:, t], ALU.add))
                    o.settle()
                    dve.wait_ge(expd, t + 1)
                    o.link(nc.vector.tensor_tensor(x, x, g1[:, t % 2], ALU.add))
                    o.link(nc.vector.tensor_tensor(m.X[:, t], m.X[:, t], x, ALU.add))

            @block.scalar
            def _(act):
                for t in range(NT):
                    act.wait_ge(pre, t + 1)
                    nc.scalar.activation(g1[:, t % 2], g1[:, t % 2], ACT.Exp).then_inc(expd, 1)

            @block.tensor
            def _(pe):
                pe.wait_ge(loaded, 48)
                nc.tensor.matmul(bias_p[:], m.ones[0:1, :], bias_r[:], start=True, stop=True).then_inc(bias_done, 1)
                with pe.Fori(0, G0 // 2) as i:
                    for b in range(2):
                        n = i * 2 + b
                        pe.wait_ge(msg_made[b], i * 3 + 4)
                        for q in range(Q):
                            nc.tensor.matmul(sum_p[b][0:TR, 0:D], hot[:, b, q], msg[:, b, q, 0:D], start=(q == 0),
                                             stop=(q == Q - 1))
                            last = nc.tensor.matmul(sum_p[b][0:TR, D:W], hot[:, b, q], msg[:, b, q, D:W],
                                                    start=(q == 0), stop=(q == Q - 1))
                        last.then_inc(summed, 1)


def experts(nc, m, name, n_out, gated, w1s, w2, route, n_exp, b1=None, b2=None):
    F = w1s[0].shape[2]
    FC = F // P
    n1 = len(w1s)
    with Stage(nc, name) as s:
        W1 = [[s.sb(f"W1_{k}_{b}", [P, KC, F]) for k in range(n1)] for b in range(2)]
        W2 = [s.sb(f"W2_{b}", [P, FC, D]) for b in range(2)]
        b2_r = [s.sb(f"b2_{b}", [1, D]) for b in range(2)] if b2 is not None else None
        b1_c = s.sb("b1_c", [P, n_exp, FC]) if b1 is not None else None
        hid = s.sb("hid", [P, 2, FC, CHN])
        gate = s.sb("gate", [P, 2, CHN])
        Wr = s.sb("Wr", [P, KC, n_exp])
        r_rows = s.sb("r_rows", [n_exp, D]) if gated else None
        br = s.sb("br", [1, n_exp])
        wts = s.sb("wts", [TR, NT, n_exp])
        tmp = [s.sb(f"tmp{k}", [TR, NT, n_exp]) for k in range(3)]
        small = s.sb("small", [TR, 6, NT])
        cur = s.sb("cur", [TR, 2, NT])
        up_p = [[s.ps(f"up_p{k}_{b}") for b in range(2)] for k in range(n1)]
        y_p = [s.ps(f"y_p{b}") for b in range(2)]
        log_p = s.ps("log_p")
        r_loaded = s.sem("r_loaded")
        w_loaded = [s.sem(f"w_loaded{b}") for b in range(2)]
        r_turned, r_kept, logged, shifted, expd, routed = (s.sem(n) for n in ("r_turned", "r_kept", "logged", "shifted", "expd", "routed"))
        up_done, gate_made, hid_made, y_added, cur_made, order = (
            s.sem(n) for n in ("up_done", "gate_made", "hid_made", "y_added", "cur_made", "order"))
        y_done = [s.sem(f"y_done{b}") for b in range(2)]
        act_past = s.sem("act_past")
        b1_rows = s.sb("b1_rows", [n_exp * FC, P]) if b1 is not None else None
        n_up = NCH * FC
        per_load = 16 * (n1 + 1 + (b2 is not None))
        n_route = 16 * (route.n_loads + (b1 is not None))

        with s.block() as block:
            @block.sync
            def _(sp):
                route.load(sp, r_loaded, Wr, r_rows, br)
                if b1 is not None:
                    sp.dma_start(b1_rows[:], b1.rearrange("e (c p) -> (e c) p", p=P)).then_inc(r_loaded, 16)
                with sp.Fori(0, n_exp // 2) as i:
                    for b in range(2):
                        e = i * 2 + b
                        sp.wait_ge(y_done[b], i * NT + 1)
                        for k in range(n1):
                            sp.dma_start(W1[b][k][:], w1s[k][e].rearrange("(c p) f -> p c f", p=P)).then_inc(w_loaded[b], 16)
                        sp.dma_start(W2[b][:], w2[e].rearrange("(c p) f -> p c f", p=P)).then_inc(w_loaded[b], 16)
                        if b2 is not None:
                            sp.dma_start(b2_r[b][:], b2[e].unsqueeze(0)).then_inc(w_loaded[b], 16)
                sp.wait_ge(r_loaded, n_route)

            @block.tensor
            def _(pe):
                for b in range(2):
                    pe.sem_inc(y_done[b], 1)
                pe.wait_ge(r_loaded, n_route)
                if gated:
                    for c in range(KC):
                        last = nc.tensor.transpose(y_p[0][:, c * n_exp:(c + 1) * n_exp], r_rows[:, c * P:(c + 1) * P],
                                                   m.ident[0:n_exp, 0:n_exp])
                    last.then_inc(r_turned, 1)
                    pe.wait_ge(r_kept, 1)
                else:
                    nc.tensor.transpose(y_p[0][:, 0:n_exp * FC], b1_rows[:],
                                        m.ident[0:n_exp * FC, 0:n_exp * FC]).then_inc(r_turned, 1)
                for t in range(NT):
                    for k in range(KC):
                        last = nc.tensor.matmul(log_p[0:TR, t * n_exp:(t + 1) * n_exp], m.XT[:, k, t * TR:(t + 1) * TR],
                                                Wr[:, k], start=(k == 0), stop=(k == KC - 1 and gated), skip_group_check=True)
                    if not gated:
                        last = nc.tensor.matmul(log_p[0:TR, t * n_exp:(t + 1) * n_exp], m.ones[0:1, 0:TR], br[:],
                                                start=False, stop=True, skip_group_check=True)
                last.then_inc(logged, 1)
                with pe.Fori(0, n_exp // 2) as i:
                    for b in range(2):
                        e = i * 2 + b
                        pe.wait_ge(w_loaded[b], i * per_load + per_load)
                        for c in range(NCH):
                            for f in range(FC):
                                n = c * FC + f
                                pe.wait_ge(hid_made, e * n_up + (n + 1))
                                for w in range(n1):
                                    for k in range(KC):
                                        last = nc.tensor.matmul(up_p[w][n % 2][:, 0:CHN], W1[b][w][:, k, f * P:(f + 1) * P],
                                                                m.XT[:, k, c * CHN:(c + 1) * CHN], start=(k == 0),
                                                                stop=(k == KC - 1))
                                last.then_inc(up_done, 1)
                            pe.wait_ge(hid_made, e * n_up + ((c + 1) * FC + 2))
                            for r in range(2):
                                t = 2 * c + r
                                pe.wait_ge(y_added, e * NT + (t + 1))
                                for f in range(FC):
                                    last = nc.tensor.matmul(y_p[t % 2][0:TR, :], hid[:, c % 2, f, r * TR:(r + 1) * TR],
                                                            W2[b][:, f], start=(f == 0), stop=(f == FC - 1 and b2 is None))
                                if b2 is not None:
                                    last = nc.tensor.matmul(y_p[t % 2][0:TR, :], m.ones[0:1, 0:TR], b2_r[b][:],
                                                            start=False, stop=True)
                                last.then_inc(y_done[b], 1)

            @block.scalar
            def _(act):
                route.act(act, shifted, expd, tmp, small)
                if not gated:
                    act.sem_inc(hid_made, 2)
                    act.wait_ge(r_kept, 1)
                with act.Fori(0, n_exp // 2) as i:
                    for b in range(2):
                        e = i * 2 + b
                        for c in range(NCH):
                            for f in range(FC):
                                n = c * FC + f
                                if not gated:
                                    wait_apart(act, up_done, e * n_up + (n + 1), act_past)
                                else:
                                    act.wait_ge(up_done, e * n_up + (n + 1))
                                if gated:
                                    act.wait_ge(hid_made, e * n_up + (n + 1))
                                    nc.scalar.activation(gate[:, n % 2], up_p[0][n % 2][:, 0:CHN], ACT.Silu
                                                         ).then_inc(gate_made, 1)
                                else:
                                    nc.scalar.activation(hid[:, c % 2, f], up_p[0][n % 2][:, 0:CHN], ACT.Relu,
                                                         bias=b1_c[:, e, f:f + 1]
                                                         ).then_inc(hid_made, 1)

            @block.vector
            def _(dve):
                o = Order(dve, order)
                if gated:
                    dve.sem_inc(hid_made, 2)
                dve.wait_ge(r_turned, 1)
                if gated:
                    nc.vector.tensor_copy(Wr[:], y_p[0][:, 0:KC * n_exp].rearrange("p (c e) -> p c e", c=KC)).then_inc(r_kept, 1)
                else:
                    nc.vector.tensor_copy(b1_c[:], y_p[0][:, 0:n_exp * FC].rearrange("p (e c) -> p e c", c=FC)
                                          ).then_inc(r_kept, 1)
                    dve.wait_ge(r_kept, 1)
                dve.sem_inc(y_added, 2)
                dve.wait_ge(logged, 1)
                route.weigh(nc, dve, o, log_p[0:TR, 0:NT * n_exp].rearrange("p (t e) -> p t e", t=NT), wts, tmp, small,
                            shifted, expd)
                o.settle()
                with dve.Fori(0, n_exp // 2) as i:
                    for b in range(2):
                        e = i * 2 + b
                        nc.vector.tensor_copy(cur[:, b], wts[:, :, e]).then_inc(cur_made, 1)
                        dve.wait_ge(cur_made, e + 1)
                        for c in range(NCH):
                            if gated:
                                for f in range(FC):
                                    n = c * FC + f
                                    dve.wait_ge(gate_made, e * n_up + (n + 1))
                                    nc.vector.tensor_tensor(hid[:, c % 2, f], gate[:, n % 2], up_p[1][n % 2][:, 0:CHN],
                                                            ALU.mult).then_inc(hid_made, 1)
                            for r in range(2):
                                t = 2 * c + r
                                dve.wait_ge(y_done[b], i * NT + (t + 2))
                                nc.vector.scalar_tensor_tensor(out=m.X[:, t], in0=y_p[t % 2][0:TR, :],
                                                               scalar=cur[:, b, t:t + 1], in1=m.X[:, t], op0=ALU.mult,
                                                               op1=ALU.add).then_inc(y_added, 1)


def first_of(nc, o, hit, out, taken):
    o.link(nc.vector.tensor_copy(out[:, :, 0], hit[:, :, 0]))
    o.link(nc.vector.tensor_copy(taken, hit[:, :, 0]))
    for e in range(1, out.shape[2]):
        o.link(nc.vector.tensor_tensor(out[:, :, e], hit[:, :, e], taken, ALU.is_gt))
        o.link(nc.vector.tensor_tensor(taken, taken, hit[:, :, e], ALU.max))


class Top1:
    n_loads = 2

    def __init__(self, Wr, br):
        self.Wr, self.br = Wr, br

    def load(self, sp, sem, Wr, r_rows, br):
        sp.dma_start(Wr[:], self.Wr.rearrange("(c p) e -> p c e", p=P)).then_inc(sem, 16)
        sp.dma_start(br[:], self.br.unsqueeze(0)).then_inc(sem, 16)

    def act(self, act, shifted, expd, tmp, small):
        act.wait_ge(shifted, 1)
        act.activation(tmp[1][:], tmp[0][:], ACT.Exp).then_inc(expd, 1)

    def weigh(self, nc, dve, o, logits, wts, tmp, small, shifted, expd):
        n = logits.shape[2]
        o.link(nc.vector.tensor_reduce(small[:, 0], logits, AX.X, ALU.max))
        nc.vector.tensor_tensor(tmp[0][:], logits, mid(small[:, 0], 2, n), ALU.subtract).then_inc(shifted, 1)
        dve.wait_ge(expd, 1)
        o.mark(nc.vector.tensor_reduce(small[:, 1], tmp[1][:], AX.X, ALU.add))
        o.link(nc.vector.tensor_reduce(small[:, 2], tmp[1][:], AX.X, ALU.max))
        o.mark(nc.vector.tensor_tensor(tmp[0][:], tmp[1][:], mid(small[:, 2], 2, n), ALU.is_ge))
        o.mark(nc.vector.reciprocal(small[:, 1], small[:, 1]))
        o.settle()
        o.link(nc.vector.tensor_tensor(small[:, 3], small[:, 1], small[:, 2], ALU.mult))
        first_of(nc, o, tmp[0], tmp[2], small[:, 4])
        o.link(nc.vector.tensor_tensor(wts[:], tmp[2][:], mid(small[:, 3], 2, n), ALU.mult))


class Top2:
    n_loads = 1

    def __init__(self, router):
        self.router = router

    def load(self, sp, sem, Wr, r_rows, br):
        sp.dma_start(r_rows[:], self.router).then_inc(sem, 16)

    def act(self, act, shifted, expd, tmp, small):
        act.wait_ge(shifted, 1)
        act.activation(small[:, 2], small[:, 2], ACT.Exp).then_inc(expd, 1)

    def weigh(self, nc, dve, o, logits, wts, tmp, small, shifted, expd):
        n = logits.shape[2]
        o.link(nc.vector.tensor_reduce(small[:, 0], logits, AX.X, ALU.max))
        o.link(nc.vector.tensor_tensor(tmp[0][:], logits, mid(small[:, 0], 2, n), ALU.is_ge))
        first_of(nc, o, tmp[0], tmp[1], small[:, 4])
        o.link(nc.vector.scalar_tensor_tensor(out=tmp[2][:], in0=tmp[1][:], scalar=-BIG, in1=logits, op0=ALU.mult,
                                              op1=ALU.add))
        o.link(nc.vector.tensor_reduce(small[:, 1], tmp[2][:], AX.X, ALU.max))
        o.link(nc.vector.tensor_tensor(tmp[0][:], tmp[2][:], mid(small[:, 1], 2, n), ALU.is_ge))
        first_of(nc, o, tmp[0], tmp[2], small[:, 4])
        nc.vector.tensor_tensor(small[:, 2], small[:, 1], small[:, 0], ALU.subtract).then_inc(shifted, 1)
        dve.wait_ge(expd, 1)
        o.link(nc.vector.tensor_scalar(small[:, 3], small[:, 2], 1.0, None, ALU.add))
        o.link(nc.vector.reciprocal(small[:, 3], small[:, 3]))
        o.link(nc.vector.tensor_tensor(small[:, 2], small[:, 2], small[:, 3], ALU.mult))
        o.link(nc.vector.tensor_tensor(tmp[1][:], tmp[1][:], mid(small[:, 3], 2, n), ALU.mult))
        o.link(nc.vector.tensor_tensor(tmp[2][:], tmp[2][:], mid(small[:, 2], 2, n), ALU.mult))
        o.link(nc.vector.tensor_tensor(wts[:], tmp[1][:], tmp[2][:], ALU.add))


F1 = 128
Y0 = float(1.0 / np.sqrt(4.0 * np.pi))
Y1 = float(np.sqrt(3.0 / (4.0 * np.pi)))
MW = 9 * F1


def convolution(nc, m, Wf1, bf1, Wf2, bf2, W1_s, W1_v, W2_s, W2_v, table, rec_dram):
    with Stage(nc, "conv") as s:
        agg = [m.XN[:], m.XT_all[0:TR, :].rearrange("p (t d) -> p t d", t=NT)]
        conv_edges(nc, m, agg, Wf1, bf1, Wf2, bf2, table, rec_dram)
        conv_nodes(nc, m, agg, W1_s, W1_v, W2_s, W2_v)


def conv_edges(nc, m, agg, Wf1, bf1, Wf2, bf2, table, rec_dram):
    with Stage(nc, "edges") as s:
        recs = s.sb("recs", [P, G1, Q * REC1])
        wf1 = s.sb("wf1", [F_RBF, F1])
        wf2_in = s.sb("wf2_in", [P, 4 * F1])
        wf2 = s.sb("wf2", [P, 4, F1])
        bf1_c = s.sb("bf1_c", [P, 1])
        bf2_in = s.sb("bf2_in", [3, 4 * F1])
        bf2_r = s.sb("bf2_r", [3, 4 * F1])
        bf2_k = [s.sb(f"bf2_k{k}", [3, 4 * F1], BF16) for k in range(3)]
        bf2_s = s.sb("bf2_s", [3, 4 * F1], BF16)
        ones_b = s.sb("ones_b", [3, P], BF16)
        part = s.sb("part", [3, 3])
        norm = s.sb("norm", [P, G1 * Q])
        idx = s.sb("idx", [P, 2, Q], U32)
        rows_g = s.sb("rows_g", [P, 2, Q, D])
        hot = s.sb("hot", [P, 2, Q, TR])
        past = s.sem("past")
        fs = s.sb("fs", [P, Q, F_RBF])
        ft = s.sb("ft", [F_RBF, Q * P])
        ab = s.sb("ab", [P, Q * P])
        hx = s.sb("hx", [P, Q * P])
        half = s.sb("half", [P, 1])
        ht = s.sb("ht", [P, Q * P])
        msg = s.sb("msg", [P, 2, Q, MW])
        dot = s.sb("dot", [P, Q, F1])
        vy = s.sb("vy", [P, Q, 3, F1])
        f_p = s.ps("f_p")
        h_p = s.ps("h_p")
        w_p = s.ps("w_p", 4)
        sum_p = s.ps("sum_p", 2)
        names = ("loaded", "prep", "sq_made", "norm_made", "idx_ready", "hot_made", "f_staged", "f_turned", "f_kept",
                 "h_done", "h_ln", "h_made", "w_done", "c_made", "b_made", "vector_made", "msg_made", "summed",
                 "added", "chain", "rows_used0", "rows_used1", "aorder")
        S = {n: s.sem(n) for n in names}
        root_made, act_past = s.sem("root_made"), s.sem("act_past")
        (loaded, prep, sq_made, norm_made, idx_ready, hot_made, f_staged, f_turned, f_kept, h_done, h_ln,
         h_made, w_done, c_made, b_made, vector_made, msg_made, summed, added, chain, used0, used1, aorder) = (S[n] for n in names)
        rows_used = [used0, used1]
        gathered = [s.pool_dma_sem(f"gathered{b}") for b in range(2)]
        rec4 = recs[:].rearrange("p g (q w) -> p g q w", q=Q)
        recf = recs[:].rearrange("p g (q w) -> p (g q) w", q=Q)
        n_loads = 4 + 3

        with s.block() as block:
            @block.sync
            def _(sp):
                sp.dma_start(recs[:], rec_dram.rearrange("(g p q) w -> p g (q w)", p=P, q=Q)).then_inc(loaded, 16)
                sp.dma_start(wf1[:], Wf1).then_inc(loaded, 16)
                sp.dma_start(wf2_in[:], Wf2[:, 0:4 * F1]).then_inc(loaded, 16)
                sp.dma_start(bf1_c[:], bf1.rearrange("(p o) -> p o", o=1)).then_inc(loaded, 16)
                for k in range(3):
                    sp.dma_start(bf2_in[k:k + 1, :], bf2[0:4 * F1].unsqueeze(0)).then_inc(loaded, 16)
                sp.wait_ge(loaded, 16 * n_loads)

            @block.gpsimd
            def _(pool):
                pool.wait_ge(loaded, 16 * n_loads)
                with pool.Fori(0, G1 // 2) as i:
                    for b in range(2):
                        rows = recs[:, i * 2 + b, :].rearrange("p (q w) -> p q w", q=Q)
                        pool.wait_ge(rows_used[b], i + 1)
                        nc.gpsimd.tensor_copy(idx[:, b], rows.bitcast(U32)[:, :, 0]).then_inc(idx_ready, 1)
                        wait_apart(pool, idx_ready, i * 2 + (b + 1), past)
                        for q in range(Q):
                            nc.gpsimd.indirect_dma_start(
                                out=rows_g[:, b, q, :], out_offset=None, in_=table[:, :],
                                in_offset=IndirectOffsetOnAxis(ap=idx[:, b, q:q + 1], axis=0)).then_inc(gathered[b], 16)

            @block.vector
            def _(dve):
                o = Order(dve, prep)
                for b in range(2):
                    dve.sem_inc(rows_used[b], 1)
                for part_ in agg:
                    o.mark(nc.vector.memset(part_, 0.0))
                o.mark(nc.vector.memset(ones_b[:], 1.0))
                o.mark(nc.vector.memset(half[:], 0.5))
                for k in range(3):
                    o.mark(nc.vector.tensor_scalar(part[:, k:k + 1], m.iota_col[0:3, 0:1], float(k), None, ALU.is_equal))
                dve.wait_ge(loaded, 16 * n_loads)
                for slot, off in ((0, 2 * F1), (1, 0), (2, 1), (3, 2 * F1 + 1)):
                    pick = slice(off, off - off % 2 + 2 * F1, 2)
                    o.mark(nc.vector.tensor_copy(wf2[:, slot], wf2_in[:, pick]))
                    o.mark(nc.vector.tensor_copy(bf2_r[:, slot * F1:(slot + 1) * F1], bf2_in[:, pick]))
                o.settle()
                for k in range(3):
                    o.link(nc.vector.tensor_copy(bf2_k[k][:], bf2_r[:]))
                    if k < 2:
                        o.link(nc.vector.tensor_tensor(bf2_r[:], bf2_r[:], bf2_k[k][:], ALU.subtract))
                o.link(nc.vector.tensor_scalar(bf2_s[:], bf2_k[0][:], part[:, 0:1], None, ALU.mult))
                for k in (1, 2):
                    o.link(nc.vector.scalar_tensor_tensor(out=bf2_s[:], in0=bf2_k[k][:], scalar=part[:, k:k + 1],
                                                          in1=bf2_s[:], op0=ALU.mult, op1=ALU.add))
                sq = vy[:].rearrange("p q i f -> p (q i f)")[:, 0:G1 * Q]
                o.link(nc.vector.tensor_tensor(norm[:], recf[:, :, 2], recf[:, :, 2], ALU.mult))
                for k in (3, 4):
                    o.link(nc.vector.tensor_tensor(sq, recf[:, :, k], recf[:, :, k], ALU.mult))
                    o.link(nc.vector.tensor_tensor(norm[:], norm[:], sq, ALU.add))
                nc.vector.memset(dot[:, 0, 0:1], 0.0).then_inc(sq_made, 1)
                dve.wait_ge(root_made, 1)
                o.link(nc.vector.reciprocal(norm[:], norm[:]))
                o.link(nc.vector.tensor_scalar(norm[:], norm[:], Y1, None, ALU.mult))
                nc.vector.tensor_tensor(recf[:, :, 2:5], recf[:, :, 2:5], mid(norm[:], 2, 3), ALU.mult).then_inc(norm_made, 1)
                dve.wait_ge(norm_made, 1)

                def softplus(i, c):
                    n, b, k = at(i, c)
                    dve.wait_ge(h_ln, n + 1)
                    nc.vector.scalar_tensor_tensor(out=ht[:], in0=hx[:], scalar=0.0, in1=ab[:], op0=ALU.max,
                                                   op1=ALU.add).then_inc(h_made, 1)

                def prepare(i, c):
                    n, b, k = at(i, c)
                    o = Order(dve, chain, n * 3)
                    rec = recs[:, n, :].rearrange("p (q w) -> p q w", q=Q)
                    for q in range(Q):
                        last = nc.vector.tensor_scalar(hot[:, b, q], m.iota_row[:, 0:TR], rec[:, q, 1:2], rec[:, q, 5:6],
                                                       ALU.is_equal, ALU.mult)
                    last.then_inc(hot_made, 1)
                    dve.wait_ge(gathered[b], k * (16 * Q) + 16 * Q)
                    v = rows_g[:, b, :, F1:D].rearrange("p q (i f) -> p q i f", i=3)
                    o.link(nc.vector.tensor_tensor(vy[:], v, mid(rec[:, :, 2:5], 3, F1), ALU.mult))
                    o.link(nc.vector.tensor_tensor(dot[:], vy[:, :, 0], vy[:, :, 1], ALU.add))
                    o.link(nc.vector.tensor_tensor(dot[:], dot[:], vy[:, :, 2], ALU.add))

                def messages(i, c):
                    n, b, k = at(i, c)
                    v = rows_g[:, b, :, F1:D].rearrange("p q (i f) -> p q i f", i=3)
                    wp = w_p[:].rearrange("p (q k f) -> p q k f", q=Q, k=4)
                    dve.wait_ge(w_done, n + 1)
                    nc.vector.tensor_tensor(msg[:, b, :, 0:2 * F1].rearrange("p q (k f) -> p q k f", k=2),
                                            mid(rows_g[:, b, :, 0:F1], 2, 2), wp[:, :, 0:2], ALU.mult).then_inc(c_made, 1)
                    nc.vector.tensor_tensor(msg[:, b, :, 2 * F1:3 * F1], dot[:], wp[:, :, 2], ALU.mult).then_inc(b_made, 1)
                    nc.vector.tensor_tensor(msg[:, b, :, 6 * F1:9 * F1].rearrange("p q (i f) -> p q i f", i=3), v,
                                            mid(wp[:, :, 3], 2, 3), ALU.mult).then_inc(rows_used[b], 1)

                def add(i, c):
                    n, b, k = at(i, c)
                    tile = nc.vector.value_load(m.tile1[0:1, ds(n, 1)], min_val=0, max_val=NT - 1)
                    dve.wait_ge(summed, n + 1)
                    for k, part in enumerate(agg):
                        nc.vector.tensor_tensor(part[:, tile, :], part[:, tile, :], sum_p[0:TR, k * 512:(k + 1) * 512],
                                                ALU.add).then_inc(added, 1)
                    dve.wait_ge(added, n * 2 + 2)

                def step(i, c, add_last=True, next1=True, next2=True):
                    if add_last:
                        add(i, c - 1)
                    if next1:
                        prepare(i, c + 1)
                        messages(i, c + 1)
                    if next2:
                        softplus(i, c + 2)

                softplus(0, 0)
                step(0, -1, add_last=False)
                step(0, 0, add_last=False)
                step(0, 1)
                with dve.Fori(1, G1 // 2 - 1) as i:
                    step(i, 0)
                    step(i, 1)
                step(0, G1 - 2, next2=False)
                step(0, G1 - 1, next1=False, next2=False)
                add(0, G1 - 1)

            @block.scalar
            def _(act):
                act.wait_ge(sq_made, 1)
                nc.scalar.activation(norm[:], norm[:], ACT.Sqrt).then_inc(root_made, 1)
                act.wait_ge(norm_made, 1)
                nc.scalar.preload_act_table_set("natural_log_exp_and_others")

                def stage(i, c):
                    n, b, k = at(i, c)
                    rec = recs[:, n, :].rearrange("p (q w) -> p q w", q=Q)
                    nc.scalar.copy(fs[:], rec[:, :, 6:6 + F_RBF]).then_inc(f_staged, 1)

                def keep(i, c):
                    n, b, k = at(i, c)
                    act.wait_ge(f_turned, n + 1)
                    nc.scalar.copy(ft[:], f_p[0:F_RBF, :]).then_inc(f_kept, 1)

                def hidden(i, c):
                    n, b, k = at(i, c)
                    act.wait_ge(h_done, n + 1)
                    a = Order(act, aorder, n * 3)
                    a.link(nc.scalar.activation(hx[:], h_p[:], ACT.Identity, bias=bf1_c[:, 0:1]))
                    a.link(nc.scalar.activation(ab[:], hx[:], ACT.Abs))
                    a.link(nc.scalar.activation(ab[:], ab[:], ACT.Exp, scale=-1.0))
                    nc.scalar.activation(ab[:], ab[:], ACT.Ln, bias=half[:, 0:1], scale=0.5).then_inc(h_ln, 1)

                def vectors(i, c):
                    n, b, k = at(i, c)
                    rec = recs[:, n, :].rearrange("p (q w) -> p q w", q=Q)
                    wait_apart(act, c_made, n + 1, act_past)
                    for q in range(Q):
                        for k in range(3):
                            last = nc.scalar.activation(msg[:, b, q, (3 + k) * F1:(4 + k) * F1], msg[:, b, q, 0:F1],
                                                        ACT.Copy, scale=rec[:, q, 2 + k:3 + k])
                    last.then_inc(vector_made, 1)

                def step(i, c, next1=True, next2=True, next3=True):
                    if next2:
                        keep(i, c + 2)
                    if next2:
                        hidden(i, c + 2)
                    if next1:
                        vectors(i, c + 1)
                    if next3:
                        stage(i, c + 3)

                stage(0, 0)
                keep(0, 0)
                hidden(0, 0)
                stage(0, 1)
                step(0, -1, next1=True)
                step(0, 0)
                step(0, 1)
                with act.Fori(1, G1 // 2 - 2) as i:
                    step(i, 0)
                    step(i, 1)
                step(0, G1 - 4)
                step(0, G1 - 3, next3=False)
                step(0, G1 - 2, next2=False, next3=False)

            @block.tensor
            def _(pe):
                pe.wait_ge(norm_made, 1)

                def turn(i, c):
                    n, b, k = at(i, c)
                    pe.wait_ge(f_staged, n + 1)
                    for q in range(Q):
                        last = nc.tensor.transpose(f_p[0:F_RBF, q * P:(q + 1) * P], fs[:, q], m.ident[:])
                    last.then_inc(f_turned, 1)

                def hidden(i, c):
                    n, b, k = at(i, c)
                    pe.wait_ge(f_kept, n + 1)
                    nc.tensor.matmul(h_p[:], wf1[:], ft[:], start=True, stop=True).then_inc(h_done, 1)

                def filters(i, c, used=True):
                    n, b, k = at(i, c)
                    pe.wait_ge(h_made, n + 1)
                    if used:
                        pe.wait_ge(rows_used[(c - 1) % 2], at(i, c - 1)[2] + 2)
                    for q in range(Q):
                        nc.tensor.matmul(w_p[:, q * 512:(q + 1) * 512], ht[:, q * P:(q + 1) * P],
                                         wf2[:].rearrange("p k f -> p (k f)"), start=True, stop=False)
                        last = nc.tensor.matmul(w_p[:, q * 512:(q + 1) * 512], ones_b[:], bf2_s[:], start=False, stop=True)
                    last.then_inc(w_done, 1)

                def sums(i, c, part, added_before):
                    n, b, k = at(i, c)
                    if part == 0:
                        pe.wait_ge(rows_used[b], k + 2)
                        pe.wait_ge(vector_made, n + 1)
                        if added_before:
                            pe.wait_ge(added, n * 2)
                    for q in range(Q):
                        last = nc.tensor.matmul(sum_p[0:TR, part * 512:(part + 1) * 512], hot[:, b, q],
                                                msg[:, b, q, F1 + part * 512:F1 + (part + 1) * 512], start=(q == 0),
                                                stop=(q == Q - 1))
                    if part == 1:
                        last.then_inc(summed, 1)

                def step(i, c, now=True, next1=True, next2=True, first=False):
                    if next2:
                        turn(i, c + 2)
                    if next1:
                        filters(i, c + 1, used=now)
                    if next2:
                        hidden(i, c + 2)
                    if now:
                        sums(i, c, 0, not first)
                        sums(i, c, 1, not first)

                turn(0, 0)
                hidden(0, 0)
                step(0, -1, now=False)
                step(0, 0, first=True)
                step(0, 1)
                with pe.Fori(1, G1 // 2 - 1) as i:
                    step(i, 0)
                    step(i, 1)
                step(0, G1 - 2, next2=False)
                step(0, G1 - 1, next1=False, next2=False)


def conv_nodes(nc, m, agg, W1_s, W1_v, W2_s, W2_v):
    with Stage(nc, "nodes") as s:
        w1 = s.sb("w1", [P, 4, F1])
        w2 = s.sb("w2", [P, 2, F1])
        agg_t = s.sb("agg_t", [P, 8, TR])
        u = s.sb("u", [P, 4, TR])
        ab = s.sb("ab", [P, TR])
        half = s.sb("half", [P, 1])
        t_p = s.ps("t_p", 2)
        u_p = s.ps("u_p")
        y_p = s.ps("y_p")
        names = ("loaded", "prep", "turned", "kept", "u_done", "u_ln", "u_made", "y_done", "added", "aorder")
        loaded, prep, turned, kept, u_done, u_ln, u_made, y_done, added, aorder = (s.sem(n) for n in names)
        with s.block() as block:
            @block.sync
            def _(sp):
                for k, w in enumerate((W1_s[0:2 * F1:2, :], W1_s[1:2 * F1:2, :], W1_v[0:2 * F1:2, :], W1_v[1:2 * F1:2, :])):
                    sp.dma_start(w1[:, k], w).then_inc(loaded, 16)
                for k, w in enumerate((W2_s, W2_v)):
                    sp.dma_start(w2[:, k], w).then_inc(loaded, 16)
                sp.wait_ge(loaded, 96)

            @block.vector
            def _(dve):
                dve.wait_ge(loaded, 96)
                r = (2 * F1) ** -0.5
                for k, f in enumerate((Y0 * r, 3.0 ** -0.5 * r, r, Y0 * r)):
                    nc.vector.tensor_scalar(w1[:, k], w1[:, k], f, None, ALU.mult).then_inc(prep, 1)
                nc.vector.memset(half[:], 0.5).then_inc(prep, 1)
                nc.vector.tensor_scalar(w2[:], w2[:], F1 ** -0.5, None, ALU.mult).then_inc(prep, 1)
                for t in range(NT):
                    dve.wait_ge(u_ln, t + 1)
                    nc.vector.scalar_tensor_tensor(out=u[:, 0], in0=u[:, 0], scalar=0.0, in1=ab[:], op0=ALU.max,
                                                   op1=ALU.add).then_inc(u_made, 1)
                    dve.wait_ge(y_done, t + 1)
                    nc.vector.tensor_tensor(m.X[:, t, 0:F1], m.X[:, t, 0:F1], y_p[0:TR, 0:F1], ALU.add).then_inc(added, 1)
                    x = m.X[:, t, F1:D].rearrange("p (d i) -> p i d", i=3)
                    nc.vector.tensor_tensor(x, x, y_p[0:TR, F1:D].rearrange("p (i d) -> p i d", i=3), ALU.add
                                            ).then_inc(added, 1)

            @block.scalar
            def _(act):
                act.wait_ge(prep, 6)
                for t in range(NT):
                    act.wait_ge(turned, t + 1)
                    nc.scalar.copy(agg_t[:], t_p[:].rearrange("p (k n) -> p k n", k=8)[:, :, 0:TR]).then_inc(kept, 1)
                    act.wait_ge(u_done, t + 1)
                    a = Order(act, aorder, 3 * t)
                    a.link(nc.scalar.copy(u[:], u_p[:, 0:4 * TR].rearrange("p (k n) -> p k n", k=4)))
                    a.link(nc.scalar.activation(ab[:], u[:, 0], ACT.Abs))
                    a.link(nc.scalar.activation(ab[:], ab[:], ACT.Exp, scale=-1.0))
                    nc.scalar.activation(ab[:], ab[:], ACT.Ln, bias=half[:, 0:1], scale=0.5).then_inc(u_ln, 1)

            @block.tensor
            def _(pe):
                pe.wait_ge(prep, 6)
                for t in range(NT):
                    for k in range(8):
                        last = nc.tensor.transpose(t_p[:, k * P:k * P + TR], agg[k // 4][:, t, (k % 4) * F1:(k % 4 + 1) * F1],
                                                   m.ident[0:TR, 0:TR])
                    last.then_inc(turned, 1)
                    pe.wait_ge(kept, t + 1)
                    nc.tensor.matmul(u_p[:, 0:TR], w1[:, 0], agg_t[:, 0], start=True, stop=False, skip_group_check=True)
                    nc.tensor.matmul(u_p[:, 0:TR], w1[:, 1], agg_t[:, 1], start=False, stop=True, skip_group_check=True)
                    vec = u_p[:, TR:4 * TR]
                    nc.tensor.matmul(vec, w1[:, 2], agg_t[:, 2:5].rearrange("p k n -> p (k n)"), start=False, stop=False,
                                     skip_group_check=True)
                    nc.tensor.matmul(vec, w1[:, 3], agg_t[:, 5:8].rearrange("p k n -> p (k n)"), start=False, stop=True,
                                     skip_group_check=True).then_inc(u_done, 1)
                    pe.wait_ge(u_made, t + 1)
                    if t >= 1:
                        pe.wait_ge(added, 2 * t)
                    for k in range(4):
                        last = nc.tensor.matmul(y_p[0:TR, k * F1:(k + 1) * F1], u[:, k], w2[:, min(k, 1)],
                                                start=True, stop=True, skip_group_check=True)
                    last.then_inc(y_done, 1)


def store(nc, m, out):
    with Stage(nc, "store") as s:
        stored = s.sem("stored")
        with s.block() as block:
            @block.sync
            def _(sp):
                sp.dma_start(out.rearrange("(t p) d -> p t d", p=TR), m.X[:]).then_inc(stored, 16)
                sp.wait_ge(stored, 16)


class Memory:

    def __init__(self, s):
        self.X = s.sb("X", [TR, NT, D])
        self.XN = s.sb("XN", [TR, NT, D])
        self.XT_all = s.sb("XT", [P, NT * D])
        self.XT = self.XT_all[:, 0:KC * N].rearrange("p (c n) -> p c n", c=KC)
        self.iota_row = s.sb("iota_row", [P, P])
        self.iota_col = s.sb("iota_col", [P, 1])
        self.ident = s.sb("ident", [P, P])
        self.ident_b = s.sb("ident_b", [P, P], BF16)
        self.above = s.sb("above", [P, P])
        self.ones = s.sb("ones", [P, P])
        self.tile0 = s.sb("tile0", [1, G0], I32)
        self.tile1 = s.sb("tile1", [1, G1], I32)


def gps_kernel(nc, i, out, stop=99):
    rec0 = nc.dram_tensor("rec0", [G0 * GROUP, REC0], F32).ap()
    rec1 = nc.dram_tensor("rec1", [G1 * GROUP, REC1], F32).ap()
    XL = nc.dram_tensor("XL", [N, D + H], F32).ap()
    T1 = nc.dram_tensor("T1", [N, D], F32).ap()
    alpha = nc.dram_tensor("alpha", [G0 * GROUP, H], F32).ap()
    weight = nc.dram_tensor("weight", [G0 * GROUP, H], F32).ap()
    by_row = lambda v: v.rearrange("(p t) -> p t", p=TR)

    Stage.used.clear()
    with Stage(nc, "all") as s:
        m = Memory(s)
        constants(nc, m, i["x"])

        sort_edges(nc, m, "sort0", G0, REC0, rec0, m.tile0,
                   lambda key, other, rest: [(key[:, 0:ER], by_row(i["dst"])), (other[:, 0:ER], by_row(i["src"]))], 2,
                   lambda key, rest, recs: nc.vector.tensor_copy(recs[:, :, 2], key[:]), N // TR)

        def loads1(key, other, rest):
            return [(key[:], by_row(i["src"])), (other[:], by_row(i["dst"])),
                    (rest[:, 0:3 * ER], i["edge_attr_3"].rearrange("(p t) c -> p (t c)", p=TR)),
                    (rest[:, 3 * ER:4 * ER], by_row(i["edge_weight"])),
                    (rest[:, 4 * ER:24 * ER], i["edge_attr_20"].rearrange("(p t) c -> p (t c)", p=TR))]

        def fill1(key, rest, recs):
            nc.vector.tensor_copy(recs[:, :, 2:5], rest[:, 0:3 * ER].rearrange("p (t c) -> p t c", c=3))
            nc.vector.tensor_copy(recs[:, :, 5], rest[:, 3 * ER:4 * ER])
            return nc.vector.tensor_copy(recs[:, :, 6:26], rest[:, 4 * ER:24 * ER].rearrange("p (t c) -> p t c", c=F_RBF))

        sort_edges(nc, m, "sort1", G1, REC1, rec1, m.tile1, loads1, 5, fill1, 0)

        clear_semaphores(nc)
        layer_norm(nc, m, "norm0", plain)
        wqkv = i["L0_mix_W_qkv"]
        if stop >= 1:
            part = lambda k: [wqkv[c * P:(c + 1) * P, k * D:(k + 1) * D] for c in range(KC)]
            attention(nc, m, "mix0", part(0), part(1), part(2), chunk_rows(i["L0_mix_W_out"], plain),
                      bias=i["L0_mix_b_out"].unsqueeze(0))
        if stop >= 2:
            with Stage(nc, "gat") as g:
                XR = g.sb("XR", [TR, NT, 3, D + H], BF16)
                node_table(nc, m, "lr", [chunk_rows(i["L0_gnn_W_l"], plain), chunk_rows(i["L0_gnn_W_r"], plain)],
                           [(slice(0, D), [(c, 0, c) for c in range(KC)])], 1.0, XL, XR, att_w=i["L0_gnn_att"])
                edge_scores(nc, m, XR, i["L0_gnn_att"], XL, rec0, alpha)
            edge_weights(nc, m, rec0, alpha, weight)
            edge_sums(nc, m, i["L0_gnn_bias"], XL, rec0, weight)
        if stop >= 3:
            layer_norm(nc, m, "norm1", plain)
            experts(nc, m, "moe0", D, False, [i["L0_ffn_W1"]], i["L0_ffn_W2"], Top1(i["L0_ffn_Wr"], i["L0_ffn_br"]), 8,
                    b1=i["L0_ffn_b1"], b2=i["L0_ffn_b2"])
        clear_semaphores(nc)
        if stop >= 4:
            layer_norm(nc, m, "norm2", by_component)
            sc, vc = i["L1_gnn_W_in2f_s"], i["L1_gnn_W_in2f_v"]
            node_table(nc, m, "t1", [[sc, vc]], [(slice(c * P, (c + 1) * P), [(c, 0, min(c, 1))]) for c in range(KC)],
                       F1 ** -0.5, T1, None)
            rows = lambda n: chunk_rows(i[n], by_component)
            attention(nc, m, "mix1", rows("L1_mix_Wq"), rows("L1_mix_Wk"), rows("L1_mix_Wv"),
                      chunk_rows(i["L1_mix_Wo"], plain), omegas=(i["L1_mix_omega_q"], i["L1_mix_omega_k"]))
        if stop >= 5:
            convolution(nc, m, i["L1_gnn_Wf1"], i["L1_gnn_bf1"], i["L1_gnn_Wf2"], i["L1_gnn_bf2"], i["L1_gnn_W1_s"],
                        i["L1_gnn_W1_v"], i["L1_gnn_W2_s"], i["L1_gnn_W2_v"], T1, rec1)
        if stop >= 6:
            layer_norm(nc, m, "norm3", plain)
            experts(nc, m, "moe1", D, True, [i["L1_ffn_w_gate"], i["L1_ffn_w_up"]], i["L1_ffn_w_down"],
                    Top2(i["L1_ffn_router_w"]), 8)
        store(nc, m, out)


def kernel(**inputs):
    import numpy as _np
    from concourse import bacc as _bacc
    from concourse.bass_utils import run_bass_kernel_spmd as _run

    nc = _bacc.Bacc("TRN2", target_bir_lowering=False, num_devices=1)
    arrays, aps = {}, {}
    for name, value in inputs.items():
        a = _np.ascontiguousarray(value)
        arrays[f"in_{name}"] = a
        aps[name] = nc.dram_tensor(f"in_{name}", a.shape, mybir.dt.from_np(a.dtype), kind="ExternalInput").ap()
    out = nc.dram_tensor("out", (N, D), F32, kind="ExternalOutput").ap()
    gps_kernel(nc, aps, out)
    r = _run(nc, [arrays], core_ids=[0])
    return r.results[0]["out"]
```

```python
from contextlib import ExitStack

import numpy as np

import concourse.bass as bass
from concourse import mybir
from concourse.bass import IndirectOffsetOnAxis, ds

ALU = mybir.AluOpType
ACT = mybir.ActivationFunctionType
AX = mybir.AxisListType
F32 = mybir.dt.float32
BF16 = mybir.dt.bfloat16
I32 = mybir.dt.int32
U32 = mybir.dt.uint32

P = 128
N, D, H = 1250, 512, 8
HD = D // H
NT, TR = 10, 125
KC = D // P
E = 40000
ER = E // TR
CHN = 2 * TR
NCH = N // CHN
BATCH = 5
GROUP = 512
Q = GROUP // P
BIG = 1e30
PAD_ROW = 999.0


def n_groups(edges):
    g = (edges + NT * (GROUP - 1)) // GROUP
    return g + g % 2


G0, G1 = n_groups(E + N), n_groups(E)
REC0, REC1 = 4, 26
F_RBF = 20


class Order:

    def __init__(self, eng, sem, base=0):
        self.eng, self.sem, self.base, self.n = eng, sem, base, 0

    def mark(self, ins):
        ins.then_inc(self.sem, 1)
        self.n += 1

    def settle(self):
        self.eng.wait_ge(self.sem, self.base + self.n)

    def link(self, ins):
        self.mark(ins)
        self.settle()


def wait_apart(eng, sem, value, passed):
    eng.wait_ge(sem, value)
    eng.sem_inc(passed, 1)


class Stage:
    used = set()

    def __init__(self, nc, name):
        self.nc, self.name, self.ctx = nc, name, ExitStack()

    def __enter__(self):
        return self

    def __exit__(self, *x):
        return self.ctx.__exit__(*x)

    def sb(self, name, shape, dt=F32):
        return self.ctx.enter_context(self.nc.sbuf_tensor(f"{self.name}_{name}", shape, dt))

    def ps(self, name, banks=1, dt=F32):
        n = banks * (512 if dt == F32 else 1024)
        return self.ctx.enter_context(self.nc.psum_tensor(f"{self.name}_{name}", [P, n], dt))

    def sem(self, name):
        sem = self.ctx.enter_context(self.nc.semaphore(f"{self.name}_{name}"))
        Stage.used.add(sem.num)
        return sem

    def pool_dma_sem(self, name):
        return self.nc.alloc_semaphore(f"{self.name}_{name}")

    def block(self):
        return self.nc.Block()


def at(i, c):
    return i * 2 + c, c % 2, i + c // 2


def clear_semaphores(nc):
    with nc.Block() as block:
        @block.gpsimd
        def _(pool):
            first = last = None
            for n in sorted(Stage.used) + [-1]:
                if last is not None and n != last + 1:
                    pool.sem_clear(range(first, last + 1))
                    first = None
                if first is None:
                    first = n
                last = n
    Stage.used.clear()


def mid(ap, axis, count):
    a = ap.unsqueeze(axis)
    shape = list(a.shape)
    shape[axis] = count
    return a.broadcast_to(shape)


def constants(nc, m, x):
    with Stage(nc, "const") as s:
        row_i = s.sb("row_i", [P, P], I32)
        col_i = s.sb("col_i", [P, 1], I32)
        iotas, order, loaded = s.sem("iotas"), s.sem("order"), s.sem("x_loaded")
        with s.block() as block:
            @block.sync
            def _(sp):
                sp.dma_start(m.X[:], x.rearrange("(t p) d -> p t d", p=TR)).then_inc(loaded, 16)
                sp.wait_ge(loaded, 16)

            @block.gpsimd
            def _(pool):
                nc.gpsimd.iota(row_i[:], [[1, P]], 0, 0).then_inc(iotas, 1)
                nc.gpsimd.iota(col_i[:], [[0, 1]], 0, 1).then_inc(iotas, 1)

            @block.vector
            def _(dve):
                o = Order(dve, order)
                o.mark(nc.vector.memset(m.ones[:], 1.0))
                dve.wait_ge(iotas, 2)
                o.mark(nc.vector.tensor_copy(m.iota_row[:], row_i[:]))
                o.link(nc.vector.tensor_copy(m.iota_col[:], col_i[:]))
                o.mark(nc.vector.tensor_scalar(m.ident[:], m.iota_row[:], m.iota_col[:, 0:1], None, ALU.is_equal))
                o.mark(nc.vector.tensor_scalar(m.ident_b[:], m.iota_row[:], m.iota_col[:, 0:1], None, ALU.is_equal))
                o.mark(nc.vector.tensor_scalar(m.above[:], m.iota_row[:], m.iota_col[:, 0:1], None, ALU.is_gt))


def sort_edges(nc, m, name, groups, rec, rec_dram, tile_row, load_list, n_loads, fill_rest, n_self):
    T = ER + n_self
    n_batches = T // BATCH
    positions = groups * GROUP
    W = BATCH * NT
    with Stage(nc, name) as s:
        key_i = s.sb("key_i", [TR, T], I32)
        other_i = s.sb("other_i", [TR, T], I32)
        recs = s.sb("recs", [TR, T, rec])
        key = s.sb("key", [TR, T])
        tile_of = s.sb("tile_of", [TR, T])
        row_of = s.sb("row_of", [TR, T])
        tile_hot = s.sb("tile_hot", [TR, T, NT], BF16)
        zeros = s.sb("zeros", [TR, P], BF16)
        row_hot = s.sb("row_hot", [TR, 2, BATCH, TR], BF16)
        row_hot_t = s.sb("row_hot_t", [TR, 2, BATCH, TR], BF16)
        before = s.sb("before", [TR, 2, BATCH, TR], BF16)
        hist = s.sb("hist", [TR, NT])
        sizes_i = s.sb("sizes_i", [TR, NT], I32)
        sizes = s.sb("sizes", [TR, NT])
        zrow = s.sb("zrow", [TR, NT])
        starts = s.sb("starts", [TR, NT])
        base = s.sb("base", [TR, NT])
        g_iota_i = s.sb("g_iota_i", [1, groups], I32)
        g_iota = s.sb("g_iota", [1, groups])
        g_tile = s.sb("g_tile", [1, groups])
        snap_i = s.sb("snap_i", [TR, BATCH + 1, NT], I32)
        low_i = s.sb("low_i", [TR, BATCH + 1, NT], I32)
        snap_hi = s.sb("snap_hi", [TR, 2, BATCH + 1, NT], BF16)
        snap_lo = s.sb("snap_lo", [TR, 2, BATCH + 1, NT], BF16)
        picked = s.sb("picked", [TR, BATCH, NT])
        place_f = s.sb("place_f", [TR, BATCH])
        place = s.sb("place", [TR, 2, BATCH], U32)
        staged = s.sb("staged", [TR, 2, BATCH, rec])
        pads = s.sb("pads", [P, 8, rec])
        rest = s.sb("rest", [TR, T * (REC1 - 2)]) if rec == REC1 else None
        hist_p = s.ps("hist_p")[0:TR, 0:NT]
        sums_p = s.ps("sums_p")[0:TR, 0:2 * NT].rearrange("p (k a) -> p k a", k=2)
        row_hot_p = s.ps("row_hot_p", 1, BF16)[0:TR, 0:BATCH * P].rearrange("p (j e) -> p j e", j=BATCH)
        same_p = s.ps("same_p", 2)[0:TR, :].rearrange("p (j e) -> p j e", e=P)
        snap_p = s.ps("snap_p")[0:TR, 0:(BATCH + 1) * NT].rearrange("p (j a) -> p j a", a=NT)
        rank_p = s.ps("rank_p")[0:TR, 0:BATCH * NT].rearrange("p (j a) -> p j a", a=NT)

        loaded, self_ids, padded = s.sem("loaded"), s.sem("self_ids"), s.sem("padded")
        pads_made = s.sem("pads_made")
        prep, hot_made, hist_added = s.sem("prep"), s.sem("hot_made"), s.sem("hist_added")
        hist_done, sums_done, fields = s.sem("hist_done"), s.sem("sums_done"), s.sem("fields")
        hot2_made, turned, turned_kept = s.sem("hot2_made"), s.sem("turned"), s.sem("turned_kept")
        snap_added, snap_split, same_done = s.sem("snap_added"), s.sem("snap_split"), s.sem("same_done")
        before_made, ranked = s.sem("before_made"), s.sem("ranked")
        split_steps, pick_steps = s.sem("split_steps"), s.sem("pick_steps")
        placed, staged_full, hist_kept = s.sem("placed"), s.sem("staged_full"), s.sem("hist_kept")
        scattered = [s.pool_dma_sem(f"scattered{b}") for b in range(2)]
        past, act_past = s.sem("past"), s.sem("act_past")
        first_dram = nc.dram_tensor(f"{name}_first", [2, rec], F32).ap()

        with s.block() as block:
            @block.sync
            def _(sp):
                for dst, src in load_list(key_i, other_i, rest):
                    sp.dma_start(dst, src).then_inc(loaded, 16)
                sp.wait_ge(pads_made, 1)
                chunks = positions // (P * 8)
                for k in range(chunks):
                    sp.dma_start(rec_dram[k * P * 8:(k + 1) * P * 8, :].rearrange("(p j) w -> p j w", p=P),
                                 pads[:]).then_inc(padded, 16)
                left = positions - chunks * P * 8
                if left:
                    sp.dma_start(rec_dram[chunks * P * 8:positions, :].rearrange("(p j) w -> p j w", p=P),
                                 pads[:, 0:left // P, :]).then_inc(padded, 16)
                sp.wait_ge(loaded, 16 * n_loads)
                sp.wait_ge(padded, 16 * ((positions + P * 8 - 1) // (P * 8)))

            @block.gpsimd
            def _(pool):
                nc.gpsimd.iota(g_iota_i[:], [[1, groups]], 0, 0).then_inc(self_ids, 1)
                if n_self:
                    nc.gpsimd.iota(key_i[:, ER:T], [[TR, n_self]], 0, 1).then_inc(self_ids, 1)
                    nc.gpsimd.iota(other_i[:, ER:T], [[TR, n_self]], 0, 1).then_inc(self_ids, 1)
                chunks = (positions + P * 8 - 1) // (P * 8)
                pool.wait_ge(padded, 16 * chunks)
                for b in range(2):
                    nc.gpsimd.dma_start(first_dram[b:b + 1, :], pads[0:1, 0, :]).then_inc(scattered[b], 16)
                with pool.Fori(0, n_batches // 2) as i:
                    for b in range(2):
                        pool.wait_ge(placed, i * 2 + (b + 1))
                        wait_apart(pool, staged_full, i * 2 + (b + 1), past)
                        for j in range(BATCH):
                            nc.gpsimd.indirect_dma_start(
                                out=rec_dram[:, :], out_offset=IndirectOffsetOnAxis(ap=place[:, b, j:j + 1], axis=0),
                                in_=staged[:, b, j, :], in_offset=None).then_inc(scattered[b], 16)
                for b in range(2):
                    pool.wait_ge(scattered[b], 16 + 8 * T)

            @block.vector
            def _(dve):
                o = Order(dve, prep)
                o.mark(nc.vector.memset(zeros[:], 0.0))
                o.link(nc.vector.memset(pads[:], 0.0))
                if rec == REC1:
                    o.link(nc.vector.memset(pads[:, :, 2:5], 1.0))
                    nc.vector.memset(pads[:, :, 1:2], PAD_ROW).then_inc(pads_made, 1)
                else:
                    o.link(nc.vector.memset(recs[:], 0.0))
                    nc.vector.memset(pads[:, :, 1:3], PAD_ROW * TR).then_inc(pads_made, 1)
                o.mark(nc.vector.memset(zrow[:], 0.0))
                dve.wait_ge(loaded, 16 * n_loads)
                dve.wait_ge(self_ids, 3 if n_self else 1)
                o.mark(nc.vector.tensor_copy(g_iota[:], g_iota_i[:]))
                o.link(nc.vector.tensor_copy(key[:], key_i[:]))
                o.link(nc.vector.tensor_scalar(tile_of[:], key[:], float(TR), None, ALU.is_ge))
                for k in range(2, NT):
                    o.link(nc.vector.scalar_tensor_tensor(out=tile_of[:], in0=key[:], scalar=float(TR * k), in1=tile_of[:],
                                                          op0=ALU.is_ge, op1=ALU.add))
                o.link(nc.vector.scalar_tensor_tensor(out=row_of[:], in0=tile_of[:], scalar=-float(TR), in1=key[:],
                                                      op0=ALU.mult, op1=ALU.add))
                o.mark(nc.vector.tensor_tensor(tile_hot[:], mid(tile_of[:], 2, NT),
                                               mid(m.iota_row[0:TR, 0:NT], 1, T), ALU.is_equal))
                o.mark(nc.vector.tensor_copy(recs[:].bitcast(I32)[:, :, 0], other_i[:]))
                o.settle()
                o.link(nc.vector.tensor_copy(recs[:, :, 1], row_of[:]))
                fill_rest(key, rest, recs).then_inc(fields, 1)

                def hots(buf, t0):
                    return nc.vector.tensor_tensor(row_hot[:, buf], mid(m.iota_row[0:TR, 0:TR], 1, BATCH),
                                                   mid(row_of[:, ds(t0, BATCH)], 2, TR), ALU.is_equal)

                with dve.Fori(0, n_batches // 2) as i:
                    for b in range(2):
                        dve.wait_ge(hist_added, i * 2 + (b + 1))
                        hots(b, i * (2 * BATCH) + b * BATCH).then_inc(hot_made, 1)
                dve.wait_ge(hist_done, 1)
                nc.vector.tensor_copy(hist[:], hist_p).then_inc(hist_kept, 1)
                dve.wait_ge(sums_done, 1)
                o.link(nc.vector.tensor_scalar(sizes[:], sums_p[:, 1], float(GROUP - 1), None, ALU.add))
                o.link(nc.vector.tensor_copy(sizes_i[:], sizes[:]))
                o.link(nc.vector.tensor_scalar(sizes_i[:], sizes_i[:], 9, None, ALU.arith_shift_right))
                o.link(nc.vector.tensor_copy(sizes[:], sizes_i[:]))
                o.link(nc.vector.tensor_tensor_scan(starts[:], sizes[:], zrow[:], 0.0, ALU.add, ALU.add))
                o.link(nc.vector.tensor_tensor(starts[:], starts[:], sizes[:], ALU.subtract))
                o.link(nc.vector.scalar_tensor_tensor(out=base[:], in0=starts[:], scalar=float(GROUP), in1=sums_p[:, 0],
                                                      op0=ALU.mult, op1=ALU.add))
                o.link(nc.vector.tensor_scalar(g_tile[:], g_iota[:], starts[0:1, 1:2], None, ALU.is_ge))
                for k in range(2, NT):
                    o.link(nc.vector.scalar_tensor_tensor(out=g_tile[:], in0=g_iota[:], scalar=starts[0:1, k:k + 1],
                                                          in1=g_tile[:], op0=ALU.is_ge, op1=ALU.add))
                o.mark(nc.vector.tensor_copy(tile_row[0:1, 0:groups], g_tile[:]))
                o.link(nc.vector.tensor_copy(snap_i[:, BATCH], base[:]))
                o.link(nc.vector.tensor_scalar(low_i[:, BATCH], snap_i[:, BATCH], 255, None, ALU.bitwise_and))
                o.mark(nc.vector.tensor_copy(snap_lo[:, 1, BATCH], low_i[:, BATCH]))
                o.settle()
                nc.vector.tensor_tensor(snap_hi[:, 1, BATCH], snap_i[:, BATCH], low_i[:, BATCH],
                                        ALU.subtract).then_inc(snap_split, 1)

                def hots2(i, c):
                    n, b, k = at(i, c)
                    hots(b, n * BATCH).then_inc(hot2_made, 1)

                def split(i, c):
                    n, b, k = at(i, c)
                    o = Order(dve, split_steps, n * 3)
                    dve.wait_ge(snap_added, n + 1)
                    o.link(nc.vector.tensor_copy(snap_i[:], snap_p))
                    o.link(nc.vector.tensor_scalar(low_i[:], snap_i[:], 255, None, ALU.bitwise_and))
                    o.link(nc.vector.tensor_copy(snap_lo[:, b], low_i[:]))
                    nc.vector.tensor_tensor(snap_hi[:, b], snap_i[:], low_i[:], ALU.subtract).then_inc(snap_split, 1)

                def earlier(i, c):
                    n, b, k = at(i, c)
                    dve.wait_ge(same_done, n + 1)
                    nc.vector.tensor_tensor(before[:, b], same_p[:, 0:BATCH, 0:TR], mid(m.above[0:TR, 0:TR], 1, BATCH),
                                            ALU.mult).then_inc(before_made, 1)

                def pick(i, c):
                    n, b, k = at(i, c)
                    o = Order(dve, pick_steps, n * 2)
                    dve.wait_ge(ranked, n + 1)
                    o.link(nc.vector.tensor_tensor(picked[:], rank_p, tile_hot[:, ds(n * BATCH, BATCH), :], ALU.mult))
                    o.link(nc.vector.tensor_reduce(place_f[:], picked[:], AX.X, ALU.add))
                    dve.wait_ge(scattered[b], k * (16 * BATCH) + 16)
                    nc.vector.tensor_copy(place[:, b], place_f[:]).then_inc(placed, 1)

                hots2(0, 0)
                hots2(0, 1)
                split(0, 0)
                earlier(0, 0)
                with dve.Fori(0, n_batches // 2 - 1) as i:
                    for c in (1, 2):
                        hots2(i, c + 1)
                        split(i, c)
                        earlier(i, c)
                        pick(i, c - 1)
                split(0, n_batches - 1)
                earlier(0, n_batches - 1)
                pick(0, n_batches - 2)
                pick(0, n_batches - 1)

            @block.scalar
            def _(act):
                act.wait_ge(fields, 1)
                def keep(i, c):
                    n, b, k = at(i, c)
                    act.wait_ge(turned, n + 1)
                    nc.scalar.copy(row_hot_t[:, b], row_hot_p[:, :, 0:TR]).then_inc(turned_kept, 1)

                def stage(i, c):
                    n, b, k = at(i, c)
                    wait_apart(act, scattered[b], k * (16 * BATCH) + 16, act_past)
                    nc.scalar.copy(staged[:, b], recs[:, ds(n * BATCH, BATCH), :]).then_inc(staged_full, 1)

                keep(0, 0)
                keep(0, 1)
                stage(0, 0)
                with act.Fori(0, n_batches // 2 - 1) as i:
                    for c in (1, 2):
                        keep(i, c + 1)
                        stage(i, c)
                stage(0, n_batches - 1)

            @block.tensor
            def _(pe):
                pe.wait_ge(prep, 1)
                nc.tensor.matmul(hist_p, zeros[:, 0:TR], zeros[:, 0:NT], start=True, stop=False,
                                 skip_group_check=True).then_inc(hist_added, 2)
                with pe.Fori(0, n_batches // 2) as i:
                    for b in range(2):
                        pe.wait_ge(hot_made, i * 2 + (b + 1))
                        for j in range(BATCH):
                            last = nc.tensor.matmul(hist_p, row_hot[:, b, j],
                                                    tile_hot[:, i * (2 * BATCH) + (b * BATCH + j), :],
                                                    start=False, stop=False, skip_group_check=True)
                        last.then_inc(hist_added, 1)
                nc.tensor.matmul(hist_p, zeros[:, 0:TR], zeros[:, 0:NT], start=False, stop=True,
                                 skip_group_check=True).then_inc(hist_done, 1)
                pe.wait_ge(hist_kept, 1)
                nc.tensor.matmul(sums_p[:, 0], m.above[0:TR, 0:TR], hist[:], start=True, stop=True)
                nc.tensor.matmul(sums_p[:, 1], m.ones[0:TR, 0:TR], hist[:], start=True, stop=True).then_inc(sums_done, 1)

                def turn(i, c, first=False):
                    n, b, k = at(i, c)
                    pe.wait_ge(hot2_made, n + 1)
                    if not first:
                        pe.wait_ge(turned_kept, n)
                    for j in range(BATCH):
                        last = nc.tensor.transpose(row_hot_p[:, j, 0:TR], row_hot[:, b, j], m.ident_b[0:TR, 0:TR])
                    last.then_inc(turned, 1)

                def count(i, c):
                    n, b, k = at(i, c)
                    pe.wait_ge(snap_split, n + 1)
                    for part in (snap_hi, snap_lo):
                        nc.tensor.matmul(snap_p, m.ident_b[0:TR, 0:TR], mid(part[:, 1 - b, BATCH], 1, BATCH + 1),
                                         start=(part is snap_hi), stop=False, skip_group_check=True)
                    for j in range(BATCH):
                        last = nc.tensor.matmul(snap_p[:, j + 1:BATCH + 1], row_hot[:, b, j],
                                                mid(tile_hot[:, n * BATCH + j, :], 1, BATCH - j),
                                                start=False, stop=(j == BATCH - 1), skip_group_check=True)
                    last.then_inc(snap_added, 1)

                def same(i, c, first=False):
                    n, b, k = at(i, c)
                    pe.wait_ge(turned_kept, n + 1)
                    if not first:
                        pe.wait_ge(before_made, n)
                    for j in range(BATCH):
                        last = nc.tensor.matmul(same_p[:, j, 0:TR], row_hot_t[:, b, j], row_hot_t[:, b, j],
                                                start=True, stop=True, skip_group_check=True)
                    last.then_inc(same_done, 1)

                def order_edges(i, c, first=False):
                    n, b, k = at(i, c)
                    pe.wait_ge(snap_split, n + 2)
                    pe.wait_ge(before_made, n + 1)
                    if not first:
                        pe.wait_ge(placed, n)
                    for j in range(BATCH):
                        nc.tensor.matmul(rank_p[:, j], row_hot_t[:, b, j], snap_hi[:, b, j], start=(j == 0), stop=False,
                                         skip_group_check=True)
                        nc.tensor.matmul(rank_p[:, j], row_hot_t[:, b, j], snap_lo[:, b, j], start=False, stop=False,
                                         skip_group_check=True)
                        last = nc.tensor.matmul(rank_p[:, j], before[:, b, j], tile_hot[:, n * BATCH + j, :], start=False,
                                                stop=True, skip_group_check=True)
                    last.then_inc(ranked, 1)

                turn(0, 0, first=True)
                count(0, 0)
                same(0, 0, first=True)
                turn(0, 1)
                count(0, 1)
                same(0, 1)
                order_edges(0, 0, first=True)
                turn(0, 2)
                count(0, 2)
                same(0, 2)
                order_edges(0, 1)
                turn(0, 3)
                with pe.Fori(1, n_batches // 2 - 1) as i:
                    for c in (1, 2):
                        count(i, c)
                        same(i, c)
                        order_edges(i, c - 1)
                        turn(i, c + 1)
                count(0, n_batches - 1)
                same(0, n_batches - 1)
                order_edges(0, n_batches - 2)
                order_edges(0, n_batches - 1)


def layer_norm(nc, m, name, src_cols):
    with Stage(nc, name) as s:
        stats = s.sb("stats", [TR, NT, 6])
        mv = s.sb("mv", [TR, NT, 2])
        rstd = s.sb("rstd", [TR, NT])
        turned_p = [s.ps(f"turned_p{b}") for b in range(2)]
        order, normed, turned, kept = s.sem("order"), s.sem("normed"), s.sem("turned"), s.sem("kept")
        var_made, std_made = s.sem("var_made"), s.sem("std_made")
        with s.block() as block:
            @block.vector
            def _(dve):
                o = Order(dve, order)
                for t in range(NT):
                    o.mark(nc.vector.bn_stats(stats[:, t], m.X[:, t]))
                o.settle()
                for t in range(NT):
                    o.mark(nc.vector.bn_aggr(mv[:, t], stats[:, t]))
                o.settle()
                nc.vector.tensor_scalar(rstd[:], mv[:, :, 1], 1e-5, None, ALU.add).then_inc(var_made, 1)
                dve.wait_ge(std_made, 1)
                o.link(nc.vector.reciprocal(rstd[:], rstd[:]))
                for t in range(NT):
                    nc.vector.tensor_scalar(m.XN[:, t], m.X[:, t], mv[:, t, 0:1], rstd[:, t:t + 1],
                                            ALU.subtract, ALU.mult).then_inc(normed, 1)

            @block.tensor
            def _(pe):
                for t in range(NT):
                    pe.wait_ge(normed, t + 1)
                    if t >= 2:
                        pe.wait_ge(kept, t - 1)
                    for c in range(KC):
                        last = nc.tensor.transpose(turned_p[t % 2][:, c * P:c * P + TR], m.XN[:, t, src_cols(c)],
                                                   m.ident[0:TR, 0:TR])
                    last.then_inc(turned, 1)

            @block.scalar
            def _(act):
                act.wait_ge(var_made, 1)
                nc.scalar.activation(rstd[:], rstd[:], ACT.Sqrt).then_inc(std_made, 1)
                for t in range(NT):
                    act.wait_ge(turned, t + 1)
                    nc.scalar.copy(m.XT[:, :, t * TR:(t + 1) * TR],
                                   turned_p[t % 2][:].rearrange("p (c n) -> p c n", c=KC)[:, :, 0:TR]).then_inc(kept, 1)


def plain(c):
    return slice(c * P, (c + 1) * P)


def by_component(c):
    return slice(0, P) if c == 0 else slice(P + c - 1, D, 3)


def chunk_rows(w, cols):
    return [w[cols(c), :] for c in range(KC)]


def attention(nc, m, name, wq, wk, wv, wo, bias=None, omegas=None):
    with Stage(nc, name) as s:
        Wq, Wk, Wv, Wo = (s.sb(n, [P, KC, D]) for n in ("Wq", "Wk", "Wv", "Wo"))
        bo = s.sb("bo", [1, D])
        QT = s.sb("QT", [P, KC, N])
        KV = s.sb("KV", [P, KC, P + 2])
        om = s.sb("om", [P, 2, P])
        pair = s.sb("pair", [P, 2])
        pair_rows = s.sb("pair_rows", [P, P])
        t1 = s.sb("t1", [P, 2, D])
        t2 = s.sb("t2", [P, 2, D])
        t3 = s.sb("t3", [P, 2, D])
        t4 = s.sb("t4", [P, 2, D])
        kt = s.sb("kt", [P, 2, KC, TR])
        kt2 = s.sb("kt2", [P, 2, KC, TR])
        kphi = s.sb("kphi", [TR, 2, D])
        vt = s.sb("vt", [TR, 2, KC, P + 1])
        den = s.sb("den", [TR, NT, H])
        att = s.sb("att", [TR, 2, D])
        att_t = s.sb("att_t", [P, 2, KC, TR])
        A = [s.ps(f"A{b}") for b in range(2)]
        B = [s.ps(f"B{b}") for b in range(2)]
        C = s.ps("C", 2)
        S = [s.ps(f"S{b}") for b in range(2)]
        loaded, ready = s.sem("loaded"), s.sem("ready")
        q_done, q_kept, f_done, f_kept = s.sem("q_done"), s.sem("q_kept"), s.sem("f_done"), s.sem("f_kept")
        q_exp, q_phi = s.sem("q_exp"), s.sem("q_phi")
        k_done, k_kept, kf_done, k_pre, k_exp, k_phi = (s.sem(n) for n in ("k_done", "k_kept", "kf_done", "k_pre", "k_exp", "k_phi"))
        v_done, v_kept, kv_added = s.sem("v_done"), s.sem("v_kept"), s.sem("kv_added")
        kv_ready, o_done, o_norm, o_turned, o_kept, y_done, y_added = (
            s.sem(n) for n in ("kv_ready", "o_done", "o_norm", "o_turned", "o_kept", "y_done", "y_added"))
        order, aorder = s.sem("order"), s.sem("aorder")
        loads = [(W[:, c], rows) for W, ws in ((Wq, wq), (Wk, wk), (Wv, wv), (Wo, wo)) for c, rows in enumerate(ws)]
        if bias is not None:
            loads.append((bo[:], bias))
        if omegas is not None:
            for k, w in enumerate(omegas):
                for h in range(2):
                    loads.append((om[h * HD:(h + 1) * HD, k, h * HD:(h + 1) * HD], w))
        n_loads = 16 * len(loads)
        n_q = NCH * 2
        L1 = omegas is not None

        with s.block() as block:
            @block.sync
            def _(sp):
                if L1:
                    sp.wait_ge(ready, 1)
                for dst, src in loads:
                    sp.dma_start(dst, src).then_inc(loaded, 16)
                sp.wait_ge(loaded, n_loads)

            @block.tensor
            def _(pe):
                pe.wait_ge(loaded, n_loads)
                pe.wait_ge(ready, 4)
                for n in range(n_q):
                    c, g = n // 2, n % 2
                    nodes = slice(c * CHN, (c + 1) * CHN)
                    if n >= 2:
                        pe.wait_ge(q_kept if L1 else q_phi, n - 1)
                    for j in range(2):
                        hp = 2 * g + j
                        for k in range(KC):
                            last = nc.tensor.matmul(A[n % 2][:, j * 256:j * 256 + CHN], Wq[:, k, hp * P:(hp + 1) * P],
                                                    m.XT[:, k, nodes], start=(k == 0), stop=(k == KC - 1))
                    last.then_inc(q_done, 1)
                    if L1:
                        pe.wait_ge(q_kept, n + 1)
                        if n >= 2:
                            pe.wait_ge(q_phi, n - 1)
                        q = t1[:, n % 2].rearrange("p (j n) -> p j n", j=2)
                        q2 = t2[:, n % 2].rearrange("p (j n) -> p j n", j=2)
                        for j in range(2):
                            nc.tensor.matmul(B[n % 2][:, j * 256:j * 256 + CHN], om[:, 0], q[:, j, 0:CHN],
                                             start=True, stop=True)
                            last = nc.tensor.matmul(S[n % 2][:, j * 256:j * 256 + CHN], pair_rows[:],
                                                    q2[:, j, 0:CHN], start=True, stop=True)
                        last.then_inc(f_done, 1)
                pe.wait_ge(q_phi, n_q)
                for t in range(NT):
                    rows = slice(t * TR, (t + 1) * TR)
                    if L1:
                        if t >= 2:
                            pe.wait_ge(k_kept, t - 1)
                        for j in range(KC):
                            for k in range(KC):
                                last = nc.tensor.matmul(A[t % 2][:, j * P:j * P + TR], Wk[:, k, j * P:(j + 1) * P],
                                                        m.XT[:, k, rows], start=(k == 0), stop=(k == KC - 1))
                        last.then_inc(k_done, 1)
                        pe.wait_ge(k_kept, t + 1)
                        if t >= 2:
                            pe.wait_ge(k_phi, t - 1)
                        for j in range(KC):
                            last = nc.tensor.matmul(S[t % 2][0:TR, j * P:(j + 1) * P], kt[:, t % 2, j], om[:, 1],
                                                    start=True, stop=True)
                        for j in range(KC):
                            last = nc.tensor.matmul(B[1][0:TR, 2 * j:2 * j + 2], kt2[:, t % 2, j], pair[:],
                                                    start=(j == 0), stop=(j == KC - 1), skip_group_check=True)
                        last.then_inc(kf_done, 1)
                    else:
                        if t >= 2:
                            pe.wait_ge(k_phi, t - 1)
                        for k in range(KC):
                            last = nc.tensor.matmul(S[t % 2][0:TR, :], m.XT[:, k, rows], Wk[:, k], start=(k == 0),
                                                    stop=(k == KC - 1))
                        last.then_inc(kf_done, 1)
                    if t >= 1:
                        pe.wait_ge(v_kept, t)
                    for k in range(KC):
                        last = nc.tensor.matmul(B[0][0:TR, :], m.XT[:, k, rows], Wv[:, k], start=(k == 0),
                                                stop=(k == KC - 1))
                    last.then_inc(v_done, 1)
                    pe.wait_ge(k_phi, t + 1)
                    pe.wait_ge(v_kept, t + 1)
                    for j in range(KC):
                        bank, off = j // 2, (j % 2) * (P + 1)
                        last = nc.tensor.matmul(C[:, bank * 512 + off:bank * 512 + off + P + 1], kphi[:, t % 2, j * P:(j + 1) * P],
                                                vt[:, t % 2, j], start=(t == 0 and j % 2 == 0), stop=(t == NT - 1),
                                                skip_group_check=True)
                    last.then_inc(kv_added, 1)
                pe.wait_ge(kv_ready, 1)
                for t in range(NT + 1):
                    if t < NT:
                        rows = slice(t * TR, (t + 1) * TR)
                        if t >= 1:
                            pe.wait_ge(o_norm, t)
                        for j in range(KC):
                            bank, off = j // 2, (j % 2) * (P + 2)
                            last = nc.tensor.matmul(C[0:TR, bank * 512 + off:bank * 512 + off + P + 2], QT[:, j, rows],
                                                    KV[:, j], start=True, stop=True, skip_group_check=True)
                        last.then_inc(o_done, 1)
                    if t >= 1:
                        u = t - 1
                        if u >= 2:
                            pe.wait_ge(o_kept, u - 1)
                        pe.wait_ge(o_norm, u + 1)
                        for j in range(KC):
                            last = nc.tensor.transpose(A[u % 2][:, j * P:j * P + TR], att[:, u % 2, j * P:(j + 1) * P],
                                                       m.ident[0:TR, 0:TR])
                        last.then_inc(o_turned, 1)
                        pe.wait_ge(o_kept, u + 1)
                        if u >= 2:
                            pe.wait_ge(y_added, u - 1)
                        for k in range(KC):
                            last = nc.tensor.matmul(B[u % 2][0:TR, :], att_t[:, u % 2, k], Wo[:, k], start=(k == 0),
                                                    stop=(k == KC - 1 and bias is None))
                        if bias is not None:
                            last = nc.tensor.matmul(B[u % 2][0:TR, :], m.ones[0:1, 0:TR], bo[:], start=False, stop=True)
                        last.then_inc(y_done, 1)

            @block.scalar
            def _(act):
                o = Order(act, aorder)
                for n in range(n_q):
                    c, g = n // 2, n % 2
                    nodes = slice(c * CHN, (c + 1) * CHN)
                    v = lambda x: x[:, n % 2].rearrange("p (j n) -> p j n", j=2)[:, :, 0:CHN]
                    w = lambda x: x[n % 2][:].rearrange("p (j n) -> p j n", j=2)[:, :, 0:CHN]
                    if L1:
                        act.wait_ge(q_done, n + 1)
                        if n >= 2:
                            act.wait_ge(q_phi, n - 1)
                        o.mark(nc.scalar.activation(v(t1), w(A), ACT.Copy, scale=HD ** -0.5))
                        o.settle()
                        nc.scalar.activation(v(t2), v(t1), ACT.Square).then_inc(q_kept, 1)
                        act.wait_ge(f_kept, n + 1)
                        nc.scalar.activation(v(t3), v(t3), ACT.Exp).then_inc(q_exp, 1)
                        nc.scalar.activation(v(t4), v(t4), ACT.Exp).then_inc(q_exp, 1)
                    else:
                        act.wait_ge(f_kept, n + 1)
                        nc.scalar.activation(v(t1), v(t1), ACT.Exp).then_inc(q_exp, 1)
                for t in range(NT):
                    if L1:
                        act.wait_ge(k_done, t + 1)
                        if t >= 2:
                            act.wait_ge(kf_done, t - 1)
                        x = A[t % 2][:].rearrange("p (j n) -> p j n", j=KC)[:, :, 0:TR]
                        o.mark(nc.scalar.activation(kt[:, t % 2], x, ACT.Copy, scale=HD ** -0.5))
                        o.settle()
                        nc.scalar.activation(kt2[:, t % 2], kt[:, t % 2], ACT.Square).then_inc(k_kept, 1)
                        act.wait_ge(k_pre, t + 1)
                        nc.scalar.activation(t3[0:TR, t % 2, 0:H], t3[0:TR, t % 2, 0:H], ACT.Exp).then_inc(k_exp, 1)
                        nc.scalar.activation(t1[0:TR, t % 2], t1[0:TR, t % 2], ACT.Exp).then_inc(k_exp, 1)
                    else:
                        act.wait_ge(k_pre, t + 1)
                        nc.scalar.activation(t1[0:TR, t % 2], t1[0:TR, t % 2], ACT.Exp).then_inc(k_exp, 1)
                    act.wait_ge(v_done, t + 1)
                    if t >= 2:
                        act.wait_ge(kv_added, t - 1)
                    nc.scalar.copy(vt[:, t % 2, :, 0:P], B[0][0:TR, :].rearrange("p (j n) -> p j n", j=KC)
                                   ).then_inc(v_kept, 1)
                for t in range(NT):
                    act.wait_ge(o_turned, t + 1)
                    if t >= 2:
                        act.wait_ge(y_done, t - 1)
                    nc.scalar.copy(att_t[:, t % 2], A[t % 2][:].rearrange("p (j n) -> p j n", j=KC)[:, :, 0:TR]
                                   ).then_inc(o_kept, 1)

            @block.vector
            def _(dve):
                o = Order(dve, order)
                nc.vector.memset(om[:], 0.0).then_inc(ready, 1)
                o.mark(nc.vector.memset(KV[:], 0.0))
                nc.vector.memset(vt[:], 1.0).then_inc(ready, 1)
                o.link(nc.vector.tensor_scalar(pair[:, 1:2], m.iota_col[:, 0:1], float(HD), None, ALU.is_ge))
                o.link(nc.vector.tensor_scalar(pair[:, 0:1], m.iota_col[:, 0:1], float(HD), None, ALU.is_lt))
                nc.vector.tensor_scalar(pair_rows[:, 0:HD], m.ones[:, 0:HD], pair[:, 0:1], None, ALU.mult).then_inc(ready, 1)
                nc.vector.tensor_scalar(pair_rows[:, HD:P], m.ones[:, 0:HD], pair[:, 1:2], None, ALU.mult).then_inc(ready, 1)
                for n in range(n_q):
                    c, g = n // 2, n % 2
                    nodes = slice(c * CHN, (c + 1) * CHN)
                    v = lambda x: x[:, n % 2].rearrange("p (j n) -> p j n", j=2)[:, :, 0:CHN]
                    w = lambda x: x[n % 2][:].rearrange("p (j n) -> p j n", j=2)[:, :, 0:CHN]
                    out = QT[:, 2 * g:2 * g + 2, nodes]
                    if L1:
                        dve.wait_ge(f_done, n + 1)
                        if n >= 2:
                            o.settle()
                        o.mark(nc.vector.tensor_scalar(v(t3), w(B), 50.0, None, ALU.min))
                        nc.vector.tensor_scalar(v(t4), w(S), 1e-16, -0.5, ALU.max, ALU.mult).then_inc(f_kept, 1)
                        dve.wait_ge(q_exp, 2 * n + 2)
                        nc.vector.scalar_tensor_tensor(out=out, in0=v(t4), scalar=1e-8, in1=v(t3), op0=ALU.max,
                                                       op1=ALU.mult).then_inc(q_phi, 1)
                    else:
                        dve.wait_ge(q_done, n + 1)
                        if n >= 2:
                            dve.wait_ge(q_phi, n - 1)
                        nc.vector.tensor_scalar(v(t1), w(A), 0.0, None, ALU.min).then_inc(f_kept, 1)
                        dve.wait_ge(q_exp, n + 1)
                        nc.vector.scalar_tensor_tensor(out=out, in0=w(A), scalar=0.0, in1=v(t1), op0=ALU.max,
                                                       op1=ALU.add).then_inc(q_phi, 1)
                dve.wait_ge(q_phi, n_q)
                for t in range(NT):
                    dve.wait_ge(kf_done, t + 1)
                    f, k = S[t % 2][0:TR, :], kphi[:, t % 2]
                    if t >= 2:
                        dve.wait_ge(k_phi, t - 1)
                        dve.wait_ge(kv_added, t - 1)
                    if L1:
                        o.mark(nc.vector.tensor_scalar(t1[0:TR, t % 2], f, 50.0, None, ALU.min))
                        nc.vector.tensor_scalar(t3[0:TR, t % 2, 0:H], B[1][0:TR, 0:H], 1e-16, -0.5, ALU.max,
                                                ALU.mult).then_inc(k_pre, 1)
                        dve.wait_ge(k_exp, 2 * t + 2)
                        o.link(nc.vector.tensor_scalar(t4[0:TR, t % 2, 0:H], t3[0:TR, t % 2, 0:H], 1e-8, None, ALU.max))
                        nc.vector.tensor_tensor(k.rearrange("p (h d) -> p h d", h=H),
                                                t1[0:TR, t % 2].rearrange("p (h d) -> p h d", h=H),
                                                mid(t4[0:TR, t % 2, 0:H], 2, HD), ALU.mult).then_inc(k_phi, 1)
                    else:
                        nc.vector.tensor_scalar(t1[0:TR, t % 2], f, 0.0, None, ALU.min).then_inc(k_pre, 1)
                        dve.wait_ge(k_exp, t + 1)
                        nc.vector.scalar_tensor_tensor(out=k, in0=f, scalar=0.0, in1=t1[0:TR, t % 2], op0=ALU.max,
                                                       op1=ALU.add).then_inc(k_phi, 1)
                dve.wait_ge(kv_added, NT)
                for j in range(KC):
                    off = (j // 2) * 512 + (j % 2) * (P + 1)
                    for h in range(2):
                        r = slice(h * HD, (h + 1) * HD)
                        o.mark(nc.vector.tensor_copy(KV[r, j, r], C[r, off + h * HD:off + (h + 1) * HD]))
                        last = nc.vector.tensor_copy(KV[r, j, P + h:P + h + 1], C[r, off + P:off + P + 1])
                        if j == KC - 1 and h == 1:
                            last.then_inc(kv_ready, 1)
                        else:
                            o.mark(last)
                o.settle()
                for t in range(NT):
                    dve.wait_ge(o_done, t + 1)
                    if t >= 2:
                        dve.wait_ge(o_turned, t - 1)
                    for b in range(2):
                        x = C[0:TR, b * 512:b * 512 + 2 * (P + 2)].rearrange("p (j n) -> p j n", j=2)
                        dn = den[:, t, 4 * b:4 * b + 4].rearrange("p (j h) -> p j h", j=2)
                        o.link(nc.vector.tensor_scalar(dn, x[:, :, P:P + 2], 0.0 if L1 else 1e-6, None, ALU.add))
                    o.link(nc.vector.reciprocal(den[:, t], den[:, t]))
                    for b in range(2):
                        x = C[0:TR, b * 512:b * 512 + 2 * (P + 2)].rearrange("p (j n) -> p j n", j=2)[:, :, 0:P]
                        for j in range(2):
                            hs = 4 * b + 2 * j
                            last = nc.vector.tensor_tensor(
                                att[:, t % 2, hs * HD:(hs + 2) * HD].rearrange("p (h d) -> p h d", h=2),
                                x[:, j].rearrange("p (h d) -> p h d", h=2), mid(den[:, t, hs:hs + 2], 2, HD), ALU.mult)
                            if b == 1 and j == 1:
                                last.then_inc(o_norm, 1)
                            else:
                                o.mark(last)
                    if t >= 1:
                        dve.wait_ge(y_done, t)
                        nc.vector.tensor_tensor(m.X[:, t - 1], m.X[:, t - 1], B[(t - 1) % 2][0:TR, :],
                                                ALU.add).then_inc(y_added, 1)
                dve.wait_ge(y_done, NT)
                nc.vector.tensor_tensor(m.X[:, NT - 1], m.X[:, NT - 1], B[(NT - 1) % 2][0:TR, :],
                                        ALU.add).then_inc(y_added, 1)


def node_table(nc, m, name, weights, blocks, scale, table, keep, att_w=None):
    with Stage(nc, name) as s:
        Ws = [s.sb(f"W{k}", [P, len(w), w[0].shape[1]]) for k, w in enumerate(weights)]
        W = D if att_w is None else D + H
        rows_sb = s.sb("rows", [TR, 2, W])
        att = s.sb("att", [TR, D])
        att_r = s.sb("att_r", [1, D])
        y = s.sb("y", [TR, D])
        kept_rows = s.sb("kept_rows", [TR, 2, W])
        rest = s.sb("rest", [TR, 2, W])
        att_p = s.ps("att_p")
        order, full, att_done = s.sem("order"), s.sem("full"), s.sem("att_done")
        out_p = [s.ps(f"out_p{b}") for b in range(2)]
        keep_p = [s.ps(f"keep_p{b}") for b in range(2)]
        loaded, done, copied, stored = s.sem("loaded"), s.sem("done"), s.sem("copied"), [s.sem(f"stored{b}") for b in range(2)]
        keep_done, kept = s.sem("keep_done"), s.sem("kept")
        loads = [(W_[:, c], rows) for W_, ws in zip(Ws, weights) for c, rows in enumerate(ws)]
        if att_w is not None:
            loads.append((att_r[:], att_w.rearrange("h c -> (h c)").unsqueeze(0)))
        with s.block() as block:
            @block.sync
            def _(sp):
                for dst, src in loads:
                    sp.dma_start(dst, src).then_inc(loaded, 16)
                for t in range(NT):
                    sp.wait_ge(copied if att_w is None else full, t + 1)
                    sp.dma_start(table[t * TR:(t + 1) * TR, :], rows_sb[:, t % 2]).then_inc(stored[t % 2], 16)
                for b in range(2):
                    sp.wait_ge(stored[b], 16 * NT // 2)

            @block.tensor
            def _(pe):
                pe.wait_ge(loaded, 16 * len(loads))
                if att_w is not None:
                    nc.tensor.matmul(att_p[0:TR, :], m.ones[0:1, 0:TR], att_r[:], start=True, stop=True).then_inc(att_done, 1)
                for t in range(NT):
                    rows = slice(t * TR, (t + 1) * TR)
                    if t >= 2:
                        pe.wait_ge(copied, t - 1)
                    for cols, pairs in blocks:
                        for i, (c, w, k) in enumerate(pairs):
                            last = nc.tensor.matmul(out_p[t % 2][0:TR, cols], m.XT[:, c, rows], Ws[w][:, k],
                                                    start=(i == 0), stop=(i == len(pairs) - 1), skip_group_check=True)
                    last.then_inc(done, 1)
                    if keep is not None:
                        if t >= 2:
                            pe.wait_ge(kept, t - 1)
                        for k in range(KC):
                            last = nc.tensor.matmul(keep_p[t % 2][0:TR, :], m.XT[:, k, rows], Ws[1][:, k],
                                                    start=(k == 0), stop=(k == KC - 1))
                        last.then_inc(keep_done, 1)

            @block.scalar
            def _(act):
                for t in range(NT):
                    act.wait_ge(done, t + 1)
                    if t >= 2:
                        act.wait_ge(stored[t % 2], 16 * (t // 2))
                    nc.scalar.activation(rows_sb[:, t % 2, 0:D], out_p[t % 2][0:TR, :], ACT.Copy, scale=scale).then_inc(copied, 1)

            @block.vector
            def _(dve):
                if keep is None:
                    return
                o = Order(dve, order)
                dve.wait_ge(att_done, 1)
                o.link(nc.vector.tensor_copy(att[:], att_p[0:TR, :]))
                heads = lambda x: x.rearrange("p (h d) -> p h d", h=H)
                for t in range(NT):
                    dve.wait_ge(copied, t + 1)
                    o.link(nc.vector.tensor_tensor(y[:], rows_sb[:, t % 2, 0:D], att[:], ALU.mult))
                    nc.vector.tensor_reduce(rows_sb[:, t % 2, D:W], heads(y[:]), AX.X, ALU.add).then_inc(full, 1)
                    dve.wait_ge(full, t + 1)
                    row = kept_rows[:, t % 2]
                    dve.wait_ge(keep_done, t + 1)
                    nc.vector.tensor_copy(row[:, 0:D], keep_p[t % 2][0:TR, :]).then_inc(kept, 1)
                    dve.wait_ge(kept, t + 1)
                    o.link(nc.vector.tensor_tensor(y[:], row[:, 0:D], att[:], ALU.mult))
                    o.link(nc.vector.tensor_reduce(row[:, D:W], heads(y[:]), AX.X, ALU.add))
                    o.link(nc.vector.tensor_copy(keep[:, t, 0], row))
                    o.link(nc.vector.tensor_tensor(rest[:, 0], row, keep[:, t, 0], ALU.subtract))
                    o.link(nc.vector.tensor_copy(keep[:, t, 1], rest[:, 0]))
                    o.link(nc.vector.tensor_tensor(rest[:, 1], rest[:, 0], keep[:, t, 1], ALU.subtract))
                    o.link(nc.vector.tensor_copy(keep[:, t, 2], rest[:, 1]))


def edge_scores(nc, m, XR, att_w, XL_dram, rec_dram, alpha_dram):
    W = D + H
    HQ = Q // 2
    with Stage(nc, "scores") as s:
        recs = s.sb("recs", [P, G0 + 1, Q * REC0])
        alpha = s.sb("alpha", [P, G0, Q * H])
        att = s.sb("att", [P, D])
        att_r = s.sb("att_r", [1, D])
        idx = s.sb("idx", [P, 2, Q], U32)
        xl = s.sb("xl", [P, 2, Q, W])
        hot = s.sb("hot", [P, 2, Q, TR], BF16)
        hot_t = s.sb("hot_t", [TR, 2, Q, P], BF16)
        past = s.sem("past")
        z = s.sb("z", [P, 2, Q, D])
        linear = s.sb("linear", [P, 2, Q, H])
        turned_p = s.ps("turned_p", 1, BF16)
        z_p = s.ps("z_p", Q)
        lin_p = s.ps("lin_p")
        att_p = s.ps("att_p")
        loaded, att_done, att_kept = s.sem("loaded"), s.sem("att_done"), s.sem("att_kept")
        gathered = [s.pool_dma_sem(f"gathered{b}") for b in range(2)]
        idx_ready, hot_made, turned, kept = s.sem("idx_ready"), s.sem("hot_made"), s.sem("turned"), s.sem("kept")
        z_done, z_relu, chain = s.sem("z_done"), s.sem("z_relu"), s.sem("chain")
        stored = s.sem("stored")
        rows_used = [s.sem(f"rows_used{b}") for b in range(2)]
        with s.block() as block:
            @block.sync
            def _(sp):
                sp.dma_start(att_r[:], att_w.rearrange("h c -> (h c)").unsqueeze(0)).then_inc(loaded, 16)
                sp.dma_start(recs[:, 0:G0], rec_dram.rearrange("(g p q) w -> p g (q w)", p=P, q=Q)).then_inc(loaded, 16)
                sp.wait_ge(chain, 3 * G0)
                sp.dma_start(alpha_dram.rearrange("(g p q) h -> p g (q h)", p=P, q=Q), alpha[:]).then_inc(stored, 16)
                sp.wait_ge(stored, 16)

            @block.gpsimd
            def _(pool):
                pool.wait_ge(loaded, 32)
                with pool.Fori(0, G0 // 2) as i:
                    for b in range(2):
                        rows = recs[:, i * 2 + b, :].rearrange("p (q w) -> p q w", w=REC0)
                        pool.wait_ge(rows_used[b], i + 1)
                        nc.gpsimd.tensor_copy(idx[:, b], rows.bitcast(U32)[:, :, 0]).then_inc(idx_ready, 1)
                        wait_apart(pool, idx_ready, i * 2 + (b + 1), past)
                        for q in range(Q):
                            nc.gpsimd.indirect_dma_start(
                                out=xl[:, b, q, :], out_offset=None, in_=XL_dram[:, :],
                                in_offset=IndirectOffsetOnAxis(ap=idx[:, b, q:q + 1], axis=0)).then_inc(gathered[b], 16)

            @block.vector
            def _(dve):
                for b in range(2):
                    dve.sem_inc(rows_used[b], 1)
                nc.vector.memset(recs[:, G0], 0.0)
                dve.wait_ge(att_done, 1)
                nc.vector.tensor_copy(att[:], att_p[:]).then_inc(att_kept, 1)
                dve.wait_ge(att_kept, 1)
                dve.wait_ge(loaded, 32)

                def hots(i, c):
                    n, b, k = at(i, c)
                    rows = recs[:, n, :].rearrange("p (q w) -> p q w", w=REC0)
                    nc.vector.tensor_tensor(hot[:, b], mid(m.iota_row[:, 0:TR], 1, Q), mid(rows[:, :, 1], 2, TR),
                                            ALU.is_equal).then_inc(hot_made, 1)

                def add(i, c):
                    n, b, k = at(i, c)
                    dve.wait_ge(z_done, n * 2 + 2)
                    dve.wait_ge(gathered[b], k * (16 * Q) + 16 * Q)
                    nc.vector.tensor_tensor(linear[:, b], lin_p[:, 0:Q * H].rearrange("p (q h) -> p q h", q=Q),
                                            xl[:, b, :, D:W], ALU.add).then_inc(rows_used[b], 1)
                    dve.wait_ge(rows_used[b], k + 2)

                def score(i, c):
                    n, b, k = at(i, c)
                    o = Order(dve, chain, n * 3)
                    dve.wait_ge(z_relu, n * 2 + 2)
                    o.link(nc.vector.tensor_tensor(z[:, b], z[:, b], mid(att[:], 1, Q), ALU.mult))
                    o.link(nc.vector.tensor_reduce(alpha[:, n, :], z[:, b].rearrange("p q (h d) -> p (q h) d", h=H), AX.X,
                                                   ALU.add))
                    o.link(nc.vector.scalar_tensor_tensor(out=alpha[:, n, :], in0=linear[:, b].rearrange("p q h -> p (q h)"),
                                                          scalar=0.2, in1=alpha[:, n, :], op0=ALU.mult, op1=ALU.add))

                hots(0, 0)
                hots(0, 1)
                add(0, 0)
                hots(0, 2)
                add(0, 1)
                hots(0, 3)
                score(0, 0)
                with dve.Fori(1, G0 // 2 - 1) as i:
                    for c in range(2):
                        hots(i, c + 2)
                        add(i, c)
                        score(i, c - 1)
                add(0, G0 - 2)
                score(0, G0 - 3)
                add(0, G0 - 1)
                score(0, G0 - 2)
                score(0, G0 - 1)

            @block.scalar
            def _(act):
                def keep(i, c):
                    n, b, k = at(i, c)
                    act.wait_ge(turned, n + 1)
                    nc.scalar.copy(hot_t[:, b], turned_p[0:TR, 0:Q * P].rearrange("p (q e) -> p q e", q=Q)).then_inc(kept, 1)

                def relu(i, c, first=False, last=False):
                    n, b, k = at(i, c)
                    for h in range(2):
                        act.wait_ge(z_done, n * 2 + (h + 1))
                        if h == 0 and not first:
                            act.wait_ge(chain, n * 3 - 4)
                        nc.scalar.activation(z[:, b, h * HQ:(h + 1) * HQ],
                                             z_p[:, h * HQ * D:(h + 1) * HQ * D].rearrange("p (q d) -> p q d", q=HQ),
                                             ACT.Relu, scale=0.8).then_inc(z_relu, 1)
                        if h == 0 and not last:
                            keep(i, c + 1)

                keep(0, 0)
                for c in range(2):
                    relu(0, c, first=True)
                with act.Fori(1, G0 // 2 - 1) as i:
                    for c in range(2):
                        relu(i, c)
                relu(0, G0 - 2)
                relu(0, G0 - 1, last=True)

            @block.tensor
            def _(pe):
                pe.wait_ge(loaded, 32)
                nc.tensor.matmul(att_p[:], m.ones[0:1, :], att_r[:], start=True, stop=True).then_inc(att_done, 1)

                def turn(i, c, first=False):
                    n, b, k = at(i, c)
                    pe.wait_ge(hot_made, n + 1)
                    if not first:
                        pe.wait_ge(kept, n)
                    for q in range(Q):
                        last = nc.tensor.transpose(turned_p[0:TR, q * P:(q + 1) * P], hot[:, b, q], m.ident_b[:])
                    last.then_inc(turned, 1)

                def spread(i, c, first=False, end=False):
                    n, b, k = at(i, c)
                    tile = nc.tensor.value_load(m.tile0[0:1, ds(n, 1)], min_val=0, max_val=NT - 1)
                    pe.wait_ge(kept, n + 1)
                    if not first:
                        _, other, before = at(i, c - 1)
                        pe.wait_ge(rows_used[other], before + 2)
                    pe.wait_ge(gathered[b], k * (16 * Q) + 16 * Q)
                    for q in range(Q):
                        if not first and q % HQ == 0:
                            pe.wait_ge(z_relu, n * 2 + (q // HQ - 1))
                        nc.tensor.matmul(z_p[:, q * D:(q + 1) * D], m.ident[:], xl[:, b, q, 0:D], start=True, stop=False)
                        for part in range(3):
                            nc.tensor.matmul(z_p[:, q * D:(q + 1) * D], hot_t[:, b, q], XR[:, tile, part, 0:D],
                                             start=False, stop=(part == 2))
                            last = nc.tensor.matmul(lin_p[:, q * H:(q + 1) * H], hot_t[:, b, q], XR[:, tile, part, D:W],
                                                    start=(part == 0 and q == 0), stop=(part == 2), skip_group_check=True)
                        if q % HQ == HQ - 1:
                            last.then_inc(z_done, 1)
                        if q == HQ - 1 and not end:
                            turn(i, c + 1)

                turn(0, 0, first=True)
                spread(0, 0, first=True)
                spread(0, 1)
                with pe.Fori(1, G0 // 2 - 1) as i:
                    for c in range(2):
                        spread(i, c)
                spread(0, G0 - 2)
                spread(0, G0 - 1, end=True)


def edge_weights(nc, m, rec_dram, alpha_dram, weight_dram):
    L = G0 * GROUP // P
    with Stage(nc, "weights") as s:
        a = s.sb("a", [P, L, H])
        recs = s.sb("recs", [P, L, REC0])
        mx = s.sb("mx", [P, L, H])
        bw = s.sb("bw", [P, L])
        cut_f = s.sb("cut_f", [P, L])
        cut_b = s.sb("cut_b", [P, L])
        at_first = s.sb("at_first", [P, L])
        at_last = s.sb("at_last", [P, L])
        ends = s.sb("ends", [P, 4, H])
        rows = s.sb("rows", [H, 4, P])
        cut = s.sb("cut", [H, 4, P])
        run = s.sb("run", [H, 2, P])
        carry = s.sb("carry", [H, 2, P])
        carried = s.sb("carried", [P, 2, H])
        ends_p, back_p = s.ps("ends_p"), s.ps("back_p")
        loaded, order, ends_made, ends_turned = s.sem("loaded"), s.sem("order"), s.sem("ends_made"), s.sem("ends_turned")
        carry_made, carry_turned, shifted, expd, stored = (s.sem(n) for n in ("carry_made", "carry_turned", "shifted", "expd", "stored"))
        with s.block() as block:
            @block.sync
            def _(sp):
                sp.dma_start(a[:], alpha_dram.rearrange("(p l) h -> p l h", p=P)).then_inc(loaded, 16)
                sp.dma_start(recs[:], rec_dram.rearrange("(p l) w -> p l w", p=P)).then_inc(loaded, 16)
                sp.wait_ge(loaded, 32)
                sp.wait_ge(expd, 1)
                sp.dma_start(weight_dram.rearrange("(p l) h -> p l h", p=P), a[:]).then_inc(stored, 16)
                sp.wait_ge(stored, 16)

            @block.vector
            def _(dve):
                o = Order(dve, order)
                node = recs[:, :, 2]

                def penalty(out, x, y):
                    o.link(nc.vector.tensor_tensor(out, x, y, ALU.is_equal))
                    o.link(nc.vector.tensor_scalar(out, out, BIG, -BIG, ALU.mult, ALU.add))

                dve.wait_ge(loaded, 32)
                o.mark(nc.vector.memset(cut_f[:], -BIG))
                o.mark(nc.vector.memset(cut_b[:], -BIG))
                o.mark(nc.vector.memset(cut[:], -BIG))
                o.mark(nc.vector.memset(carry[:], -BIG))
                o.settle()
                penalty(cut_f[:, 1:L], node[:, 1:L], node[:, 0:L - 1])
                o.link(nc.vector.tensor_copy(cut_b[:, 0:L - 1], cut_f[:, 1:L]))
                for h in range(H):
                    o.mark(nc.vector.tensor_tensor_scan(mx[:, :, h], cut_f[:], a[:, :, h], -BIG, ALU.add, ALU.max))
                o.settle()
                o.mark(nc.vector.tensor_copy(ends[:, 0], mx[:, L - 1]))
                for h in range(H):
                    o.link(nc.vector.tensor_tensor_scan(bw[:, ::-1], cut_b[:, ::-1], a[:, ::-1, h], -BIG, ALU.add, ALU.max))
                    o.mark(nc.vector.tensor_copy(ends[:, 1, h:h + 1], bw[:, 0:1]))
                    o.link(nc.vector.tensor_tensor(mx[:, :, h], mx[:, :, h], bw[:], ALU.max))
                o.mark(nc.vector.tensor_copy(ends[:, 2], node[:, 0:1].broadcast_to([P, H])))
                o.mark(nc.vector.tensor_copy(ends[:, 3], node[:, L - 1:L].broadcast_to([P, H])))
                o.settle()
                nc.vector.memset(bw[:, 0:1], 0.0).then_inc(ends_made, 1)
                dve.wait_ge(ends_turned, 1)
                o.link(nc.vector.tensor_copy(rows[:], ends_p[0:H, :].rearrange("p (k n) -> p k n", k=4)))
                first, last_ = rows[:, 2], rows[:, 3]
                penalty(cut[:, 0, 1:P], first[:, 1:P], last_[:, 0:P - 1])
                o.link(nc.vector.tensor_copy(cut[:, 1, 0:P - 1], cut[:, 0, 1:P]))
                penalty(cut[:, 2], first, last_)
                o.link(nc.vector.tensor_tensor(cut[:, 3], cut[:, 2], cut[:, 1], ALU.min))
                o.link(nc.vector.tensor_tensor(cut[:, 2], cut[:, 2], cut[:, 0], ALU.min))
                o.mark(nc.vector.tensor_tensor_scan(run[:, 0], cut[:, 2], rows[:, 0], -BIG, ALU.add, ALU.max))
                o.link(nc.vector.tensor_tensor_scan(run[:, 1, ::-1], cut[:, 3, ::-1], rows[:, 1, ::-1], -BIG,
                                                    ALU.add, ALU.max))
                o.mark(nc.vector.tensor_tensor(carry[:, 0, 1:P], run[:, 0, 0:P - 1], cut[:, 0, 1:P], ALU.add))
                o.mark(nc.vector.tensor_tensor(carry[:, 1, 0:P - 1], run[:, 1, 1:P], cut[:, 1, 0:P - 1], ALU.add))
                o.settle()
                nc.vector.memset(run[:, 0, 0:1], 0.0).then_inc(carry_made, 1)
                dve.wait_ge(carry_turned, 1)
                o.link(nc.vector.tensor_copy(carried[:], back_p[:, 0:2 * H].rearrange("p (k h) -> p k h", k=2)))
                for out, j in ((at_first, 0), (at_last, L - 1)):
                    o.link(nc.vector.tensor_scalar(out[:], node, recs[:, j, 2:3], None, ALU.is_equal))
                    o.link(nc.vector.tensor_scalar(out[:], out[:], BIG, -BIG, ALU.mult, ALU.add))
                for k, pen in enumerate((at_first, at_last)):
                    for h in range(H):
                        o.mark(nc.vector.scalar_tensor_tensor(out=mx[:, :, h], in0=pen[:], scalar=carried[:, k, h:h + 1],
                                                              in1=mx[:, :, h], op0=ALU.add, op1=ALU.max))
                    o.settle()
                nc.vector.tensor_tensor(a[:], a[:], mx[:], ALU.subtract).then_inc(shifted, 1)

            @block.tensor
            def _(pe):
                pe.wait_ge(ends_made, 1)
                for k in range(4):
                    last = nc.tensor.transpose(ends_p[0:H, k * P:(k + 1) * P], ends[:, k], m.ident[:])
                last.then_inc(ends_turned, 1)
                pe.wait_ge(carry_made, 1)
                for k in range(2):
                    last = nc.tensor.transpose(back_p[:, k * H:(k + 1) * H], carry[:, k], m.ident[0:H, 0:H])
                last.then_inc(carry_turned, 1)

            @block.scalar
            def _(act):
                act.wait_ge(shifted, 1)
                nc.scalar.activation(a[:], a[:], ACT.Exp).then_inc(expd, 1)


def edge_sums(nc, m, bias, XL_dram, rec_dram, weight_dram):
    W = D + H
    RB = 3
    assert G0 % (2 * RB) == 0
    with Stage(nc, "sums") as s:
        recs = s.sb("recs", [P, G0, Q * REC0])
        wts = s.sb("wts", [P, G0, Q * H])
        idx = s.sb("idx", [P, RB, Q], U32)
        xl = s.sb("xl", [P, RB, Q, W])
        msg = s.sb("msg", [P, 2, Q, W])
        hot = s.sb("hot", [P, 2, Q, TR])
        past = s.sem("past")
        acc = s.sb("acc", [TR, NT, W])
        bias_r = s.sb("bias_r", [1, D])
        g1 = s.sb("g1", [TR, 2, D])
        sum_p = [s.ps(f"sum_p{b}", 2) for b in range(2)]
        bias_p = s.ps("bias_p")
        loaded, acc_zero, bias_done = s.sem("loaded"), s.sem("acc_zero"), s.sem("bias_done")
        gathered = [s.pool_dma_sem(f"gathered{r}") for r in range(RB)]
        idx_ready, summed, added = s.sem("idx_ready"), s.sem("summed"), s.sem("added")
        msg_made = [s.sem(f"msg_made{b}") for b in range(2)]
        order, pre, expd = s.sem("order"), s.sem("pre"), s.sem("expd")
        with s.block() as block:
            @block.sync
            def _(sp):
                sp.dma_start(bias_r[:], bias.unsqueeze(0)).then_inc(loaded, 16)
                sp.dma_start(recs[:], rec_dram.rearrange("(g p q) w -> p g (q w)", p=P, q=Q)).then_inc(loaded, 16)
                sp.dma_start(wts[:], weight_dram.rearrange("(g p q) h -> p g (q h)", p=P, q=Q)).then_inc(loaded, 16)
                sp.wait_ge(loaded, 48)

            @block.gpsimd
            def _(pool):
                pool.wait_ge(loaded, 48)

                def gather(i, c, first=False):
                    n, r = i * (2 * RB) + c, c % RB
                    rows = recs[:, n, :].rearrange("p (q w) -> p q w", w=REC0)
                    if not first:
                        _, b, k = at(i * RB, c - RB)
                        pool.wait_ge(msg_made[b], k * 3 + 4)
                    nc.gpsimd.tensor_copy(idx[:, r], rows.bitcast(U32)[:, :, 0]).then_inc(idx_ready, 1)
                    wait_apart(pool, idx_ready, n + 1, past)
                    for q in range(Q):
                        nc.gpsimd.indirect_dma_start(
                            out=xl[:, r, q, :], out_offset=None, in_=XL_dram[:, :],
                            in_offset=IndirectOffsetOnAxis(ap=idx[:, r, q:q + 1], axis=0)).then_inc(gathered[r], 16)

                for c in range(2 * RB):
                    gather(0, c, first=(c < RB))
                with pool.Fori(1, G0 // (2 * RB)) as i:
                    for c in range(2 * RB):
                        gather(i, c)

            @block.vector
            def _(dve):
                for b in range(2):
                    dve.sem_inc(msg_made[b], 1)
                nc.vector.memset(acc[:], 0.0).then_inc(acc_zero, 1)
                dve.wait_ge(acc_zero, 1)
                dve.wait_ge(loaded, 48)

                def messages(i, c):
                        n, b, k = at(i * RB, c)
                        r, turn = c % RB, i * 2 + c // RB
                        rows = recs[:, n, :].rearrange("p (q w) -> p q w", w=REC0)
                        w = wts[:, n, :]
                        nc.vector.tensor_tensor(hot[:, b], mid(m.iota_row[:, 0:TR], 1, Q), mid(rows[:, :, 1], 2, TR),
                                                ALU.is_equal).then_inc(msg_made[b], 1)
                        nc.vector.tensor_copy(msg[:, b, :, D:W], w.rearrange("p (q h) -> p q h", q=Q)).then_inc(msg_made[b], 1)
                        dve.wait_ge(gathered[r], turn * (16 * Q) + 16 * Q)
                        nc.vector.tensor_tensor(
                            msg[:, b, :, 0:D].rearrange("p q (h d) -> p q h d", h=H),
                            xl[:, r, :, 0:D].rearrange("p q (h d) -> p q h d", h=H),
                            mid(w.rearrange("p (q h) -> p q h", q=Q), 3, HD), ALU.mult).then_inc(msg_made[b], 1)

                def add(i, c):
                        n, b, k = at(i * RB, c)
                        tile = nc.vector.value_load(m.tile0[0:1, ds(n, 1)], min_val=0, max_val=NT - 1)
                        dve.wait_ge(summed, n + 1)
                        nc.vector.tensor_tensor(acc[:, tile, :], acc[:, tile, :], sum_p[b][0:TR, 0:W],
                                                ALU.add).then_inc(added, 1)
                        dve.wait_ge(added, n + 1)

                messages(0, 0)
                for c in range(1, 2 * RB):
                    messages(0, c)
                    add(0, c - 1)
                with dve.Fori(1, G0 // (2 * RB)) as i:
                    for c in range(2 * RB):
                        messages(i, c)
                        add(i, c - 1)
                add(0, G0 - 1)
                o = Order(dve, order)
                for t in range(NT):
                    den = acc[:, t, D:W]
                    o.mark(nc.vector.tensor_scalar(den, den, 1e-16, None, ALU.max))
                o.settle()
                o.link(nc.vector.reciprocal(acc[:, :, D:W], acc[:, :, D:W]))
                dve.wait_ge(bias_done, 1)
                for t in range(NT):
                    x = acc[:, t, 0:D]
                    o.link(nc.vector.tensor_tensor(x.rearrange("p (h d) -> p h d", h=H), x.rearrange("p (h d) -> p h d", h=H),
                                                   mid(acc[:, t, D:W], 2, HD), ALU.mult))
                    o.link(nc.vector.tensor_tensor(x, x, bias_p[0:TR, :], ALU.add))
                    if t >= 2:
                        o.settle()
                    nc.vector.tensor_scalar(g1[:, t % 2], x, 0.0, None, ALU.min).then_inc(pre, 1)
                    o.mark(nc.vector.tensor_scalar(x, x, 0.0, -1.0, ALU.max, ALU.add))
                    o.mark(nc.vector.tensor_tensor(m.X[:, t], m.X[:, t], m.XN[:, t], ALU.add))
                    o.settle()
                    dve.wait_ge(expd, t + 1)
                    o.link(nc.vector.tensor_tensor(x, x, g1[:, t % 2], ALU.add))
                    o.link(nc.vector.tensor_tensor(m.X[:, t], m.X[:, t], x, ALU.add))

            @block.scalar
            def _(act):
                for t in range(NT):
                    act.wait_ge(pre, t + 1)
                    nc.scalar.activation(g1[:, t % 2], g1[:, t % 2], ACT.Exp).then_inc(expd, 1)

            @block.tensor
            def _(pe):
                pe.wait_ge(loaded, 48)
                nc.tensor.matmul(bias_p[:], m.ones[0:1, :], bias_r[:], start=True, stop=True).then_inc(bias_done, 1)
                with pe.Fori(0, G0 // 2) as i:
                    for b in range(2):
                        n = i * 2 + b
                        pe.wait_ge(msg_made[b], i * 3 + 4)
                        for q in range(Q):
                            nc.tensor.matmul(sum_p[b][0:TR, 0:D], hot[:, b, q], msg[:, b, q, 0:D], start=(q == 0),
                                             stop=(q == Q - 1))
                            last = nc.tensor.matmul(sum_p[b][0:TR, D:W], hot[:, b, q], msg[:, b, q, D:W],
                                                    start=(q == 0), stop=(q == Q - 1))
                        last.then_inc(summed, 1)


CAPACITY = 256


def mixture(nc, m, name, layer, gated, w1s, w2, route, b1=None, b2=None):
    n_exp = w2.shape[0]
    K = route.choices
    cap = CAPACITY * K
    with Stage(nc, f"{name}_all") as s:
        left = s.sb("left", [TR, NT, n_exp])
        over = m.over[0:1, layer:layer + 1]
        sparse_experts(nc, m, name, gated, w1s, w2, route, n_exp, K, cap, left, over, b1, b2)
        with nc.If(nc.values_load(over, min_val=0, max_val=1) > 0):
            dense_experts(nc, m, f"{name}_dense", gated, w1s, w2, n_exp, left, b1, b2)


def sparse_experts(nc, m, name, gated, w1s, w2, route, n_exp, K, cap, left, over, b1, b2):
    F = w1s[0].shape[2]
    FC = F // P
    n1 = len(w1s)
    CT = cap // P
    J = K * NT
    slots = n_exp * cap
    rows_dram = nc.dram_tensor(f"{name}_rows", [slots + K * N, D], F32).ap()
    y_dram = nc.dram_tensor(f"{name}_y", [slots, D], F32).ap()
    with Stage(nc, name) as s:
        W_all = s.sb("W", [P, 2, n1 * KC * F + FC * D])
        W1 = [[W_all[:, b, k * KC * F:(k + 1) * KC * F].rearrange("p (c f) -> p c f", c=KC) for k in range(n1)]
              for b in range(2)]
        W2 = [W_all[:, b, n1 * KC * F:].rearrange("p (f d) -> p f d", f=FC) for b in range(2)]
        b2_r = [s.sb(f"b2_{b}", [1, D]) for b in range(2)] if b2 is not None else None
        b1_c = s.sb("b1_c", [P, n_exp, FC]) if b1 is not None else None
        b1_rows = s.sb("b1_rows", [n_exp * FC, P]) if b1 is not None else None
        Wr = s.sb("Wr", [P, KC, n_exp])
        r_rows = s.sb("r_rows", [n_exp, D]) if gated else None
        br = s.sb("br", [1, n_exp])
        hits = s.sb("hits", [TR, K, NT, n_exp])
        wts = s.sb("wts", [TR, K, NT])
        tmp = [s.sb(f"tmp{k}", [TR, NT, n_exp]) for k in range(2)]
        small = s.sb("small", [TR, 4, NT])
        rank = s.sb("rank", [TR, J, n_exp])
        ahead = s.sb("ahead", [TR, J + 1, n_exp])
        place = s.sb("place", [TR, J])
        expert = s.sb("expert", [TR, J])
        fits = s.sb("fits", [TR, J])
        spare = s.sb("spare", [TR, J])
        send_f = s.sb("send_f", [TR, J])
        send = s.sb("send", [TR, J], U32)
        fetch = s.sb("fetch", [TR, J], U32)
        peak = s.sb("peak", [TR, 1])
        zeros = s.sb("zeros", [P, D])
        xt = s.sb("xt", [P, KC, cap])
        hid = s.sb("hid", [P, FC, cap])
        gate = s.sb("gate", [P, 2, cap])
        y_sb = s.sb("y_sb", [P, CT, D])
        rows_sb = m.XN_all[:, 0:2 * CT * D].rearrange("p (b s d) -> p b s d", b=2, s=CT)
        up_p = [[s.ps(f"up_p{k}_{b}") for b in range(2)] for k in range(n1)]
        y_p = [s.ps(f"y_p{b}") for b in range(2)]
        turn_p = [s.ps(f"turn_p{b}") for b in range(2)]
        log_p, rank_p = up_p[0]
        r_loaded, r_turned, r_kept, logged, shifted, expd = (
            s.sem(n) for n in ("r_loaded", "r_turned", "r_kept", "logged", "shifted", "expd"))
        order, hits_made, ranked, zeros_made, zeroed, sent = (
            s.sem(n) for n in ("order", "hits_made", "ranked", "zeros_made", "zeroed", "sent"))
        w_loaded = [s.sem(f"w_loaded{b}") for b in range(2)]
        rows_loaded = [s.sem(f"rows_loaded{b}") for b in range(2)]
        turned, xt_kept, up_done, gate_made, hid_made, y_kept, y_stored, act_past = (
            s.sem(n) for n in ("turned", "xt_kept", "up_done", "gate_made", "hid_made", "y_kept", "y_stored", "act_past"))
        y_done = [s.sem(f"y_done{b}") for b in range(2)]
        summed = s.sem("summed")
        scattered = s.pool_dma_sem("scattered")
        fetched = [s.pool_dma_sem(f"fetched{k}") for k in range(K)]
        per_load = 16 * (n1 + 1 + (b2 is not None))
        n_route = 16 * (route.n_loads + (b1 is not None))

        def load_weights(sp, e, b):
            for k in range(n1):
                sp.dma_start(W1[b][k], w1s[k][e].rearrange("(c p) f -> p c f", p=P)).then_inc(w_loaded[b], 16)
            sp.dma_start(W2[b], w2[e].rearrange("(c p) f -> p c f", p=P)).then_inc(w_loaded[b], 16)
            if b2 is not None:
                sp.dma_start(b2_r[b][:], b2[e].unsqueeze(0)).then_inc(w_loaded[b], 16)

        with s.block() as block:
            @block.sync
            def _(sp):
                route.load(sp, r_loaded, Wr, r_rows, br)
                if b1 is not None:
                    sp.dma_start(b1_rows[:], b1.rearrange("e (c p) -> (e c) p", p=P)).then_inc(r_loaded, 16)
                sp.wait_ge(zeros_made, 1)
                sp.dma_start(rows_dram[0:slots, :].rearrange("(p s) d -> p s d", p=P),
                             mid(zeros[:], 1, slots // P)).then_inc(zeroed, 16)
                for b in range(2):
                    load_weights(sp, b, b)
                sp.wait_ge(r_loaded, n_route)
                for b in range(2):
                    sp.wait_ge(w_loaded[b], per_load)

            @block.tensor
            def _(pe):
                pe.wait_ge(r_loaded, n_route)
                if gated:
                    for c in range(KC):
                        last = nc.tensor.transpose(y_p[0][:, c * n_exp:(c + 1) * n_exp], r_rows[:, c * P:(c + 1) * P],
                                                   m.ident[0:n_exp, 0:n_exp])
                    last.then_inc(r_turned, 1)
                    pe.wait_ge(r_kept, 1)
                else:
                    nc.tensor.transpose(y_p[0][:, 0:n_exp * FC], b1_rows[:],
                                        m.ident[0:n_exp * FC, 0:n_exp * FC]).then_inc(r_turned, 1)
                for t in range(NT):
                    out = log_p[0:TR, t * n_exp:(t + 1) * n_exp]
                    for k in range(KC):
                        last = nc.tensor.matmul(out, m.XT[:, k, t * TR:(t + 1) * TR], Wr[:, k], start=(k == 0),
                                                stop=(k == KC - 1 and gated), skip_group_check=True)
                    if not gated:
                        last = nc.tensor.matmul(out, m.ones[0:1, 0:TR], br[:], start=False, stop=True,
                                                skip_group_check=True)
                last.then_inc(logged, 1)
                pe.wait_ge(hits_made, 1)
                all_hits = hits[:].rearrange("p k t e -> p (k t e)")
                nc.tensor.matmul(rank_p[0:TR, 0:J * n_exp], m.above[0:TR, 0:TR], all_hits, start=True, stop=True)
                nc.tensor.matmul(rank_p[0:TR, J * n_exp:2 * J * n_exp], m.ones[0:TR, 0:TR], all_hits, start=True,
                                 stop=True).then_inc(ranked, 1)

            @block.scalar
            def _(act):
                route.act(act, shifted, expd, tmp, small)

            @block.vector
            def _(dve):
                o = Order(dve, order)
                nc.vector.memset(zeros[:], 0.0).then_inc(zeros_made, 1)
                dve.wait_ge(r_turned, 1)
                if gated:
                    nc.vector.tensor_copy(Wr[:], y_p[0][:, 0:KC * n_exp].rearrange("p (c e) -> p c e", c=KC)).then_inc(r_kept, 1)
                else:
                    nc.vector.tensor_copy(b1_c[:], y_p[0][:, 0:n_exp * FC].rearrange("p (e c) -> p e c", c=FC)
                                          ).then_inc(r_kept, 1)
                dve.wait_ge(logged, 1)
                route.choose(nc, dve, o, log_p[0:TR, 0:NT * n_exp].rearrange("p (t e) -> p t e", t=NT), hits, wts, tmp,
                             small, shifted, expd)
                o.settle()
                dve.sem_inc(hits_made, 1)
                by_choice = hits[:].rearrange("p k t e -> p (k t) e")
                o.link(nc.vector.tensor_tensor(rank[:], by_choice, mid(m.iota_row[0:TR, 0:n_exp], 1, J), ALU.mult))
                o.mark(nc.vector.tensor_reduce(expert[:], rank[:], AX.X, ALU.add))
                o.link(nc.vector.tensor_scalar(spare[:], m.iota_row[0:TR, 0:J], float(TR), float(slots), ALU.mult, ALU.add))
                o.link(nc.vector.tensor_scalar(spare[:], spare[:], m.iota_col[0:TR, 0:1], None, ALU.add))
                o.link(nc.vector.memset(ahead[:, 0], 0.0))
                dve.wait_ge(ranked, 1)
                for j in range(J):
                    o.link(nc.vector.tensor_tensor(ahead[:, j + 1], ahead[:, j],
                                                   rank_p[0:TR, (J + j) * n_exp:(J + j + 1) * n_exp], ALU.add))
                o.link(nc.vector.tensor_tensor(rank[:], rank_p[0:TR, 0:J * n_exp].rearrange("p (j e) -> p j e", j=J),
                                               ahead[:, 0:J], ALU.add))
                o.link(nc.vector.tensor_tensor(rank[:], rank[:], by_choice, ALU.mult))
                o.link(nc.vector.tensor_reduce(place[:], rank[:], AX.X, ALU.add))
                o.link(nc.vector.tensor_scalar(fits[:], place[:], float(cap), None, ALU.is_lt))
                o.link(nc.vector.scalar_tensor_tensor(out=place[:], in0=expert[:], scalar=float(cap), in1=place[:],
                                                      op0=ALU.mult, op1=ALU.add))
                o.link(nc.vector.tensor_tensor(send_f[:], place[:], spare[:], ALU.subtract))
                o.link(nc.vector.tensor_tensor(send_f[:], send_f[:], fits[:], ALU.mult))
                o.link(nc.vector.tensor_tensor(send_f[:], send_f[:], spare[:], ALU.add))
                o.link(nc.vector.tensor_copy(send[:], send_f[:]))
                dve.sem_inc(sent, 1)
                o.link(nc.vector.tensor_tensor(place[:], place[:], fits[:], ALU.mult))
                o.mark(nc.vector.tensor_copy(fetch[:], place[:]))
                o.mark(nc.vector.tensor_reduce(peak[:], ahead[:, J], AX.X, ALU.max))
                all_wts = wts[:].rearrange("p k t -> p (k t)")
                o.link(nc.vector.tensor_tensor(expert[:], all_wts, fits[:], ALU.mult))
                o.link(nc.vector.tensor_scalar(over, peak[0:1, :], float(cap), None, ALU.is_gt))
                o.link(nc.vector.tensor_tensor(spare[:], all_wts, expert[:], ALU.subtract))
                o.link(nc.vector.tensor_copy(all_wts, expert[:]))
                for k in range(K):
                    target = left if k == 0 else tmp[0]
                    o.link(nc.vector.tensor_tensor(target[:], hits[:, k], mid(spare[:, k * NT:(k + 1) * NT], 2, n_exp),
                                                   ALU.mult))
                    if k:
                        o.link(nc.vector.tensor_tensor(left[:], left[:], tmp[0][:], ALU.add))

            @block.gpsimd
            def _(pool):
                pool.wait_ge(zeroed, 16)
                pool.wait_ge(sent, 1)
                for j in range(J):
                    nc.gpsimd.indirect_dma_start(
                        out=rows_dram[:, :], out_offset=IndirectOffsetOnAxis(ap=send[:, j:j + 1], axis=0),
                        in_=m.XN[:, j % NT, :], in_offset=None).then_inc(scattered, 16)
                pool.wait_ge(scattered, 16 * J)

        with s.block() as block:
            def over_experts(eng, step):
                for c in range(2):
                    step(0, c, first=(c == 0))
                with eng.Fori(1, n_exp // 2 - 1) as i:
                    for c in range(2):
                        step(i, c)
                for c in range(2):
                    step(0, n_exp - 2 + c, last=(c == 1))

            @block.sync
            def _(sp):
                def load_rows(i, c):
                    e, b, k = at(i, c)
                    sp.dma_start(rows_sb[:, b], rows_dram[ds(e * cap, cap), :].rearrange("(s p) d -> p s d", p=P)
                                 ).then_inc(rows_loaded[b], 16)

                def step(i, c, more=True):
                    e, b, k = at(i, c)
                    if more:
                        sp.wait_ge(turned, e * KC + KC)
                        load_rows(i, c + 2)
                        sp.wait_ge(y_done[b], k * CT + CT)
                        load_weights(sp, e + 2, b)
                    sp.wait_ge(y_kept, e * CT + (CT + 2))
                    sp.dma_start(y_dram[ds(e * cap, cap), :].rearrange("(s p) d -> p s d", p=P), y_sb[:]).then_inc(y_stored, 16)

                load_rows(0, 0)
                load_rows(0, 1)
                with sp.Fori(0, n_exp // 2 - 1) as i:
                    for c in range(2):
                        step(i, c)
                for c in range(2):
                    step(0, n_exp - 2 + c, more=False)
                sp.wait_ge(y_stored, 16 * n_exp)

            @block.tensor
            def _(pe):
                def turn(i, c):
                    e, b, k = at(i, c)
                    pe.wait_ge(rows_loaded[b], k * 16 + 16)
                    for c in range(KC):
                        pe.wait_ge(xt_kept, e * KC + (c + 1))
                        for t in range(CT):
                            last = nc.tensor.transpose(turn_p[c % 2][:, t * P:(t + 1) * P],
                                                       rows_sb[:, b, t, c * P:(c + 1) * P], m.ident[:])
                        last.then_inc(turned, 1)

                def step(i, c, first=False, last=False):
                    e, b, k = at(i, c)
                    if first:
                        turn(i, c)
                    else:
                        pe.wait_ge(w_loaded[b], k * per_load + per_load)
                    pe.wait_ge(xt_kept, e * KC + (KC + 2))
                    for f in range(FC):
                        pe.wait_ge(hid_made, e * FC + (f + 1))
                        for w in range(n1):
                            for kc in range(KC):
                                mm = nc.tensor.matmul(up_p[w][f % 2][:, 0:cap], W1[b][w][:, kc, f * P:(f + 1) * P],
                                                      xt[:, kc], start=(kc == 0), stop=(kc == KC - 1))
                        mm.then_inc(up_done, 1)
                    if not last:
                        turn(i, c + 1)
                    pe.wait_ge(hid_made, e * FC + (FC + 2))
                    for t in range(CT):
                        out = y_p[(c * CT + t) % 2]
                        pe.wait_ge(y_kept, e * CT + (t + 1))
                        for f in range(FC):
                            mm = nc.tensor.matmul(out[:], hid[:, f, t * P:(t + 1) * P], W2[b][:, f], start=(f == 0),
                                                  stop=(f == FC - 1 and b2 is None))
                        if b2 is not None:
                            mm = nc.tensor.matmul(out[:], m.ones[0:1, :], b2_r[b][:], start=False, stop=True)
                        mm.then_inc(y_done[b], 1)

                over_experts(pe, step)

            @block.scalar
            def _(act):
                def keep(i, c):
                    e, b, k = at(i, c)
                    for c in range(KC):
                        act.wait_ge(turned, e * KC + (c + 1))
                        nc.scalar.copy(xt[:, c], turn_p[c % 2][:, 0:cap]).then_inc(xt_kept, 1)

                def step(i, c, first=False, last=False):
                    e, b, k = at(i, c)
                    if first:
                        keep(i, c)
                    for f in range(FC):
                        if gated:
                            act.wait_ge(up_done, e * FC + (f + 1))
                            act.wait_ge(hid_made, e * FC + (f + 1))
                            nc.scalar.activation(gate[:, f % 2], up_p[0][f % 2][:, 0:cap], ACT.Silu).then_inc(gate_made, 1)
                        else:
                            wait_apart(act, up_done, e * FC + (f + 1), act_past)
                            nc.scalar.activation(hid[:, f], up_p[0][f % 2][:, 0:cap], ACT.Relu,
                                                 bias=b1_c[:, e, f:f + 1]).then_inc(hid_made, 1)
                    if not last:
                        keep(i, c + 1)

                act.sem_inc(xt_kept, 2)
                if not gated:
                    act.sem_inc(hid_made, 2)
                over_experts(act, step)

            @block.vector
            def _(dve):
                def step(i, c, first=False, last=False):
                    e, b, k = at(i, c)
                    if gated:
                        for f in range(FC):
                            dve.wait_ge(gate_made, e * FC + (f + 1))
                            nc.vector.tensor_tensor(hid[:, f], gate[:, f % 2], up_p[1][f % 2][:, 0:cap],
                                                    ALU.mult).then_inc(hid_made, 1)
                    if not first:
                        dve.wait_ge(y_stored, e * 16)
                    for t in range(CT):
                        dve.wait_ge(y_done[b], k * CT + (t + 1))
                        nc.vector.tensor_copy(y_sb[:, t], y_p[(c * CT + t) % 2][:]).then_inc(y_kept, 1)

                dve.sem_inc(y_kept, 2)
                if gated:
                    dve.sem_inc(hid_made, 2)
                over_experts(dve, step)

        with s.block() as block:
            back = [m.XN, W_all[0:TR, 0, 0:NT * D].rearrange("p (t d) -> p t d", t=NT) if K > 1 else None]

            @block.gpsimd
            def _(pool):
                for j in range(J):
                    nc.gpsimd.indirect_dma_start(
                        out=back[j // NT][:, j % NT, :], out_offset=None, in_=y_dram[:, :],
                        in_offset=IndirectOffsetOnAxis(ap=fetch[:, j:j + 1], axis=0)).then_inc(fetched[j // NT], 16)

            @block.vector
            def _(dve):
                o = Order(dve, summed)
                for k in range(K):
                    dve.wait_ge(fetched[k], 16 * NT)
                    for t in range(NT):
                        o.mark(nc.vector.scalar_tensor_tensor(out=m.X[:, t], in0=back[k][:, t], scalar=wts[:, k, t:t + 1],
                                                              in1=m.X[:, t], op0=ALU.mult, op1=ALU.add))
                    o.settle()


def dense_experts(nc, m, name, gated, w1s, w2, n_exp, wts, b1=None, b2=None):
    F = w1s[0].shape[2]
    FC = F // P
    n1 = len(w1s)
    with Stage(nc, name) as s:
        W1 = [[s.sb(f"W1_{k}_{b}", [P, KC, F]) for k in range(n1)] for b in range(2)]
        W2 = [s.sb(f"W2_{b}", [P, FC, D]) for b in range(2)]
        b2_r = [s.sb(f"b2_{b}", [1, D]) for b in range(2)] if b2 is not None else None
        b1_c = s.sb("b1_c", [P, n_exp, FC]) if b1 is not None else None
        hid = s.sb("hid", [P, 2, FC, CHN])
        gate = s.sb("gate", [P, 2, CHN])
        cur = s.sb("cur", [TR, 2, NT])
        up_p = [[s.ps(f"up_p{k}_{b}") for b in range(2)] for k in range(n1)]
        y_p = [s.ps(f"y_p{b}") for b in range(2)]
        r_loaded = s.sem("r_loaded")
        w_loaded = [s.sem(f"w_loaded{b}") for b in range(2)]
        r_turned, r_kept = s.sem("r_turned"), s.sem("r_kept")
        up_done, gate_made, hid_made, y_added, cur_made = (
            s.sem(n) for n in ("up_done", "gate_made", "hid_made", "y_added", "cur_made"))
        y_done = [s.sem(f"y_done{b}") for b in range(2)]
        act_past = s.sem("act_past")
        b1_rows = s.sb("b1_rows", [n_exp * FC, P]) if b1 is not None else None
        n_up = NCH * FC
        per_load = 16 * (n1 + 1 + (b2 is not None))

        with s.block() as block:
            @block.sync
            def _(sp):
                if b1 is not None:
                    sp.dma_start(b1_rows[:], b1.rearrange("e (c p) -> (e c) p", p=P)).then_inc(r_loaded, 16)
                with sp.Fori(0, n_exp // 2) as i:
                    for b in range(2):
                        e = i * 2 + b
                        sp.wait_ge(y_done[b], i * NT + 1)
                        for k in range(n1):
                            sp.dma_start(W1[b][k][:], w1s[k][e].rearrange("(c p) f -> p c f", p=P)).then_inc(w_loaded[b], 16)
                        sp.dma_start(W2[b][:], w2[e].rearrange("(c p) f -> p c f", p=P)).then_inc(w_loaded[b], 16)
                        if b2 is not None:
                            sp.dma_start(b2_r[b][:], b2[e].unsqueeze(0)).then_inc(w_loaded[b], 16)

            @block.tensor
            def _(pe):
                for b in range(2):
                    pe.sem_inc(y_done[b], 1)
                if b1 is not None:
                    pe.wait_ge(r_loaded, 16)
                    nc.tensor.transpose(y_p[0][:, 0:n_exp * FC], b1_rows[:],
                                        m.ident[0:n_exp * FC, 0:n_exp * FC]).then_inc(r_turned, 1)
                with pe.Fori(0, n_exp // 2) as i:
                    for b in range(2):
                        e = i * 2 + b
                        pe.wait_ge(w_loaded[b], i * per_load + per_load)
                        for c in range(NCH):
                            for f in range(FC):
                                n = c * FC + f
                                pe.wait_ge(hid_made, e * n_up + (n + 1))
                                for w in range(n1):
                                    for k in range(KC):
                                        last = nc.tensor.matmul(up_p[w][n % 2][:, 0:CHN], W1[b][w][:, k, f * P:(f + 1) * P],
                                                                m.XT[:, k, c * CHN:(c + 1) * CHN], start=(k == 0),
                                                                stop=(k == KC - 1))
                                last.then_inc(up_done, 1)
                            pe.wait_ge(hid_made, e * n_up + ((c + 1) * FC + 2))
                            for r in range(2):
                                t = 2 * c + r
                                pe.wait_ge(y_added, e * NT + (t + 1))
                                for f in range(FC):
                                    last = nc.tensor.matmul(y_p[t % 2][0:TR, :], hid[:, c % 2, f, r * TR:(r + 1) * TR],
                                                            W2[b][:, f], start=(f == 0), stop=(f == FC - 1 and b2 is None))
                                if b2 is not None:
                                    last = nc.tensor.matmul(y_p[t % 2][0:TR, :], m.ones[0:1, 0:TR], b2_r[b][:],
                                                            start=False, stop=True)
                                last.then_inc(y_done[b], 1)

            @block.gpsimd
            def _(pool):
                pool.sem_inc(y_added, 2)

            @block.scalar
            def _(act):
                if not gated:
                    act.sem_inc(hid_made, 2)
                    act.wait_ge(r_kept, 1)
                with act.Fori(0, n_exp // 2) as i:
                    for b in range(2):
                        e = i * 2 + b
                        for c in range(NCH):
                            for f in range(FC):
                                n = c * FC + f
                                if not gated:
                                    wait_apart(act, up_done, e * n_up + (n + 1), act_past)
                                else:
                                    act.wait_ge(up_done, e * n_up + (n + 1))
                                if gated:
                                    act.wait_ge(hid_made, e * n_up + (n + 1))
                                    nc.scalar.activation(gate[:, n % 2], up_p[0][n % 2][:, 0:CHN], ACT.Silu
                                                         ).then_inc(gate_made, 1)
                                else:
                                    nc.scalar.activation(hid[:, c % 2, f], up_p[0][n % 2][:, 0:CHN], ACT.Relu,
                                                         bias=b1_c[:, e, f:f + 1]
                                                         ).then_inc(hid_made, 1)

            @block.vector
            def _(dve):
                if gated:
                    dve.sem_inc(hid_made, 2)
                if b1 is not None:
                    dve.wait_ge(r_turned, 1)
                    nc.vector.tensor_copy(b1_c[:], y_p[0][:, 0:n_exp * FC].rearrange("p (e c) -> p e c", c=FC)
                                          ).then_inc(r_kept, 1)
                    dve.wait_ge(r_kept, 1)
                with dve.Fori(0, n_exp // 2) as i:
                    for b in range(2):
                        e = i * 2 + b
                        nc.vector.tensor_copy(cur[:, b], wts[:, :, e]).then_inc(cur_made, 1)
                        dve.wait_ge(cur_made, e + 1)
                        for c in range(NCH):
                            if gated:
                                for f in range(FC):
                                    n = c * FC + f
                                    dve.wait_ge(gate_made, e * n_up + (n + 1))
                                    nc.vector.tensor_tensor(hid[:, c % 2, f], gate[:, n % 2], up_p[1][n % 2][:, 0:CHN],
                                                            ALU.mult).then_inc(hid_made, 1)
                            for r in range(2):
                                t = 2 * c + r
                                dve.wait_ge(y_done[b], i * NT + (t + 2))
                                nc.vector.scalar_tensor_tensor(out=m.X[:, t], in0=y_p[t % 2][0:TR, :],
                                                               scalar=cur[:, b, t:t + 1], in1=m.X[:, t], op0=ALU.mult,
                                                               op1=ALU.add).then_inc(y_added, 1)


def first_of(nc, o, hit, out, taken):
    o.link(nc.vector.tensor_copy(out[:, :, 0], hit[:, :, 0]))
    o.link(nc.vector.tensor_copy(taken, hit[:, :, 0]))
    for e in range(1, out.shape[2]):
        o.link(nc.vector.tensor_tensor(out[:, :, e], hit[:, :, e], taken, ALU.is_gt))
        o.link(nc.vector.tensor_tensor(taken, taken, hit[:, :, e], ALU.max))


class Top1:
    n_loads = 2
    choices = 1

    def __init__(self, Wr, br):
        self.Wr, self.br = Wr, br

    def load(self, sp, sem, Wr, r_rows, br):
        sp.dma_start(Wr[:], self.Wr.rearrange("(c p) e -> p c e", p=P)).then_inc(sem, 16)
        sp.dma_start(br[:], self.br.unsqueeze(0)).then_inc(sem, 16)

    def act(self, act, shifted, expd, tmp, small):
        act.wait_ge(shifted, 1)
        act.activation(tmp[1][:], tmp[0][:], ACT.Exp).then_inc(expd, 1)

    def choose(self, nc, dve, o, logits, hits, wts, tmp, small, shifted, expd):
        n = logits.shape[2]
        o.link(nc.vector.tensor_reduce(small[:, 0], logits, AX.X, ALU.max))
        nc.vector.tensor_tensor(tmp[0][:], logits, mid(small[:, 0], 2, n), ALU.subtract).then_inc(shifted, 1)
        dve.wait_ge(expd, 1)
        o.mark(nc.vector.tensor_reduce(small[:, 1], tmp[1][:], AX.X, ALU.add))
        o.link(nc.vector.tensor_reduce(small[:, 2], tmp[1][:], AX.X, ALU.max))
        o.mark(nc.vector.tensor_tensor(tmp[0][:], tmp[1][:], mid(small[:, 2], 2, n), ALU.is_ge))
        o.mark(nc.vector.reciprocal(small[:, 1], small[:, 1]))
        o.settle()
        o.link(nc.vector.tensor_tensor(wts[:, 0], small[:, 1], small[:, 2], ALU.mult))
        first_of(nc, o, tmp[0], hits[:, 0], small[:, 3])


class Top2:
    n_loads = 1
    choices = 2

    def __init__(self, router):
        self.router = router

    def load(self, sp, sem, Wr, r_rows, br):
        sp.dma_start(r_rows[:], self.router).then_inc(sem, 16)

    def act(self, act, shifted, expd, tmp, small):
        act.wait_ge(shifted, 1)
        act.activation(small[:, 2], small[:, 2], ACT.Exp).then_inc(expd, 1)

    def choose(self, nc, dve, o, logits, hits, wts, tmp, small, shifted, expd):
        n = logits.shape[2]
        o.link(nc.vector.tensor_reduce(small[:, 0], logits, AX.X, ALU.max))
        o.link(nc.vector.tensor_tensor(tmp[0][:], logits, mid(small[:, 0], 2, n), ALU.is_ge))
        first_of(nc, o, tmp[0], hits[:, 0], small[:, 3])
        o.link(nc.vector.scalar_tensor_tensor(out=tmp[1][:], in0=hits[:, 0], scalar=-BIG, in1=logits, op0=ALU.mult,
                                              op1=ALU.add))
        o.link(nc.vector.tensor_reduce(small[:, 1], tmp[1][:], AX.X, ALU.max))
        o.link(nc.vector.tensor_tensor(tmp[0][:], tmp[1][:], mid(small[:, 1], 2, n), ALU.is_ge))
        first_of(nc, o, tmp[0], hits[:, 1], small[:, 3])
        nc.vector.tensor_tensor(small[:, 2], small[:, 1], small[:, 0], ALU.subtract).then_inc(shifted, 1)
        dve.wait_ge(expd, 1)
        o.link(nc.vector.tensor_scalar(small[:, 3], small[:, 2], 1.0, None, ALU.add))
        o.link(nc.vector.reciprocal(wts[:, 0], small[:, 3]))
        o.link(nc.vector.tensor_tensor(wts[:, 1], small[:, 2], wts[:, 0], ALU.mult))


F1 = 128
Y0 = float(1.0 / np.sqrt(4.0 * np.pi))
Y1 = float(np.sqrt(3.0 / (4.0 * np.pi)))
MW = 9 * F1


def convolution(nc, m, Wf1, bf1, Wf2, bf2, W1_s, W1_v, W2_s, W2_v, table, rec_dram):
    with Stage(nc, "conv") as s:
        agg = [m.XN[:], m.XT_all[0:TR, :].rearrange("p (t d) -> p t d", t=NT)]
        conv_edges(nc, m, agg, Wf1, bf1, Wf2, bf2, table, rec_dram)
        conv_nodes(nc, m, agg, W1_s, W1_v, W2_s, W2_v)


def conv_edges(nc, m, agg, Wf1, bf1, Wf2, bf2, table, rec_dram):
    with Stage(nc, "edges") as s:
        recs = s.sb("recs", [P, G1, Q * REC1])
        wf1 = s.sb("wf1", [F_RBF, F1])
        wf2_in = s.sb("wf2_in", [P, 4 * F1])
        wf2 = s.sb("wf2", [P, 4, F1])
        bf1_c = s.sb("bf1_c", [P, 1])
        bf2_in = s.sb("bf2_in", [3, 4 * F1])
        bf2_r = s.sb("bf2_r", [3, 4 * F1])
        bf2_k = [s.sb(f"bf2_k{k}", [3, 4 * F1], BF16) for k in range(3)]
        bf2_s = s.sb("bf2_s", [3, 4 * F1], BF16)
        ones_b = s.sb("ones_b", [3, P], BF16)
        part = s.sb("part", [3, 3])
        norm = s.sb("norm", [P, G1 * Q])
        idx = s.sb("idx", [P, 2, Q], U32)
        rows_g = s.sb("rows_g", [P, 2, Q, D])
        hot = s.sb("hot", [P, 2, Q, TR])
        past = s.sem("past")
        fs = s.sb("fs", [P, Q, F_RBF])
        ft = s.sb("ft", [F_RBF, Q * P])
        ab = s.sb("ab", [P, Q * P])
        hx = s.sb("hx", [P, Q * P])
        half = s.sb("half", [P, 1])
        ht = s.sb("ht", [P, Q * P])
        msg = s.sb("msg", [P, 2, Q, MW])
        dot = s.sb("dot", [P, Q, F1])
        vy = s.sb("vy", [P, Q, 3, F1])
        f_p = s.ps("f_p")
        h_p = s.ps("h_p")
        w_p = s.ps("w_p", 4)
        sum_p = s.ps("sum_p", 2)
        names = ("loaded", "prep", "sq_made", "norm_made", "idx_ready", "hot_made", "f_staged", "f_turned", "f_kept",
                 "h_done", "h_ln", "h_made", "w_done", "c_made", "b_made", "vector_made", "msg_made", "summed",
                 "added", "chain", "rows_used0", "rows_used1", "aorder")
        S = {n: s.sem(n) for n in names}
        root_made, act_past = s.sem("root_made"), s.sem("act_past")
        (loaded, prep, sq_made, norm_made, idx_ready, hot_made, f_staged, f_turned, f_kept, h_done, h_ln,
         h_made, w_done, c_made, b_made, vector_made, msg_made, summed, added, chain, used0, used1, aorder) = (S[n] for n in names)
        rows_used = [used0, used1]
        gathered = [s.pool_dma_sem(f"gathered{b}") for b in range(2)]
        rec4 = recs[:].rearrange("p g (q w) -> p g q w", q=Q)
        recf = recs[:].rearrange("p g (q w) -> p (g q) w", q=Q)
        n_loads = 4 + 3

        with s.block() as block:
            @block.sync
            def _(sp):
                sp.dma_start(recs[:], rec_dram.rearrange("(g p q) w -> p g (q w)", p=P, q=Q)).then_inc(loaded, 16)
                sp.dma_start(wf1[:], Wf1).then_inc(loaded, 16)
                sp.dma_start(wf2_in[:], Wf2[:, 0:4 * F1]).then_inc(loaded, 16)
                sp.dma_start(bf1_c[:], bf1.rearrange("(p o) -> p o", o=1)).then_inc(loaded, 16)
                for k in range(3):
                    sp.dma_start(bf2_in[k:k + 1, :], bf2[0:4 * F1].unsqueeze(0)).then_inc(loaded, 16)
                sp.wait_ge(loaded, 16 * n_loads)

            @block.gpsimd
            def _(pool):
                pool.wait_ge(loaded, 16 * n_loads)
                with pool.Fori(0, G1 // 2) as i:
                    for b in range(2):
                        rows = recs[:, i * 2 + b, :].rearrange("p (q w) -> p q w", q=Q)
                        pool.wait_ge(rows_used[b], i + 1)
                        nc.gpsimd.tensor_copy(idx[:, b], rows.bitcast(U32)[:, :, 0]).then_inc(idx_ready, 1)
                        wait_apart(pool, idx_ready, i * 2 + (b + 1), past)
                        for q in range(Q):
                            nc.gpsimd.indirect_dma_start(
                                out=rows_g[:, b, q, :], out_offset=None, in_=table[:, :],
                                in_offset=IndirectOffsetOnAxis(ap=idx[:, b, q:q + 1], axis=0)).then_inc(gathered[b], 16)

            @block.vector
            def _(dve):
                o = Order(dve, prep)
                for b in range(2):
                    dve.sem_inc(rows_used[b], 1)
                for part_ in agg:
                    o.mark(nc.vector.memset(part_, 0.0))
                o.mark(nc.vector.memset(ones_b[:], 1.0))
                o.mark(nc.vector.memset(half[:], 0.5))
                for k in range(3):
                    o.mark(nc.vector.tensor_scalar(part[:, k:k + 1], m.iota_col[0:3, 0:1], float(k), None, ALU.is_equal))
                dve.wait_ge(loaded, 16 * n_loads)
                for slot, off in ((0, 2 * F1), (1, 0), (2, 1), (3, 2 * F1 + 1)):
                    pick = slice(off, off - off % 2 + 2 * F1, 2)
                    o.mark(nc.vector.tensor_copy(wf2[:, slot], wf2_in[:, pick]))
                    o.mark(nc.vector.tensor_copy(bf2_r[:, slot * F1:(slot + 1) * F1], bf2_in[:, pick]))
                o.settle()
                for k in range(3):
                    o.link(nc.vector.tensor_copy(bf2_k[k][:], bf2_r[:]))
                    if k < 2:
                        o.link(nc.vector.tensor_tensor(bf2_r[:], bf2_r[:], bf2_k[k][:], ALU.subtract))
                o.link(nc.vector.tensor_scalar(bf2_s[:], bf2_k[0][:], part[:, 0:1], None, ALU.mult))
                for k in (1, 2):
                    o.link(nc.vector.scalar_tensor_tensor(out=bf2_s[:], in0=bf2_k[k][:], scalar=part[:, k:k + 1],
                                                          in1=bf2_s[:], op0=ALU.mult, op1=ALU.add))
                sq = vy[:].rearrange("p q i f -> p (q i f)")[:, 0:G1 * Q]
                o.link(nc.vector.tensor_tensor(norm[:], recf[:, :, 2], recf[:, :, 2], ALU.mult))
                for k in (3, 4):
                    o.link(nc.vector.tensor_tensor(sq, recf[:, :, k], recf[:, :, k], ALU.mult))
                    o.link(nc.vector.tensor_tensor(norm[:], norm[:], sq, ALU.add))
                nc.vector.memset(dot[:, 0, 0:1], 0.0).then_inc(sq_made, 1)
                dve.wait_ge(root_made, 1)
                o.link(nc.vector.reciprocal(norm[:], norm[:]))
                o.link(nc.vector.tensor_scalar(norm[:], norm[:], Y1, None, ALU.mult))
                nc.vector.tensor_tensor(recf[:, :, 2:5], recf[:, :, 2:5], mid(norm[:], 2, 3), ALU.mult).then_inc(norm_made, 1)
                dve.wait_ge(norm_made, 1)

                def softplus(i, c):
                    n, b, k = at(i, c)
                    dve.wait_ge(h_ln, n + 1)
                    nc.vector.scalar_tensor_tensor(out=ht[:], in0=hx[:], scalar=0.0, in1=ab[:], op0=ALU.max,
                                                   op1=ALU.add).then_inc(h_made, 1)

                def prepare(i, c):
                    n, b, k = at(i, c)
                    o = Order(dve, chain, n * 3)
                    rec = recs[:, n, :].rearrange("p (q w) -> p q w", q=Q)
                    for q in range(Q):
                        last = nc.vector.tensor_scalar(hot[:, b, q], m.iota_row[:, 0:TR], rec[:, q, 1:2], rec[:, q, 5:6],
                                                       ALU.is_equal, ALU.mult)
                    last.then_inc(hot_made, 1)
                    dve.wait_ge(gathered[b], k * (16 * Q) + 16 * Q)
                    v = rows_g[:, b, :, F1:D].rearrange("p q (i f) -> p q i f", i=3)
                    o.link(nc.vector.tensor_tensor(vy[:], v, mid(rec[:, :, 2:5], 3, F1), ALU.mult))
                    o.link(nc.vector.tensor_tensor(dot[:], vy[:, :, 0], vy[:, :, 1], ALU.add))
                    o.link(nc.vector.tensor_tensor(dot[:], dot[:], vy[:, :, 2], ALU.add))

                def messages(i, c):
                    n, b, k = at(i, c)
                    v = rows_g[:, b, :, F1:D].rearrange("p q (i f) -> p q i f", i=3)
                    wp = w_p[:].rearrange("p (q k f) -> p q k f", q=Q, k=4)
                    dve.wait_ge(w_done, n + 1)
                    nc.vector.tensor_tensor(msg[:, b, :, 0:2 * F1].rearrange("p q (k f) -> p q k f", k=2),
                                            mid(rows_g[:, b, :, 0:F1], 2, 2), wp[:, :, 0:2], ALU.mult).then_inc(c_made, 1)
                    nc.vector.tensor_tensor(msg[:, b, :, 2 * F1:3 * F1], dot[:], wp[:, :, 2], ALU.mult).then_inc(b_made, 1)
                    nc.vector.tensor_tensor(msg[:, b, :, 6 * F1:9 * F1].rearrange("p q (i f) -> p q i f", i=3), v,
                                            mid(wp[:, :, 3], 2, 3), ALU.mult).then_inc(rows_used[b], 1)

                def add(i, c):
                    n, b, k = at(i, c)
                    tile = nc.vector.value_load(m.tile1[0:1, ds(n, 1)], min_val=0, max_val=NT - 1)
                    dve.wait_ge(summed, n + 1)
                    for k, part in enumerate(agg):
                        nc.vector.tensor_tensor(part[:, tile, :], part[:, tile, :], sum_p[0:TR, k * 512:(k + 1) * 512],
                                                ALU.add).then_inc(added, 1)
                    dve.wait_ge(added, n * 2 + 2)

                def step(i, c, add_last=True, next1=True, next2=True):
                    if add_last:
                        add(i, c - 1)
                    if next1:
                        prepare(i, c + 1)
                        messages(i, c + 1)
                    if next2:
                        softplus(i, c + 2)

                softplus(0, 0)
                step(0, -1, add_last=False)
                step(0, 0, add_last=False)
                step(0, 1)
                with dve.Fori(1, G1 // 2 - 1) as i:
                    step(i, 0)
                    step(i, 1)
                step(0, G1 - 2, next2=False)
                step(0, G1 - 1, next1=False, next2=False)
                add(0, G1 - 1)

            @block.scalar
            def _(act):
                act.wait_ge(sq_made, 1)
                nc.scalar.activation(norm[:], norm[:], ACT.Sqrt).then_inc(root_made, 1)
                act.wait_ge(norm_made, 1)
                nc.scalar.preload_act_table_set("natural_log_exp_and_others")

                def stage(i, c):
                    n, b, k = at(i, c)
                    rec = recs[:, n, :].rearrange("p (q w) -> p q w", q=Q)
                    nc.scalar.copy(fs[:], rec[:, :, 6:6 + F_RBF]).then_inc(f_staged, 1)

                def keep(i, c):
                    n, b, k = at(i, c)
                    act.wait_ge(f_turned, n + 1)
                    nc.scalar.copy(ft[:], f_p[0:F_RBF, :]).then_inc(f_kept, 1)

                def hidden(i, c):
                    n, b, k = at(i, c)
                    act.wait_ge(h_done, n + 1)
                    a = Order(act, aorder, n * 3)
                    a.link(nc.scalar.activation(hx[:], h_p[:], ACT.Identity, bias=bf1_c[:, 0:1]))
                    a.link(nc.scalar.activation(ab[:], hx[:], ACT.Abs))
                    a.link(nc.scalar.activation(ab[:], ab[:], ACT.Exp, scale=-1.0))
                    nc.scalar.activation(ab[:], ab[:], ACT.Ln, bias=half[:, 0:1], scale=0.5).then_inc(h_ln, 1)

                def vectors(i, c):
                    n, b, k = at(i, c)
                    rec = recs[:, n, :].rearrange("p (q w) -> p q w", q=Q)
                    wait_apart(act, c_made, n + 1, act_past)
                    for q in range(Q):
                        for k in range(3):
                            last = nc.scalar.activation(msg[:, b, q, (3 + k) * F1:(4 + k) * F1], msg[:, b, q, 0:F1],
                                                        ACT.Copy, scale=rec[:, q, 2 + k:3 + k])
                    last.then_inc(vector_made, 1)

                def step(i, c, next1=True, next2=True, next3=True):
                    if next2:
                        keep(i, c + 2)
                    if next2:
                        hidden(i, c + 2)
                    if next1:
                        vectors(i, c + 1)
                    if next3:
                        stage(i, c + 3)

                stage(0, 0)
                keep(0, 0)
                hidden(0, 0)
                stage(0, 1)
                step(0, -1, next1=True)
                step(0, 0)
                step(0, 1)
                with act.Fori(1, G1 // 2 - 2) as i:
                    step(i, 0)
                    step(i, 1)
                step(0, G1 - 4)
                step(0, G1 - 3, next3=False)
                step(0, G1 - 2, next2=False, next3=False)

            @block.tensor
            def _(pe):
                pe.wait_ge(norm_made, 1)

                def turn(i, c):
                    n, b, k = at(i, c)
                    pe.wait_ge(f_staged, n + 1)
                    for q in range(Q):
                        last = nc.tensor.transpose(f_p[0:F_RBF, q * P:(q + 1) * P], fs[:, q], m.ident[:])
                    last.then_inc(f_turned, 1)

                def hidden(i, c):
                    n, b, k = at(i, c)
                    pe.wait_ge(f_kept, n + 1)
                    nc.tensor.matmul(h_p[:], wf1[:], ft[:], start=True, stop=True).then_inc(h_done, 1)

                def filters(i, c, used=True):
                    n, b, k = at(i, c)
                    pe.wait_ge(h_made, n + 1)
                    if used:
                        pe.wait_ge(rows_used[(c - 1) % 2], at(i, c - 1)[2] + 2)
                    for q in range(Q):
                        nc.tensor.matmul(w_p[:, q * 512:(q + 1) * 512], ht[:, q * P:(q + 1) * P],
                                         wf2[:].rearrange("p k f -> p (k f)"), start=True, stop=False)
                        last = nc.tensor.matmul(w_p[:, q * 512:(q + 1) * 512], ones_b[:], bf2_s[:], start=False, stop=True)
                    last.then_inc(w_done, 1)

                def sums(i, c, part, added_before):
                    n, b, k = at(i, c)
                    if part == 0:
                        pe.wait_ge(rows_used[b], k + 2)
                        pe.wait_ge(vector_made, n + 1)
                        if added_before:
                            pe.wait_ge(added, n * 2)
                    for q in range(Q):
                        last = nc.tensor.matmul(sum_p[0:TR, part * 512:(part + 1) * 512], hot[:, b, q],
                                                msg[:, b, q, F1 + part * 512:F1 + (part + 1) * 512], start=(q == 0),
                                                stop=(q == Q - 1))
                    if part == 1:
                        last.then_inc(summed, 1)

                def step(i, c, now=True, next1=True, next2=True, first=False):
                    if next2:
                        turn(i, c + 2)
                    if next1:
                        filters(i, c + 1, used=now)
                    if next2:
                        hidden(i, c + 2)
                    if now:
                        sums(i, c, 0, not first)
                        sums(i, c, 1, not first)

                turn(0, 0)
                hidden(0, 0)
                step(0, -1, now=False)
                step(0, 0, first=True)
                step(0, 1)
                with pe.Fori(1, G1 // 2 - 1) as i:
                    step(i, 0)
                    step(i, 1)
                step(0, G1 - 2, next2=False)
                step(0, G1 - 1, next1=False, next2=False)


def conv_nodes(nc, m, agg, W1_s, W1_v, W2_s, W2_v):
    with Stage(nc, "nodes") as s:
        w1 = s.sb("w1", [P, 4, F1])
        w2 = s.sb("w2", [P, 2, F1])
        agg_t = s.sb("agg_t", [P, 8, TR])
        u = s.sb("u", [P, 4, TR])
        ab = s.sb("ab", [P, TR])
        half = s.sb("half", [P, 1])
        t_p = s.ps("t_p", 2)
        u_p = s.ps("u_p")
        y_p = s.ps("y_p")
        names = ("loaded", "prep", "turned", "kept", "u_done", "u_ln", "u_made", "y_done", "added", "aorder")
        loaded, prep, turned, kept, u_done, u_ln, u_made, y_done, added, aorder = (s.sem(n) for n in names)
        with s.block() as block:
            @block.sync
            def _(sp):
                for k, w in enumerate((W1_s[0:2 * F1:2, :], W1_s[1:2 * F1:2, :], W1_v[0:2 * F1:2, :], W1_v[1:2 * F1:2, :])):
                    sp.dma_start(w1[:, k], w).then_inc(loaded, 16)
                for k, w in enumerate((W2_s, W2_v)):
                    sp.dma_start(w2[:, k], w).then_inc(loaded, 16)
                sp.wait_ge(loaded, 96)

            @block.vector
            def _(dve):
                dve.wait_ge(loaded, 96)
                r = (2 * F1) ** -0.5
                for k, f in enumerate((Y0 * r, 3.0 ** -0.5 * r, r, Y0 * r)):
                    nc.vector.tensor_scalar(w1[:, k], w1[:, k], f, None, ALU.mult).then_inc(prep, 1)
                nc.vector.memset(half[:], 0.5).then_inc(prep, 1)
                nc.vector.tensor_scalar(w2[:], w2[:], F1 ** -0.5, None, ALU.mult).then_inc(prep, 1)
                for t in range(NT):
                    dve.wait_ge(u_ln, t + 1)
                    nc.vector.scalar_tensor_tensor(out=u[:, 0], in0=u[:, 0], scalar=0.0, in1=ab[:], op0=ALU.max,
                                                   op1=ALU.add).then_inc(u_made, 1)
                    dve.wait_ge(y_done, t + 1)
                    nc.vector.tensor_tensor(m.X[:, t, 0:F1], m.X[:, t, 0:F1], y_p[0:TR, 0:F1], ALU.add).then_inc(added, 1)
                    x = m.X[:, t, F1:D].rearrange("p (d i) -> p i d", i=3)
                    nc.vector.tensor_tensor(x, x, y_p[0:TR, F1:D].rearrange("p (i d) -> p i d", i=3), ALU.add
                                            ).then_inc(added, 1)

            @block.scalar
            def _(act):
                act.wait_ge(prep, 6)
                for t in range(NT):
                    act.wait_ge(turned, t + 1)
                    nc.scalar.copy(agg_t[:], t_p[:].rearrange("p (k n) -> p k n", k=8)[:, :, 0:TR]).then_inc(kept, 1)
                    act.wait_ge(u_done, t + 1)
                    a = Order(act, aorder, 3 * t)
                    a.link(nc.scalar.copy(u[:], u_p[:, 0:4 * TR].rearrange("p (k n) -> p k n", k=4)))
                    a.link(nc.scalar.activation(ab[:], u[:, 0], ACT.Abs))
                    a.link(nc.scalar.activation(ab[:], ab[:], ACT.Exp, scale=-1.0))
                    nc.scalar.activation(ab[:], ab[:], ACT.Ln, bias=half[:, 0:1], scale=0.5).then_inc(u_ln, 1)

            @block.tensor
            def _(pe):
                pe.wait_ge(prep, 6)
                for t in range(NT):
                    for k in range(8):
                        last = nc.tensor.transpose(t_p[:, k * P:k * P + TR], agg[k // 4][:, t, (k % 4) * F1:(k % 4 + 1) * F1],
                                                   m.ident[0:TR, 0:TR])
                    last.then_inc(turned, 1)
                    pe.wait_ge(kept, t + 1)
                    nc.tensor.matmul(u_p[:, 0:TR], w1[:, 0], agg_t[:, 0], start=True, stop=False, skip_group_check=True)
                    nc.tensor.matmul(u_p[:, 0:TR], w1[:, 1], agg_t[:, 1], start=False, stop=True, skip_group_check=True)
                    vec = u_p[:, TR:4 * TR]
                    nc.tensor.matmul(vec, w1[:, 2], agg_t[:, 2:5].rearrange("p k n -> p (k n)"), start=False, stop=False,
                                     skip_group_check=True)
                    nc.tensor.matmul(vec, w1[:, 3], agg_t[:, 5:8].rearrange("p k n -> p (k n)"), start=False, stop=True,
                                     skip_group_check=True).then_inc(u_done, 1)
                    pe.wait_ge(u_made, t + 1)
                    if t >= 1:
                        pe.wait_ge(added, 2 * t)
                    for k in range(4):
                        last = nc.tensor.matmul(y_p[0:TR, k * F1:(k + 1) * F1], u[:, k], w2[:, min(k, 1)],
                                                start=True, stop=True, skip_group_check=True)
                    last.then_inc(y_done, 1)


def store(nc, m, out):
    with Stage(nc, "store") as s:
        stored = s.sem("stored")
        with s.block() as block:
            @block.sync
            def _(sp):
                sp.dma_start(out.rearrange("(t p) d -> p t d", p=TR), m.X[:]).then_inc(stored, 16)
                sp.wait_ge(stored, 16)


class Memory:

    def __init__(self, s):
        self.X = s.sb("X", [TR, NT, D])
        self.XN_all = s.sb("XN", [P, NT * D])
        self.XN = self.XN_all[0:TR].rearrange("p (t d) -> p t d", t=NT)
        self.XT_all = s.sb("XT", [P, NT * D])
        self.XT = self.XT_all[:, 0:KC * N].rearrange("p (c n) -> p c n", c=KC)
        self.iota_row = s.sb("iota_row", [P, P])
        self.iota_col = s.sb("iota_col", [P, 1])
        self.ident = s.sb("ident", [P, P])
        self.ident_b = s.sb("ident_b", [P, P], BF16)
        self.above = s.sb("above", [P, P])
        self.ones = s.sb("ones", [P, P])
        self.over = s.sb("over", [1, 2], I32)
        self.tile0 = s.sb("tile0", [1, G0], I32)
        self.tile1 = s.sb("tile1", [1, G1], I32)


def gps_kernel(nc, i, out, stop=99):
    rec0 = nc.dram_tensor("rec0", [G0 * GROUP, REC0], F32).ap()
    rec1 = nc.dram_tensor("rec1", [G1 * GROUP, REC1], F32).ap()
    XL = nc.dram_tensor("XL", [N, D + H], F32).ap()
    T1 = nc.dram_tensor("T1", [N, D], F32).ap()
    alpha = nc.dram_tensor("alpha", [G0 * GROUP, H], F32).ap()
    weight = nc.dram_tensor("weight", [G0 * GROUP, H], F32).ap()
    by_row = lambda v: v.rearrange("(p t) -> p t", p=TR)

    Stage.used.clear()
    with Stage(nc, "all") as s:
        m = Memory(s)
        constants(nc, m, i["x"])

        sort_edges(nc, m, "sort0", G0, REC0, rec0, m.tile0,
                   lambda key, other, rest: [(key[:, 0:ER], by_row(i["dst"])), (other[:, 0:ER], by_row(i["src"]))], 2,
                   lambda key, rest, recs: nc.vector.tensor_copy(recs[:, :, 2], key[:]), N // TR)

        def loads1(key, other, rest):
            return [(key[:], by_row(i["src"])), (other[:], by_row(i["dst"])),
                    (rest[:, 0:3 * ER], i["edge_attr_3"].rearrange("(p t) c -> p (t c)", p=TR)),
                    (rest[:, 3 * ER:4 * ER], by_row(i["edge_weight"])),
                    (rest[:, 4 * ER:24 * ER], i["edge_attr_20"].rearrange("(p t) c -> p (t c)", p=TR))]

        def fill1(key, rest, recs):
            nc.vector.tensor_copy(recs[:, :, 2:5], rest[:, 0:3 * ER].rearrange("p (t c) -> p t c", c=3))
            nc.vector.tensor_copy(recs[:, :, 5], rest[:, 3 * ER:4 * ER])
            return nc.vector.tensor_copy(recs[:, :, 6:26], rest[:, 4 * ER:24 * ER].rearrange("p (t c) -> p t c", c=F_RBF))

        sort_edges(nc, m, "sort1", G1, REC1, rec1, m.tile1, loads1, 5, fill1, 0)

        clear_semaphores(nc)
        layer_norm(nc, m, "norm0", plain)
        wqkv = i["L0_mix_W_qkv"]
        if stop >= 1:
            part = lambda k: [wqkv[c * P:(c + 1) * P, k * D:(k + 1) * D] for c in range(KC)]
            attention(nc, m, "mix0", part(0), part(1), part(2), chunk_rows(i["L0_mix_W_out"], plain),
                      bias=i["L0_mix_b_out"].unsqueeze(0))
        if stop >= 2:
            with Stage(nc, "gat") as g:
                XR = g.sb("XR", [TR, NT, 3, D + H], BF16)
                node_table(nc, m, "lr", [chunk_rows(i["L0_gnn_W_l"], plain), chunk_rows(i["L0_gnn_W_r"], plain)],
                           [(slice(0, D), [(c, 0, c) for c in range(KC)])], 1.0, XL, XR, att_w=i["L0_gnn_att"])
                edge_scores(nc, m, XR, i["L0_gnn_att"], XL, rec0, alpha)
            edge_weights(nc, m, rec0, alpha, weight)
            edge_sums(nc, m, i["L0_gnn_bias"], XL, rec0, weight)
        if stop >= 3:
            layer_norm(nc, m, "norm1", plain)
            mixture(nc, m, "moe0", 0, False, [i["L0_ffn_W1"]], i["L0_ffn_W2"], Top1(i["L0_ffn_Wr"], i["L0_ffn_br"]),
                    b1=i["L0_ffn_b1"], b2=i["L0_ffn_b2"])
        clear_semaphores(nc)
        if stop >= 4:
            layer_norm(nc, m, "norm2", by_component)
            sc, vc = i["L1_gnn_W_in2f_s"], i["L1_gnn_W_in2f_v"]
            node_table(nc, m, "t1", [[sc, vc]], [(slice(c * P, (c + 1) * P), [(c, 0, min(c, 1))]) for c in range(KC)],
                       F1 ** -0.5, T1, None)
            rows = lambda n: chunk_rows(i[n], by_component)
            attention(nc, m, "mix1", rows("L1_mix_Wq"), rows("L1_mix_Wk"), rows("L1_mix_Wv"),
                      chunk_rows(i["L1_mix_Wo"], plain), omegas=(i["L1_mix_omega_q"], i["L1_mix_omega_k"]))
        if stop >= 5:
            convolution(nc, m, i["L1_gnn_Wf1"], i["L1_gnn_bf1"], i["L1_gnn_Wf2"], i["L1_gnn_bf2"], i["L1_gnn_W1_s"],
                        i["L1_gnn_W1_v"], i["L1_gnn_W2_s"], i["L1_gnn_W2_v"], T1, rec1)
        if stop >= 6:
            layer_norm(nc, m, "norm3", plain)
            clear_semaphores(nc)
            mixture(nc, m, "moe1", 1, True, [i["L1_ffn_w_gate"], i["L1_ffn_w_up"]], i["L1_ffn_w_down"],
                    Top2(i["L1_ffn_router_w"]))
        store(nc, m, out)


def kernel(**inputs):
    import numpy as _np
    from concourse import bacc as _bacc
    from concourse.bass_utils import run_bass_kernel_spmd as _run

    nc = _bacc.Bacc("TRN2", target_bir_lowering=False, num_devices=1)
    arrays, aps = {}, {}
    for name, value in inputs.items():
        a = _np.ascontiguousarray(value)
        arrays[f"in_{name}"] = a
        aps[name] = nc.dram_tensor(f"in_{name}", a.shape, mybir.dt.from_np(a.dtype), kind="ExternalInput").ap()
    out = nc.dram_tensor("out", (N, D), F32, kind="ExternalOutput").ap()
    gps_kernel(nc, aps, out)
    r = _run(nc, [arrays], core_ids=[0])
    return r.results[0]["out"]
```
